# Optimizing a Trainium2 kernel written in Bass

```python
import numpy as np
import jax
import jax.numpy as jnp

def _softmax(x, axis=-1):
    return jax.nn.softmax(x, axis=axis)

def _gelu(x):
    return jax.nn.gelu(x, approximate=True)

def _silu(x):
    return jax.nn.silu(x)

def _sigmoid(x):
    return jax.nn.sigmoid(x)

def _layernorm(x, axis=-1, eps=1e-05):
    m = jnp.mean(x, axis=axis, keepdims=True)
    v = jnp.var(x, axis=axis, keepdims=True)
    return (x - m) / jnp.sqrt(v + eps)

def _scatter_add(tgt, idx, src, axis=0):
    return tgt.at[idx].add(src)

def _segment_sum(src, seg, n):
    return jax.ops.segment_sum(src, seg, n)
kernel_name = 'mk_decoder_postln_d2_seqx_r8_ba683f'

def setup_inputs(seed: int=0):
    np.random.seed(seed)
    _w = jnp.asarray

    def _rec_inputs():
        import jax
        import jax.numpy as jnp
        _rk = jax.random.key(seed)
        x = -0.0002928 + 1 * jax.random.normal(jax.random.fold_in(_rk, 1), (64, 64, 128), jnp.float32)
        _lenS = 64 - jax.random.randint(jax.random.fold_in(_rk, 7), (64,), 0, max(1, 64 // 4) + 1, jnp.int32)
        _lenS2 = 64 - jax.random.randint(jax.random.fold_in(_rk, 8), (64,), 0, max(1, 64 // 4) + 1, jnp.int32)
        _ctx_1024P = jax.random.normal(jax.random.fold_in(_rk, 11), (64, 16, 128), jnp.float32)
        _ctx_1024c = jax.random.dirichlet(jax.random.fold_in(_rk, 511), 0.3 * jnp.ones((16,), jnp.float32), (64, 64))
        _ctx_1024t = jnp.einsum('bsk,bkd->bsd', _ctx_1024c, _ctx_1024P)
        _ctx_1024t = _ctx_1024t * jax.lax.rsqrt(jnp.mean(jnp.square(_ctx_1024t)) + 1e-12) * 0.953939
        ctx_1024 = -1.39393e-06 + 0.999914 * (_ctx_1024t + 0.3 * jax.random.normal(jax.random.fold_in(_rk, 611), (64, 64, 128), jnp.float32))
        return (x, ctx_1024)
    x, ctx_1024 = _rec_inputs()

    def _L0_attn_setup():
        import math
        import jax, jax.numpy as jnp
        import numpy as np
        NUM_HEADS = 16
        HEAD_SIZE = 64
        HIDDEN = 128
        ROPE_BASE = 10000.0

        def _rope_cos_sin(seq_len, dim, dtype):
            inv_freq = 1.0 / ROPE_BASE ** (jnp.arange(0, dim, 2, dtype=jnp.float32) / dim)
            t = jnp.arange(seq_len, dtype=jnp.float32)
            freqs = jnp.einsum('s,d->sd', t, inv_freq)
            emb = jnp.concatenate([freqs, freqs], axis=-1)
            return (jnp.cos(emb).astype(dtype), jnp.sin(emb).astype(dtype))

        def _rotate_half(x):
            half = x.shape[-1] // 2
            return jnp.concatenate([-x[..., half:], x[..., :half]], axis=-1)

        def _apply_rope(q, k):
            cos, sin = _rope_cos_sin(q.shape[-2], q.shape[-1], q.dtype)
            q = q * cos + _rotate_half(q) * sin
            k = k * cos + _rotate_half(k) * sin
            return (q, k)
        key = jax.random.key(seed)
        ks = jax.random.split(key, 9)
        B, S = (2, 512)
        dt = jnp.bfloat16
        lim_in = 1.0 / math.sqrt(HIDDEN)
        inp = {'input_embeds': jax.random.normal(ks[0], (B, S, HIDDEN), dtype=dt), 'Wq': jax.random.uniform(ks[1], (NUM_HEADS * HEAD_SIZE, HIDDEN), dtype=dt, minval=-lim_in, maxval=lim_in), 'bq': jnp.zeros((NUM_HEADS * HEAD_SIZE,), dtype=dt), 'Wk': jax.random.uniform(ks[2], (NUM_HEADS * HEAD_SIZE, HIDDEN), dtype=dt, minval=-lim_in, maxval=lim_in), 'bk': jnp.zeros((NUM_HEADS * HEAD_SIZE,), dtype=dt), 'Wv': jax.random.uniform(ks[3], (NUM_HEADS * HEAD_SIZE, HIDDEN), dtype=dt, minval=-lim_in, maxval=lim_in), 'bv': jnp.zeros((NUM_HEADS * HEAD_SIZE,), dtype=dt), 'Wo': jax.random.uniform(ks[4], (HIDDEN, NUM_HEADS * HEAD_SIZE), dtype=dt, minval=-lim_in, maxval=lim_in), 'bo': jnp.zeros((HIDDEN,), dtype=dt)}
        return inp
    _L0_attn_all = _L0_attn_setup()
    _L0_attn_in = {k: v for k, v in _L0_attn_all.items() if k in ('Wq', 'bq', 'Wk', 'bk', 'Wv', 'bv', 'Wo', 'bo')}
    del _L0_attn_all

    def _L0_xattn_setup():
        import jax, jax.numpy as jnp
        import numpy as np
        B, T, D, H = (2, 256, 128, 16)
        DH = D // H
        key = jax.random.key(seed)
        ks = jax.random.split(key, 11)
        s = 1.0 / np.sqrt(D)
        return {'q': jax.random.normal(ks[0], (B, T, D), jnp.float32), 'k': jax.random.normal(ks[1], (B, T, D), jnp.float32), 'v': jax.random.normal(ks[2], (B, T, D), jnp.float32), 'wq_w': jax.random.normal(ks[3], (D, D), jnp.float32) * s, 'wq_b': jnp.zeros((D,), jnp.float32), 'wk_w': jax.random.normal(ks[4], (D, D), jnp.float32) * s, 'wk_b': jnp.zeros((D,), jnp.float32), 'wv_w': jax.random.normal(ks[5], (D, D), jnp.float32) * s, 'wv_b': jnp.zeros((D,), jnp.float32), 'wo_w': jax.random.normal(ks[6], (D, D), jnp.float32) * s, 'wo_b': jnp.zeros((D,), jnp.float32)}
    _L0_xattn_all = _L0_xattn_setup()
    _L0_xattn_in = {k: v for k, v in _L0_xattn_all.items() if k in ('wq_w', 'wq_b', 'wk_w', 'wk_b', 'wv_w', 'wv_b', 'wo_w', 'wo_b')}
    del _L0_xattn_all

    def _L0_ffn_setup():
        import jax, jax.numpy as jnp
        import numpy as np
        LN_EPS = 1e-05
        NORM_EPS = 1e-12

        def _layernorm(x, gamma, beta):
            mu = x.mean(axis=-1, keepdims=True)
            var = ((x - mu) ** 2).mean(axis=-1, keepdims=True)
            return (x - mu) * jax.lax.rsqrt(var + LN_EPS) * gamma + beta

        def _l2norm(x, axis):
            n = jnp.sqrt((x ** 2).sum(axis=axis, keepdims=True))
            return x / jnp.maximum(n, NORM_EPS)
        key = jax.random.key(seed)
        ks = jax.random.split(key, 4)
        B, N, D, E, S, H = (64, 32, 128, 16, 16, 32)
        x = jax.random.normal(ks[0], (B, N, D), dtype=jnp.float32)
        mu = jax.random.normal(ks[1], (D, E, S), dtype=jnp.float32) / np.sqrt(D)
        w1 = jax.random.normal(ks[2], (E, D, H), dtype=jnp.float32) * np.sqrt(2.0 / D)
        w2 = jax.random.normal(ks[3], (E, H, D), dtype=jnp.float32) * np.sqrt(2.0 / (H + D))
        return {'x': x, 'ln_gamma': jnp.ones((D,), jnp.float32), 'ln_beta': jnp.zeros((D,), jnp.float32), 'mu': mu, 'scale': jnp.ones((1,), jnp.float32), 'w1': w1, 'b1': jnp.zeros((E, H), jnp.float32), 'w2': w2, 'b2': jnp.zeros((E, D), jnp.float32)}
    _L0_ffn_all = _L0_ffn_setup()
    _L0_ffn_in = {k: v for k, v in _L0_ffn_all.items() if k in ('ln_gamma', 'ln_beta', 'mu', 'scale', 'w1', 'b1', 'w2', 'b2')}
    del _L0_ffn_all

    def _L1_attn_setup():
        import jax, jax.numpy as jnp
        import numpy as np
        EPS = 1e-06
        DECAY = 0.9
        THR = 0.5
        SBETA = 10.0
        KW = 4

        def _rms(x, w):
            return x * jax.lax.rsqrt(jnp.mean(x * x, axis=-1, keepdims=True) + EPS) * w
        B, T, D, H, dk, dv, r, dff = (2, 256, 128, 8, 64, 64, 64, 512)
        keys = iter(jax.random.split(jax.random.key(seed), 24))

        def g(shape, s=0.02):
            return jax.random.normal(next(keys), shape, jnp.float32) * s
        return {'x': jax.random.normal(next(keys), (B, T, D), jnp.float32), 'norm_in_w': jnp.ones((D,), jnp.float32), 'conv_w': g((D, 1, KW), 0.3), 'conv_b': jnp.zeros((D,), jnp.float32), 'Wq': g((D, H * dk)), 'Wk': g((D, H * dk)), 'Wv': g((D, H * dv)), 'Wo': g((H * dv, D)), 'Wspike': g((D, H * dk), 0.1), 'Wau': g((D, r)), 'bau': jnp.zeros((r,), jnp.float32), 'Wad': g((r, H * dk)), 'bad': jnp.zeros((H * dk,), jnp.float32), 'alpha_spike': jnp.zeros((1, H, dk), jnp.float32), 'Wbeta': g((D, H)), 'bbeta': jnp.zeros((H,), jnp.float32), 'beta_spike': jnp.zeros((1, H, dk), jnp.float32), 'head_norm_w': jnp.ones((H, dv), jnp.float32), 'Wu1': g((D, r)), 'bu1': jnp.zeros((r,), jnp.float32), 'Wu2': g((r, D)), 'bu2': jnp.zeros((D,), jnp.float32), 'ff_norm_w': jnp.ones((D,), jnp.float32), 'Wff1': g((D, dff)), 'Wff3': g((D, dff)), 'Wff2': g((dff, D))}
    _L1_attn_all = _L1_attn_setup()
    _L1_attn_in = {k: v for k, v in _L1_attn_all.items() if k in ('norm_in_w', 'conv_w', 'conv_b', 'Wq', 'Wk', 'Wv', 'Wo', 'Wspike', 'Wau', 'bau', 'Wad', 'bad', 'alpha_spike', 'Wbeta', 'bbeta', 'beta_spike', 'head_norm_w', 'Wu1', 'bu1', 'Wu2', 'bu2', 'ff_norm_w', 'Wff1', 'Wff3', 'Wff2')}
    del _L1_attn_all

    def _L1_xattn_setup():
        import jax, jax.numpy as jnp
        import numpy as np
        E, T, H, F = (8, 256, 128, 512)
        key = jax.random.key(seed)
        k1, k2, k3 = jax.random.split(key, 3)
        x = jax.random.normal(k1, (E, T, H), dtype=jnp.float32)
        w1 = jax.random.normal(k2, (E, F, H), dtype=jnp.float32) * 0.02
        w2 = jax.random.normal(k3, (E, F, H), dtype=jnp.float32) * 0.02
        return {'x': x, 'w1': w1, 'w2': w2}
    _L1_xattn_all = _L1_xattn_setup()
    _L1_xattn_in = {k: v for k, v in _L1_xattn_all.items() if k in ()}
    del _L1_xattn_all

    def _L1_ffn_setup():
        import jax, jax.numpy as jnp
        import numpy as np
        NUM_EXPERTS = 8
        EXPERT_CAPACITY = 2.0
        DIM = 128
        HIDDEN_DIM = 512
        key = jax.random.key(seed)
        k_x, k_g, k_w1, k_w2 = jax.random.split(key, 4)
        n, t, d, f, e = (8, 128, DIM, HIDDEN_DIM, NUM_EXPERTS)
        x = jax.random.normal(k_x, (n, t, d), dtype=jnp.float32)
        gate_w = jax.random.normal(k_g, (e, d), dtype=jnp.float32) * 0.02
        w1 = jax.random.normal(k_w1, (e, d, f), dtype=jnp.float32) * 0.02
        w2 = jax.random.normal(k_w2, (e, f, d), dtype=jnp.float32) * 0.02
        return {'x': x, 'gate_w': gate_w, 'w1': w1, 'w2': w2}
    _L1_ffn_all = _L1_ffn_setup()
    _L1_ffn_in = {k: v for k, v in _L1_ffn_all.items() if k in ('gate_w', 'w1', 'w2')}
    del _L1_ffn_all
    return {'x': x, 'ctx_1024': ctx_1024, 'L0_attn_Wq': _L0_attn_in['Wq'], 'L0_attn_bq': _L0_attn_in['bq'], 'L0_attn_Wk': _L0_attn_in['Wk'], 'L0_attn_bk': _L0_attn_in['bk'], 'L0_attn_Wv': _L0_attn_in['Wv'], 'L0_attn_bv': _L0_attn_in['bv'], 'L0_attn_Wo': _L0_attn_in['Wo'], 'L0_attn_bo': _L0_attn_in['bo'], 'L0_xattn_wq_w': _L0_xattn_in['wq_w'], 'L0_xattn_wq_b': _L0_xattn_in['wq_b'], 'L0_xattn_wk_w': _L0_xattn_in['wk_w'], 'L0_xattn_wk_b': _L0_xattn_in['wk_b'], 'L0_xattn_wv_w': _L0_xattn_in['wv_w'], 'L0_xattn_wv_b': _L0_xattn_in['wv_b'], 'L0_xattn_wo_w': _L0_xattn_in['wo_w'], 'L0_xattn_wo_b': _L0_xattn_in['wo_b'], 'L0_ffn_ln_gamma': _L0_ffn_in['ln_gamma'], 'L0_ffn_ln_beta': _L0_ffn_in['ln_beta'], 'L0_ffn_mu': _L0_ffn_in['mu'], 'L0_ffn_scale': _L0_ffn_in['scale'], 'L0_ffn_w1': _L0_ffn_in['w1'], 'L0_ffn_b1': _L0_ffn_in['b1'], 'L0_ffn_w2': _L0_ffn_in['w2'], 'L0_ffn_b2': _L0_ffn_in['b2'], 'L1_attn_norm_in_w': _L1_attn_in['norm_in_w'], 'L1_attn_conv_w': _L1_attn_in['conv_w'], 'L1_attn_conv_b': _L1_attn_in['conv_b'], 'L1_attn_Wq': _L1_attn_in['Wq'], 'L1_attn_Wk': _L1_attn_in['Wk'], 'L1_attn_Wv': _L1_attn_in['Wv'], 'L1_attn_Wo': _L1_attn_in['Wo'], 'L1_attn_Wspike': _L1_attn_in['Wspike'], 'L1_attn_Wau': _L1_attn_in['Wau'], 'L1_attn_bau': _L1_attn_in['bau'], 'L1_attn_Wad': _L1_attn_in['Wad'], 'L1_attn_bad': _L1_attn_in['bad'], 'L1_attn_alpha_spike': _L1_attn_in['alpha_spike'], 'L1_attn_Wbeta': _L1_attn_in['Wbeta'], 'L1_attn_bbeta': _L1_attn_in['bbeta'], 'L1_attn_beta_spike': _L1_attn_in['beta_spike'], 'L1_attn_head_norm_w': _L1_attn_in['head_norm_w'], 'L1_attn_Wu1': _L1_attn_in['Wu1'], 'L1_attn_bu1': _L1_attn_in['bu1'], 'L1_attn_Wu2': _L1_attn_in['Wu2'], 'L1_attn_bu2': _L1_attn_in['bu2'], 'L1_attn_ff_norm_w': _L1_attn_in['ff_norm_w'], 'L1_attn_Wff1': _L1_attn_in['Wff1'], 'L1_attn_Wff3': _L1_attn_in['Wff3'], 'L1_attn_Wff2': _L1_attn_in['Wff2'], 'L1_ffn_gate_w': _L1_ffn_in['gate_w'], 'L1_ffn_w1': _L1_ffn_in['w1'], 'L1_ffn_w2': _L1_ffn_in['w2']}

def reference(x, ctx_1024, L0_attn_Wq, L0_attn_bq, L0_attn_Wk, L0_attn_bk, L0_attn_Wv, L0_attn_bv, L0_attn_Wo, L0_attn_bo, L0_xattn_wq_w, L0_xattn_wq_b, L0_xattn_wk_w, L0_xattn_wk_b, L0_xattn_wv_w, L0_xattn_wv_b, L0_xattn_wo_w, L0_xattn_wo_b, L0_ffn_ln_gamma, L0_ffn_ln_beta, L0_ffn_mu, L0_ffn_scale, L0_ffn_w1, L0_ffn_b1, L0_ffn_w2, L0_ffn_b2, L1_attn_norm_in_w, L1_attn_conv_w, L1_attn_conv_b, L1_attn_Wq, L1_attn_Wk, L1_attn_Wv, L1_attn_Wo, L1_attn_Wspike, L1_attn_Wau, L1_attn_bau, L1_attn_Wad, L1_attn_bad, L1_attn_alpha_spike, L1_attn_Wbeta, L1_attn_bbeta, L1_attn_beta_spike, L1_attn_head_norm_w, L1_attn_Wu1, L1_attn_bu1, L1_attn_Wu2, L1_attn_bu2, L1_attn_ff_norm_w, L1_attn_Wff1, L1_attn_Wff3, L1_attn_Wff2, L1_ffn_gate_w, L1_ffn_w1, L1_ffn_w2):
    import jax
    import jax.numpy as jnp

    def _L0_attn_ref(input_embeds, Wq, bq, Wk, bk, Wv, bv, Wo, bo):
        import math
        import jax, jax.numpy as jnp
        import numpy as np
        NUM_HEADS = 16
        HEAD_SIZE = 64
        HIDDEN = 128
        ROPE_BASE = 10000.0

        def _rope_cos_sin(seq_len, dim, dtype):
            inv_freq = 1.0 / ROPE_BASE ** (jnp.arange(0, dim, 2, dtype=jnp.float32) / dim)
            t = jnp.arange(seq_len, dtype=jnp.float32)
            freqs = jnp.einsum('s,d->sd', t, inv_freq)
            emb = jnp.concatenate([freqs, freqs], axis=-1)
            return (jnp.cos(emb).astype(dtype), jnp.sin(emb).astype(dtype))

        def _rotate_half(x):
            half = x.shape[-1] // 2
            return jnp.concatenate([-x[..., half:], x[..., :half]], axis=-1)

        def _apply_rope(q, k):
            cos, sin = _rope_cos_sin(q.shape[-2], q.shape[-1], q.dtype)
            q = q * cos + _rotate_half(q) * sin
            k = k * cos + _rotate_half(k) * sin
            return (q, k)
        B, S, _ = input_embeds.shape
        q = input_embeds @ Wq.T + bq
        k = input_embeds @ Wk.T + bk
        v = input_embeds @ Wv.T + bv

        def split_heads(x):
            return x.reshape(B, S, NUM_HEADS, HEAD_SIZE).transpose(0, 2, 1, 3)
        q, k, v = (split_heads(q), split_heads(k), split_heads(v))
        q, k = _apply_rope(q, k)
        scale = 1.0 / math.sqrt(HEAD_SIZE)
        scores = jnp.einsum('bhqd,bhkd->bhqk', q, k) * scale
        attn = jax.nn.softmax(scores, axis=-1)
        out = jnp.einsum('bhqk,bhkd->bhqd', attn, v)
        out = out.transpose(0, 2, 1, 3).reshape(B, S, NUM_HEADS * HEAD_SIZE)
        return out @ Wo.T + bo

    def _L0_xattn_ref(q, k, v, wq_w, wq_b, wk_w, wk_b, wv_w, wv_b, wo_w, wo_b):
        import jax, jax.numpy as jnp
        import numpy as np
        B, T, D, H = (2, 256, 128, 16)
        DH = D // H
        b, t, d = q.shape
        wq = (q @ wq_w.T + wq_b).reshape(b, t, H, DH)
        wk = (k @ wk_w.T + wk_b).reshape(b, t, H, DH)
        wv = (v @ wv_w.T + wv_b).reshape(b, t, H, DH)
        scores = jnp.einsum('bthd,bshd->bhts', wq, wk) / jnp.sqrt(jnp.float32(DH))
        probs = jax.nn.softmax(scores, axis=-1)
        attn = jnp.einsum('bhts,bshd->bthd', probs, wv)
        attn = attn.reshape(b, t, d)
        return attn @ wo_w.T + wo_b

    def _L0_ffn_ref(x, ln_gamma, ln_beta, mu, scale, w1, b1, w2, b2):
        import jax, jax.numpy as jnp
        import numpy as np
        LN_EPS = 1e-05
        NORM_EPS = 1e-12

        def _layernorm(x, gamma, beta):
            mu = x.mean(axis=-1, keepdims=True)
            var = ((x - mu) ** 2).mean(axis=-1, keepdims=True)
            return (x - mu) * jax.lax.rsqrt(var + LN_EPS) * gamma + beta

        def _l2norm(x, axis):
            n = jnp.sqrt((x ** 2).sum(axis=axis, keepdims=True))
            return x / jnp.maximum(n, NORM_EPS)
        B, N, D = x.shape
        _, E, S = mu.shape
        xn = _layernorm(x, ln_gamma, ln_beta)
        x_unit = _l2norm(xn, axis=-1)
        mu_unit = _l2norm(mu, axis=0)
        logits = jnp.einsum('bnd,des->bnes', x_unit * scale, mu_unit)
        dispatch = jax.nn.softmax(logits, axis=1)
        combine = jax.nn.softmax(logits.reshape(B, N, E * S), axis=-1).reshape(B, N, E, S)
        slot_in = jnp.einsum('bnd,bnes->besd', xn, dispatch)
        h = jax.nn.gelu(jnp.einsum('besd,edh->besh', slot_in, w1) + b1[None, :, None, :], approximate=False)
        slot_out = jnp.einsum('besh,ehd->besd', h, w2) + b2[None, :, None, :]
        out = jnp.einsum('besd,bnes->bnd', slot_out, combine)
        return out

    def _L1_attn_ref(x, norm_in_w, conv_w, conv_b, Wq, Wk, Wv, Wo, Wspike, Wau, bau, Wad, bad, alpha_spike, Wbeta, bbeta, beta_spike, head_norm_w, Wu1, bu1, Wu2, bu2, ff_norm_w, Wff1, Wff3, Wff2):
        import jax, jax.numpy as jnp
        import numpy as np
        EPS = 1e-06
        DECAY = 0.9
        THR = 0.5
        SBETA = 10.0
        KW = 4

        def _rms(x, w):
            return x * jax.lax.rsqrt(jnp.mean(x * x, axis=-1, keepdims=True) + EPS) * w
        B, T, D = x.shape
        H, dk = (alpha_spike.shape[1], alpha_spike.shape[2])
        dv = head_norm_w.shape[1]
        h = _rms(x, norm_in_w)
        hc = jnp.transpose(h, (0, 2, 1))
        conv = jax.lax.conv_general_dilated(hc, conv_w, window_strides=(1,), padding=[(KW - 1, 0)], dimension_numbers=('NCH', 'OIH', 'NCH'), feature_group_count=D)
        conv = conv + conv_b[None, :, None]
        h = jax.nn.silu(jnp.transpose(conv, (0, 2, 1)))

        def heads(z, d):
            return z.reshape(B, T, H, d)
        q = heads(h @ Wq, dk)
        k = heads(h @ Wk, dk)
        v = heads(h @ Wv, dv)
        q = q / (jnp.linalg.norm(q, axis=-1, keepdims=True) + 1e-06)
        k = k / (jnp.linalg.norm(k, axis=-1, keepdims=True) + 1e-06)
        drive = heads(h @ Wspike, dk)
        alpha_base = heads(jax.nn.silu(h @ Wau + bau) @ Wad + bad, dk)
        beta_base = h @ Wbeta + bbeta
        asp = alpha_spike[0]
        bsp = beta_spike[0]

        def step(carry, ins):
            s, mem = carry
            qt, kt, vt, dt, at, bt = ins
            mem = DECAY * mem + dt
            sg = jax.nn.sigmoid(SBETA * (mem - THR))
            hard = (mem > THR).astype(mem.dtype)
            spike = sg + jax.lax.stop_gradient(hard - sg)
            mem = mem - spike * THR
            alpha = jax.nn.sigmoid(at + asp * spike)
            beta = jax.nn.sigmoid(bt[..., None] + jnp.sum(spike * bsp, -1, keepdims=True))
            active = (jnp.sum(jnp.abs(spike), -1, keepdims=True) > 0).astype(qt.dtype)
            alpha = jnp.where(active > 0, alpha, jnp.ones_like(alpha))
            beta = beta * active
            s = s * alpha[..., None]
            pred = jnp.einsum('bhk,bhkv->bhv', kt, s)
            s = s + (beta * kt)[..., None] * (vt - pred)[:, :, None, :]
            out = jnp.einsum('bhk,bhkv->bhv', qt, s)
            return ((s, mem), out)
        s0 = jnp.zeros((B, H, dk, dv), x.dtype)
        m0 = jnp.zeros((B, H, dk), x.dtype)
        xs = (jnp.moveaxis(q, 1, 0), jnp.moveaxis(k, 1, 0), jnp.moveaxis(v, 1, 0), jnp.moveaxis(drive, 1, 0), jnp.moveaxis(alpha_base, 1, 0), jnp.moveaxis(beta_base, 1, 0))
        _, y = jax.lax.scan(step, (s0, m0), xs)
        y = jnp.moveaxis(y, 0, 1)
        y = y * jax.lax.rsqrt(jnp.mean(y * y, axis=-1, keepdims=True) + EPS) * head_norm_w
        y = y.reshape(B, T, H * dv)
        gate = jax.nn.sigmoid(jax.nn.silu(x @ Wu1 + bu1) @ Wu2 + bu2)
        y = x + y @ Wo * gate
        z = _rms(y, ff_norm_w)
        y = y + jax.nn.silu(z @ Wff1) * (z @ Wff3) @ Wff2
        return y

    def _L1_xattn_ref(x, w1, w2):
        import jax, jax.numpy as jnp
        import numpy as np
        E, T, H, F = (8, 256, 128, 512)
        h = jnp.einsum('eth,efh->etf', x, w1)
        a = jax.nn.gelu(h, approximate=True)
        return jnp.einsum('etf,efh->eth', a, w2)

    def _L1_ffn_ref(x, gate_w, w1, w2):
        import jax, jax.numpy as jnp
        import numpy as np
        NUM_EXPERTS = 8
        EXPERT_CAPACITY = 2.0
        DIM = 128
        HIDDEN_DIM = 512
        n, t, d = x.shape
        e = gate_w.shape[0]
        k = int(EXPERT_CAPACITY * t / e)
        scores = jnp.einsum('ntd,ed->nte', x, gate_w)
        probs = jax.nn.softmax(scores, axis=-1)
        g, m = jax.lax.top_k(probs.transpose(0, 2, 1), k)
        batch_idx = jnp.arange(n)[:, None, None]
        xin = x[batch_idx, m]
        h = jnp.einsum('nekd,edf->nekf', xin, w1)
        h = jax.nn.gelu(h, approximate=False)
        h = jnp.einsum('nekf,efd->nekd', h, w2)
        out_tok = g[..., None] * h
        out = jnp.zeros((n, t, d), dtype=x.dtype).at[batch_idx, m].add(out_tok)
        return out
    x = _layernorm(x + _L0_attn_ref(x, L0_attn_Wq, L0_attn_bq, L0_attn_Wk, L0_attn_bk, L0_attn_Wv, L0_attn_bv, L0_attn_Wo, L0_attn_bo), axis=-1)
    x = _layernorm(x + _L0_xattn_ref(x, ctx_1024, ctx_1024, L0_xattn_wq_w, L0_xattn_wq_b, L0_xattn_wk_w, L0_xattn_wk_b, L0_xattn_wv_w, L0_xattn_wv_b, L0_xattn_wo_w, L0_xattn_wo_b), axis=-1)
    x = _layernorm(x + _L0_ffn_ref(x, L0_ffn_ln_gamma, L0_ffn_ln_beta, L0_ffn_mu, L0_ffn_scale, L0_ffn_w1, L0_ffn_b1, L0_ffn_w2, L0_ffn_b2), axis=-1)
    x = _layernorm(x + _L1_attn_ref(x, L1_attn_norm_in_w, L1_attn_conv_w, L1_attn_conv_b, L1_attn_Wq, L1_attn_Wk, L1_attn_Wv, L1_attn_Wo, L1_attn_Wspike, L1_attn_Wau, L1_attn_bau, L1_attn_Wad, L1_attn_bad, L1_attn_alpha_spike, L1_attn_Wbeta, L1_attn_bbeta, L1_attn_beta_spike, L1_attn_head_norm_w, L1_attn_Wu1, L1_attn_bu1, L1_attn_Wu2, L1_attn_bu2, L1_attn_ff_norm_w, L1_attn_Wff1, L1_attn_Wff3, L1_attn_Wff2), axis=-1)
    x = _layernorm(x + _L1_xattn_ref(x, ctx_1024, ctx_1024), axis=-1)
    x = _layernorm(x + _L1_ffn_ref(x, L1_ffn_gate_w, L1_ffn_w1, L1_ffn_w2), axis=-1)
    return x

_drawn_inputs = setup_inputs


def setup_inputs(seed=0):
    import zlib

    import numpy as np

    out = dict(_drawn_inputs(seed))
    spreads = {'L0_attn_bq': (0.0, 0.8),
     'L0_attn_bk': (0.0, 0.8),
     'L0_attn_bv': (0.0, 0.1),
     'L0_attn_bo': (0.0, 0.1),
     'L0_xattn_wq_b': (0.0, 0.441),
     'L0_xattn_wk_b': (0.0, 0.8),
     'L0_xattn_wv_b': (0.0, 0.1),
     'L0_xattn_wo_b': (0.0, 0.1),
     'L0_ffn_ln_gamma': (1.0, 0.6),
     'L0_ffn_ln_beta': (0.0, 0.628),
     'L0_ffn_b1': (0.0, 0.8),
     'L0_ffn_b2': (0.0, 0.435),
     'L1_attn_norm_in_w': (1.0, 0.2),
     'L1_attn_conv_b': (0.0, 0.274),
     'L1_attn_bau': (0.0, 0.8),
     'L1_attn_bad': (0.0, 0.8),
     'L1_attn_alpha_spike': (0.0, 0.8),
     'L1_attn_bbeta': (0.0, 0.8),
     'L1_attn_beta_spike': (0.0, 0.8),
     'L1_attn_head_norm_w': (1.0, 0.6),
     'L1_attn_bu1': (0.0, 0.8),
     'L1_attn_bu2': (0.0, 0.8),
     'L1_attn_ff_norm_w': (1.0, 0.6)}
    factors = {'L0_ffn_mu': 8.0,
     'L1_attn_Wspike': 7.154,
     'L1_attn_Wau': 8.0,
     'L1_attn_Wad': 8.0,
     'L1_attn_Wbeta': 8.0,
     'L1_attn_Wu1': 8.0,
     'L1_attn_Wu2': 8.0,
     'L1_attn_Wff1': 8.0,
     'L1_attn_Wff3': 8.0,
     'L1_attn_Wff2': 8.0,
     'L1_ffn_gate_w': 6.037,
     'L1_ffn_w1': 5.309,
     'L1_ffn_w2': 5.271}
    for name, (base, spread) in spreads.items():
        noise = np.random.default_rng([zlib.crc32(name.encode()), seed]).standard_normal(out[name].shape)
        drawn = base * np.exp(spread * noise) if base else spread * noise
        out[name] = jnp.asarray(drawn.astype(out[name].dtype))
    for name, factor in factors.items():
        out[name] = (out[name] * factor).astype(out[name].dtype)
    return out
```

```python
from contextlib import ExitStack

import numpy as np

import concourse.bass as bass
from concourse import mybir

ALU = mybir.AluOpType
ACT = mybir.ActivationFunctionType
F32 = mybir.dt.float32
BF16 = mybir.dt.bfloat16
U32 = mybir.dt.uint32
AX_X = mybir.AxisListType.X
ds = bass.ds

P = 128
B, T, D = 64, 64, 128
N = B * T
TT = 2 * T
NT = N // TT
G = 512
NG = N // G
BG = G // T
LN_EPS = 1e-5
LOG_EXP = "natural_log_exp_and_others"
RMS_EPS = 1e-6


class Core:

    def hold(self, pe):
        pe.wait_ge(self.eye_made, 2)


class Stage:

    def __init__(self, k, name):
        self.nc, self.name, self.stack, self.own = k.nc, name, ExitStack(), []

    def __enter__(self):
        self.stack.__enter__()
        return self

    def __exit__(self, *e):
        done = self.stack.__exit__(*e)
        if self.own:
            self.nc.clear_and_free_semaphores(self.own)
            self.nc.all_engine_barrier()
        return done

    def sb(self, name, shape, dt=F32):
        return self.stack.enter_context(self.nc.sbuf_tensor(f"{self.name}_{name}", shape, dt))

    def sems(self, *names):
        new = [self.nc.alloc_semaphore(f"{self.name}_{n}") for n in names]
        self.own += new
        return new

    def block(self):
        return self.stack.enter_context(self.nc.Block())


def load_tokens(k):
    nc = k.nc
    with Stage(k, "load") as s:
        rows = s.sb("rows", [P, NT, D])
        eye_ready = k.eye_made
        loaded, ones_ready, turned, kept = s.sems("x_loaded", "ones_ready", "turned", "kept")
        block = s.block()
        NB = 8

        @block.sync
        def _(sync):
            sync.dma_start(rows[:, :, :], k.a["x"].rearrange("(n u) t d -> (u t) n d", u=2)).then_inc(loaded, 16)
            sync.dma_start(k.ctx_rows[:, :, :],
                           k.a["ctx_1024"].rearrange("(n u) t d -> (u t) n d", u=2)).then_inc(k.ctx_loaded, 16)

        @block.gpsimd
        def _(pool):
            pool.memset(k.eye[:, :], 0.0).then_inc(eye_ready, 1)
            pool.wait_ge(eye_ready, 1)
            pool.affine_select(out=k.eye[:, :], in_=k.eye[:, :], compare_op=ALU.not_equal, fill=1.0, base=0,
                               pattern=[[-1, P]], channel_multiplier=1).then_inc(eye_ready, 1)

        @block.tensor
        def _(pe):
            pe.wait_ge(eye_ready, 2)
            pe.wait_ge(loaded, 16)
            for g in range(NB):
                for j in range(4):
                    last = nc.tensor.transpose(k.bank[g][:, j * D:(j + 1) * D], rows[:, 4 * g + j, :], k.eye[:, :])
                last.then_inc(turned, 1)

        @block.vector
        def _(dve):
            dve.memset(k.ones_mean[:, :], 1.0 / D).then_inc(ones_ready, 1)
            dve.memset(k.ln_eps[:, :], LN_EPS).then_inc(ones_ready, 1)
            for g in range(NB):
                dve.wait_ge(turned, g + 1)
                dve.tensor_copy(k.X[:, g * G:(g + 1) * G], k.bank[g][:, :]).then_inc(kept, 1)


def turn_context(k, s, name):
    nc = k.nc
    k.ctxT = s.sb("ctxT", [P, N])
    with Stage(k, name) as t:
        turned, kept = t.sems("turned", "kept")
        block = t.block()

        @block.tensor
        def _(pe):
            pe.wait_ge(k.ctx_loaded, 16)
            for g in range(NG):
                for j in range(4):
                    last = nc.tensor.transpose(k.bank[g][:, j * D:(j + 1) * D], k.ctx_rows[:, 4 * g + j, :], k.eye[:, :])
                last.then_inc(turned, 1)

        @block.vector
        def _(dve):
            for g in range(NG):
                dve.wait_ge(turned, g + 1)
                dve.tensor_copy(k.ctxT[:, g * G:(g + 1) * G], k.bank[g][:, :]).then_inc(kept, 1)


def layer_norm(k, call):
    nc = k.nc
    base = call * NG
    with Stage(k, f"ln{call}") as s:
        sq = [s.sb(f"sq{u}", [P, G]) for u in range(2)]
        log_var = [s.sb(f"log_var{u}", [P, G]) for u in range(2)]
        rstd = [s.sb(f"rstd{u}", [P, G]) for u in range(2)]
        mean_ready, centred, squared, var_ready, log_ready, rstd_ready, normed = k.ln_sems
        block = s.block()
        mean, var = k.bank[0:2], k.bank[2:4]

        @block.tensor
        def _(pe):
            with pe.Fori(0, NG // 2) as i:
                for u in range(2):
                    nc.tensor.matmul(mean[u][:, :], k.ones_mean[:, :], k.X[:, ds(i * (2 * G) + u * G, G)],
                                     start=True, stop=True).then_inc(mean_ready, 1)
                for u in range(2):
                    pe.wait_ge(squared, i * 2 + (base + u + 1))
                    nc.tensor.matmul(var[u][:, :], k.ones_mean[:, :], sq[u][:, :],
                                     start=True, stop=True).then_inc(var_ready, 1)

        @block.vector
        def _(dve):
            with dve.Fori(0, NG // 2) as i:
                for u in range(2):
                    dve.wait_ge(mean_ready, i * 2 + (base + u + 1))
                    x = k.X[:, ds(i * (2 * G) + u * G, G)]
                    dve.tensor_tensor(x, x, mean[u][:, :], ALU.subtract).then_inc(centred, 1)
                for u in range(2):
                    dve.wait_ge(rstd_ready, i * 2 + (base + u + 1))
                    x = k.X[:, ds(i * (2 * G) + u * G, G)]
                    dve.tensor_tensor(x, x, rstd[u][:, :], ALU.mult).then_inc(normed, 1)

        @block.scalar
        def _(act):
            act.preload_act_table_set(LOG_EXP)
            with act.Fori(0, NG // 2) as i:
                for u in range(2):
                    act.wait_ge(centred, i * 2 + (base + u + 1))
                    act.activation(sq[u][:, :], k.X[:, ds(i * (2 * G) + u * G, G)], ACT.Square).then_inc(squared, 1)
                for u in range(2):
                    act.wait_ge(var_ready, i * 2 + (base + u + 1))
                    act.activation(log_var[u][:, :], var[u][:, :], ACT.Ln, bias=k.ln_eps[:, :]).then_inc(log_ready, 1)
                    act.wait_ge(log_ready, i * 2 + (base + u + 1))
                    act.activation(rstd[u][:, :], log_var[u][:, :], ACT.Exp, scale=-0.5).then_inc(rstd_ready, 1)


def attention_weights(k, s):
    nc = k.nc
    AD = AH * AK
    NR = AD // P
    w = Core()
    w.q, w.k, w.q_rot, w.k_rot, w.v = (s.sb(n, [P, AD], BF16) for n in ("wqT", "wkT", "wqT_rot", "wkT_rot", "wvT"))
    w.o = s.sb("woT", [P, NR, D])
    w.bq, w.bk, w.bq_rot, w.bk_rot = (s.sb(n, [1, AD], BF16) for n in ("bq", "bk", "bq_rot", "bk_rot"))
    w.ones = s.sb("ones", [1, TT], BF16)
    w.o_bias = s.sb("o_bias", [P, 1])
    w.rope_q, w.rope_k = s.sb("rope_q", [P, 2, T]), s.sb("rope_k", [P, 2, T])
    w.parts = s.sb("x_parts", [P, 3, N], BF16)
    with Stage(k, "attn_w") as t:
        rows = t.sb("rows", [P, 4, NR, P], BF16)
        eye = t.sb("eye", [P, P], BF16)
        left = t.sb("left", [P, 2, N // 2])
        bv_col, bo_col = t.sb("bv_col", [P, NR], BF16), t.sb("bo_col", [P, 1], BF16)
        bv, bo = t.sb("bv", [P, NR]), t.sb("bo", [P, 1])
        rows_loaded, small_loaded, eye_ready, turned, kept, part_ready, bias_ready, wobv_ready, small_ready = t.sems(
            "rows_loaded", "small_loaded", "eye_ready", "turned", "kept", "part_ready", "bias_ready", "wobv_ready",
            "small_ready")
        block = t.block()
        half_bank = [k.bank[i].bitcast(BF16) for i in range(8)]
        rotated = lambda ap: ap.rearrange("p (h c e) -> p h c e", c=2, e=AK // 2)

        @block.sync
        def _(sync):
            for n, name in enumerate(("Wq", "Wk", "Wv")):
                sync.dma_start(rows[:, n, :, :], k.a[f"L0_attn_{name}"].rearrange("(r p) i -> p r i", p=P)
                               ).then_inc(rows_loaded, 16)
            sync.dma_start(rows[:, 3, :, :], k.a["L0_attn_Wo"].rearrange("o (r p) -> o r p", p=P)
                           ).then_inc(rows_loaded, 16)

        @block.gpsimd
        def _(pool):
            flat = lambda name: k.a[name].rearrange("(o n) -> o n", o=1)
            with nc.allow_non_contiguous_dma(reason="biases: 2 KB"):
                pool.dma_start(w.bq[:, :], flat("L0_attn_bq")).then_inc(small_loaded, 16)
                pool.dma_start(w.bk[:, :], flat("L0_attn_bk")).then_inc(small_loaded, 16)
                for c in range(2):
                    pool.dma_start(rotated(w.bq_rot[:, :])[:, :, c, :], rotated(flat("L0_attn_bq"))[:, :, 1 - c, :]
                                   ).then_inc(small_loaded, 16)
                    pool.dma_start(rotated(w.bk_rot[:, :])[:, :, c, :], rotated(flat("L0_attn_bk"))[:, :, 1 - c, :]
                                   ).then_inc(small_loaded, 16)
                pool.dma_start(bv_col[:, :], k.a["L0_attn_bv"].rearrange("(r p) -> p r", p=P)).then_inc(small_loaded, 16)
                pool.dma_start(bo_col[:, :], k.a["L0_attn_bo"].rearrange("(p o) -> p o", o=1)).then_inc(small_loaded, 16)
                pool.dma_start(w.rope_q[:, :, :], k.a["rope_q"]).then_inc(small_loaded, 16)
                pool.dma_start(w.rope_k[:, :, :], k.a["rope_k"]).then_inc(small_loaded, 16)

        @block.tensor
        def _(pe):
            pe.wait_ge(rows_loaded, 64)
            pe.wait_ge(eye_ready, 2)
            for n in range(4):
                for r in range(NR):
                    last = nc.tensor.transpose(half_bank[n][:, r * P:(r + 1) * P], rows[:, n, r, :], eye[:, :])
                last.then_inc(turned, 1)
            pe.wait_ge(kept, 6)
            pe.wait_ge(bias_ready, 2)
            for r in range(NR):
                last = nc.tensor.matmul(k.bank[4][:, 0:1], w.o[:, r, :], bv[:, r:r + 1], start=(r == 0),
                                        stop=(r == NR - 1))
            last.then_inc(wobv_ready, 1)

        @block.vector
        def _(dve):
            dve.memset(w.ones[:, :], 1.0).then_inc(eye_ready, 1)
            dve.tensor_copy(eye[:, :], k.eye[:, :]).then_inc(eye_ready, 1)
            for c in range(2):
                cols = slice(c * N // 2, (c + 1) * N // 2)
                for part in range(3):
                    src = k.X[:, cols] if part == 0 else left[:, part - 1, :]
                    if part:
                        dve.wait_ge(part_ready, 5 * c + 2 * part)
                    dve.tensor_copy(w.parts[:, part, cols], src).then_inc(part_ready, 1)
                    if part < 2:
                        dve.wait_ge(part_ready, 5 * c + 2 * part + 1)
                        dve.tensor_tensor(left[:, part, :], src, w.parts[:, part, cols], ALU.subtract
                                          ).then_inc(part_ready, 1)
            for n, (plain, rot) in enumerate(((w.q, w.q_rot), (w.k, w.k_rot), (w.v, None), (w.o, None))):
                dve.wait_ge(turned, n + 1)
                dst = plain[:, :] if n < 3 else plain[:, :, :].rearrange("p r o -> p (r o)")
                dve.tensor_copy(dst, half_bank[n][:, 0:AD]).then_inc(kept, 1)
                if rot is not None:
                    for c in range(2):
                        last = dve.tensor_copy(rotated(rot[:, :])[:, :, c, :],
                                               rotated(half_bank[n][:, 0:AD])[:, :, 1 - c, :])
                    last.then_inc(kept, 1)
            dve.wait_ge(small_loaded, 16 * 10)
            dve.tensor_copy(bv[:, :], bv_col[:, :]).then_inc(bias_ready, 1)
            dve.tensor_copy(bo[:, :], bo_col[:, :]).then_inc(bias_ready, 1)
            dve.wait_ge(bias_ready, 2)
            dve.wait_ge(wobv_ready, 1)
            dve.tensor_tensor(w.o_bias[:, :], k.bank[4][:, 0:1], bo[:, :], ALU.add).then_inc(small_ready, 1)
    return w


AH, AK = 16, 64
HP = AH * AK // P


def rope_attention(k):
    nc = k.nc
    with Stage(k, "attn") as s:
        w = attention_weights(k, s)
        HG = HP // 2
        qk = [s.sb(n, [P, HP, TT]) for n in ("q", "k")]
        by_cos = [s.sb(f"by_cos{r}", [P, G]) for r in range(2)]
        by_sin = [s.sb(f"by_sin{r}", [P, G]) for r in range(2)]
        v = [s.sb(f"v{u}", [P, AH * AK]) for u in range(2)]
        shifted, expd, probs = (s.sb(n, [P, HP, TT]) for n in ("shifted", "exp", "probs"))
        probsT = s.sb("probsT", [P, HP, TT])
        heads = s.sb("heads", [P, 2, HP, T])
        top, total, inv = (s.sb(n, [P, AH]) for n in ("row_max", "row_sum", "row_inv"))
        (projected, turned, roped, v_kept, scored, maxed, shift_ready, exp_ready, summed, inv_ready, probs_ready,
         probs_turned, probsT_ready, attended, heads_ready, out_ready, added) = s.sems(
            "projected", "cos_sin_ready", "roped", "v_kept", "scored", "maxed", "shift_ready", "exp_ready", "summed",
            "inv_ready", "probs_ready", "probs_turned", "probsT_ready", "attended", "heads_ready", "out_ready", "added")
        block = s.block()
        PROJ = 5
        S_BANK = k.psum[:, 4:6, :].rearrange("p b c -> p (b c)")
        O_BANK = k.psum[:, 6:8, :]
        Y_BANK = k.bank[3][:, 0:TT]
        KINDS = [(w.q, w.q_rot, w.bq, w.bq_rot), (w.k, w.k_rot, w.bk, w.bk_rot)]

        def pe_project(pe, t):
            for st in range(4):
                if st >= 2:
                    pe.wait_ge(turned, t * 4 + (st - 1))
                elif st == 1 and (not isinstance(t, int) or t > 1):
                    pe.wait_ge(added, t)
                elif st == 0 and not isinstance(t, int):
                    pe.wait_ge(v_kept, t)
                c0 = (st // 2) * HG
                for wt, bias, bank in zip(KINDS[st % 2][0:2], KINDS[st % 2][2:4], (2 * (st % 2), 2 * (st % 2) + 1)):
                    for c in range(HG):
                        out = k.bank[bank][:, c * TT:(c + 1) * TT]
                        cols = slice((c0 + c) * P, (c0 + c + 1) * P)
                        for part in range(3):
                            nc.tensor.matmul(out, wt[:, cols], w.parts[:, part, ds(t * TT, TT)],
                                             start=(part == 0), stop=False)
                        last = nc.tensor.matmul(out, bias[:, cols], w.ones[:, :], start=False, stop=True)
                last.then_inc(projected, 1)
            pe.wait_ge(turned, t * 4 + 3)
            for half in range(2):
                for part in range(3):
                    last = nc.tensor.matmul(k.bank[half][:, :], w.parts[:, part, ds(t * TT, TT)],
                                            w.v[:, half * G:(half + 1) * G], start=(part == 0), stop=(part == 2))
            last.then_inc(projected, 1)

        def pe_scores(pe, t):
            for hp in range(HP):
                for b in range(2):
                    for j in range(2):
                        r, cols = slice(j * AK, (j + 1) * AK), slice(b * T, (b + 1) * T)
                        last = nc.tensor.matmul(S_BANK[r, hp * TT + b * T:hp * TT + (b + 1) * T],
                                                qk[0][r, hp, cols], qk[1][r, hp, cols], start=True, stop=True)
            last.then_inc(scored, 1)

        def pe_values(pe, t, u, more):
            pe.wait_ge(probs_ready, t + 1)
            for hp in range(HP):
                last = nc.tensor.transpose(S_BANK[:, hp * TT:(hp + 1) * TT], probs[:, hp, :], k.eye[:, :])
            last.then_inc(probs_turned, 1)
            k.hold(pe)
            pe.wait_ge(probsT_ready, t + 1)
            pe.wait_ge(v_kept, t + 1)
            for hp in range(HP):
                for j in range(2):
                    for b in range(2):
                        r, h = slice(b * T, (b + 1) * T), 2 * hp + j
                        last = nc.tensor.matmul(O_BANK[j * AK:(j + 1) * AK, b, hp * T:(hp + 1) * T],
                                                v[u][r, h * AK:(h + 1) * AK], probsT[r, hp, j * T:(j + 1) * T],
                                                start=True, stop=True)
            last.then_inc(attended, 1)
            pe.wait_ge(heads_ready, t + 1)
            if more:
                pe.wait_ge(roped, t * 4 + 8)
            for hp in range(HP):
                last = nc.tensor.matmul(Y_BANK, w.o[:, hp, :], heads[:, :, hp, :], start=(hp == 0),
                                        stop=(hp == HP - 1))
            last.then_inc(out_ready, 1)

        def dve_rope(dve, t, st):
            dve.wait_ge(projected, t * PROJ + (st + 1))
            if not isinstance(t, int) or st >= 2:
                dve.wait_ge(roped, t * 4 + (st - 1))
            tab, r = (w.rope_q, w.rope_k)[st % 2], st % 2
            for part, dst in enumerate((by_cos[r], by_sin[r])):
                last = dve.tensor_tensor(dst[:, :].rearrange("p (n t) -> p n t", t=T),
                                         k.bank[2 * r + part][:, :].rearrange("p (n t) -> p n t", t=T),
                                         tab[:, part:part + 1, :].to_broadcast([P, 2 * HG, T]), ALU.mult)
            last.then_inc(turned, 1)

        def rows_of(ap):
            return ap.rearrange("p h (b t) -> p (h b) t", b=2)

        def dve_shift(dve, t):
            dve.wait_ge(scored, t + 1)
            sc = S_BANK.rearrange("p (h t) -> p h t", t=T)
            dve.tensor_reduce(top[:, :], sc, AX_X, ALU.max).then_inc(maxed, 1)
            dve.wait_ge(maxed, t + 1)
            dve.tensor_tensor(rows_of(shifted[:, :, :]), sc, top[:, :].unsqueeze(2).to_broadcast([P, AH, T]),
                              ALU.subtract).then_inc(shift_ready, 1)

        def dve_sum(dve, t):
            dve.wait_ge(exp_ready, t + 1)
            dve.tensor_reduce(total[:, :], rows_of(expd[:, :, :]), AX_X, ALU.add).then_inc(summed, 1)
            dve.wait_ge(summed, t + 1)
            dve.reciprocal(inv[:, :], total[:, :]).then_inc(inv_ready, 1)

        def dve_add(dve, t):
            dve.wait_ge(out_ready, t + 1)
            x = k.X[:, ds(t * TT, TT)]
            dve.scalar_tensor_tensor(x, Y_BANK, w.o_bias[:, :], x, ALU.add, ALU.add).then_inc(added, 1)

        def pool_rope(pool, t, st):
            pool.wait_ge(turned, t * 4 + (st + 1))
            if not isinstance(t, int):
                pool.wait_ge(scored, t)
            c0 = (st // 2) * HG
            pool.tensor_tensor(qk[st % 2][:, c0:c0 + HG, :].rearrange("p h t -> p (h t)"), by_cos[st % 2][:, :],
                               by_sin[st % 2][:, :], ALU.add).then_inc(roped, 1)

        def pool_norm(pool, t):
            pool.wait_ge(inv_ready, t + 1)
            pool.tensor_tensor(rows_of(probs[:, :, :]), rows_of(expd[:, :, :]),
                               inv[:, :].unsqueeze(2).to_broadcast([P, AH, T]), ALU.mult).then_inc(probs_ready, 1)

        def act_v(act, t, u):
            act.wait_ge(projected, t * PROJ + PROJ)
            act.activation(v[u][:, :], k.psum[:, 0:2, :].rearrange("p b c -> p (b c)"), ACT.Copy).then_inc(v_kept, 1)

        def act_exp(act, t):
            act.wait_ge(shift_ready, t + 1)
            act.activation(expd[:, :, :], shifted[:, :, :], ACT.Exp).then_inc(exp_ready, 1)

        def act_values(act, t):
            act.wait_ge(probs_turned, t + 1)
            act.activation(probsT[:, :, :].rearrange("p h t -> p (h t)"), S_BANK, ACT.Copy).then_inc(probsT_ready, 1)
            act.wait_ge(attended, t + 1)
            act.activation(heads[:, :, :, :].rearrange("p b h t -> p b (h t)"), O_BANK, ACT.Copy
                           ).then_inc(heads_ready, 1)

        def tiles(eng, body):
            with eng.Fori(0, NT // 2 - 1) as i:
                for u in range(2):
                    body(i * 2 + u, u, True)
            body(NT - 2, 0, True)
            body(NT - 1, 1, False)

        @block.tensor
        def _(pe):
            pe_project(pe, 0)
            pe.wait_ge(roped, 4)

            def body(t, u, more):
                pe_scores(pe, t)
                if more:
                    pe_project(pe, t + 1)
                pe_values(pe, t, u, more)
            tiles(pe, body)

        @block.vector
        def _(dve):
            dve.memset(top[:, :], 0.0).then_inc(added, 1)
            for st in range(4):
                dve_rope(dve, 0, st)

            def body(t, u, more):
                dve_shift(dve, t)
                for st in range(4):
                    if st == 2:
                        dve_sum(dve, t)
                    if more:
                        dve_rope(dve, t + 1, st)
                dve_add(dve, t)
            tiles(dve, body)

        @block.gpsimd
        def _(pool):
            for st in range(4):
                pool_rope(pool, 0, st)

            def body(t, u, more):
                for st in range(4):
                    if st == 2:
                        pool_norm(pool, t)
                    if more:
                        pool_rope(pool, t + 1, st)
            tiles(pool, body)

        @block.scalar
        def _(act):
            act_v(act, 0, 0)

            def body(t, u, more):
                act_exp(act, t)
                if more:
                    act_v(act, t + 1, 1 - u)
                act_values(act, t)
            tiles(act, body)


XH, XK = 16, 8
XG = 4


def turn_square(k, name, loads, out, bank0=0):
    nc = k.nc
    with Stage(k, name) as s:
        rows = s.sb("rows", [P, len(loads), D])
        loaded, turned, kept = s.sems("loaded", "turned", "kept")
        block = s.block()

        @block.sync
        def _(sync):
            for i, w in enumerate(loads):
                sync.dma_start(rows[:, i, :], w).then_inc(loaded, 16)

        @block.tensor
        def _(pe):
            pe.wait_ge(loaded, 16 * len(loads))
            for i in range(len(loads)):
                last = nc.tensor.transpose(k.bank[bank0][:, i * D:(i + 1) * D], rows[:, i, :], k.eye[:, :])
            last.then_inc(turned, 1)

        @block.vector
        def _(dve):
            dve.wait_ge(turned, 1)
            dve.tensor_copy(out.rearrange("p n d -> p (n d)"), k.bank[bank0][:, 0:len(loads) * D]).then_inc(kept, 1)


def column(ap):
    return ap.rearrange("(p o) -> p o", o=1)


def cross_attention(k):
    nc = k.nc
    with Stage(k, "xattn") as s:
        wT = s.sb("wT", [P, 4, D])
        turn_context(k, s, "xattn_ctx")
        turn_square(k, "xattn_w", [k.a[f"L0_xattn_{n}_w"] for n in ("wq", "wk", "wv", "wo")], wT[:, :, :])
        qT, kT = s.sb("qT", [P, N]), s.sb("kT", [P, N])
        v = s.sb("v", [P, NT, D])
        bias = s.sb("bias", [P, 4])
        bq, o_bias, head_mask = s.sb("bq_scaled", [P, 1]), s.sb("o_bias", [P, 1]), s.sb("head_mask", [P, 4])
        scale = float(XK) ** -0.5
        with Stage(k, "xproj") as t:
            ctx_g = [t.sb(f"ctx{u}", [P, G]) for u in range(2)]
            bias_loaded, masked, staged, projected, kept, small_ready, wobv_ready, scaled_ready, ob_ready = t.sems(
                "bias_loaded", "masked", "ctx_staged", "projected", "kept", "small_ready", "wobv_ready", "scaled_ready",
                "o_bias_ready")
            block = t.block()

            @block.sync
            def _(sync):
                with nc.allow_non_contiguous_dma(reason="four columns of biases"):
                    for i, n in enumerate(("wq", "wk", "wv", "wo")):
                        sync.dma_start(bias[:, i:i + 1], column(k.a[f"L0_xattn_{n}_b"])).then_inc(bias_loaded, 16)

            @block.gpsimd
            def _(pool):
                pool.memset(head_mask[:, :], 1.0).then_inc(masked, 1)
                for g in range(XG):
                    m = head_mask[32 * g:32 * g + 32, :]
                    pool.wait_ge(masked, 2 * g + 1)
                    pool.affine_select(out=m, in_=m, compare_op=ALU.is_ge, fill=0.0, base=0,
                                       pattern=[[-XK, 4]], channel_multiplier=1).then_inc(masked, 1)
                    pool.wait_ge(masked, 2 * g + 2)
                    pool.affine_select(out=m, in_=m, compare_op=ALU.is_ge, fill=0.0, base=XK - 1,
                                       pattern=[[XK, 4]], channel_multiplier=-1).then_inc(masked, 1)

            @block.tensor
            def _(pe):
                pe.wait_ge(bias_loaded, 64)
                nc.tensor.matmul(k.bank[6][:, 0:1], wT[:, 3, :], bias[:, 2:3], start=True, stop=True
                                 ).then_inc(wobv_ready, 1)
                with pe.Fori(0, NG // 2) as i:
                    for u in range(2):
                        g_at = ds(i * (2 * G) + u * G, G)
                        nc.tensor.matmul(k.bank[3 * u][:, :], wT[:, 0, :], k.X[:, g_at], start=True, stop=True)
                        nc.tensor.matmul(k.bank[3 * u + 1][:, :], wT[:, 1, :], k.ctxT[:, g_at], start=True, stop=True)
                        pe.wait_ge(staged, i * 2 + (u + 1))
                        for n in range(4):
                            last = nc.tensor.matmul(k.bank[3 * u + 2][:, n * D:(n + 1) * D],
                                                    ctx_g[u][:, n * D:(n + 1) * D], wT[:, 2, :], start=True, stop=True)
                        last.then_inc(projected, 1)
                    pe.wait_ge(kept, i * 2 + 2)
                    pe.wait_ge(small_ready, i * 2 + 2)

            @block.vector
            def _(dve):
                dve.wait_ge(bias_loaded, 64)
                dve.tensor_scalar(bq[:, :], bias[:, 0:1], scale, None, ALU.mult).then_inc(scaled_ready, 1)
                dve.wait_ge(wobv_ready, 1)
                dve.tensor_tensor(o_bias[:, :], k.bank[6][:, 0:1], bias[:, 3:4], ALU.add).then_inc(ob_ready, 1)
                with dve.Fori(0, NG // 2) as i:
                    for u in range(2):
                        dve.tensor_copy(ctx_g[u][:, :], k.ctxT[:, ds(i * (2 * G) + u * G, G)]).then_inc(staged, 1)
                    for u in range(2):
                        dve.wait_ge(projected, i * 2 + (u + 1))
                        dve.tensor_copy(v[:, ds(i * 8 + u * 4, 4), :].rearrange("p n d -> p (n d)"),
                                        k.bank[3 * u + 2][:, :]).then_inc(kept, 1)

            @block.scalar
            def _(act):
                act.wait_ge(scaled_ready, 1)
                with act.Fori(0, NG // 2) as i:
                    for u in range(2):
                        g_at = ds(i * (2 * G) + u * G, G)
                        act.wait_ge(projected, i * 2 + (u + 1))
                        act.activation(qT[:, g_at], k.bank[3 * u][:, :], ACT.Identity, scale=scale, bias=bq[:, :])
                        act.activation(kT[:, g_at], k.bank[3 * u + 1][:, :], ACT.Identity, bias=bias[:, 1:2]
                                       ).then_inc(small_ready, 1)

        q_t = [s.sb(f"q{u}", [P, TT]) for u in range(2)]
        v_t = [s.sb(f"v{u}", [P, D]) for u in range(2)]
        kx = [s.sb(f"kx{u}", [P, 4, TT]) for u in range(2)]
        W = 4 * TT // 2
        shifted, expd, probs, probsT = (s.sb(n, [P, XG, W]) for n in ("shifted", "exp", "probs", "probsT"))
        top, total, inv = (s.sb(n, [P, XG * 4]) for n in ("row_max", "row_sum", "row_inv"))
        mixed, mixedT = s.sb("mixed", [P, D]), s.sb("mixedT", [P, TT])
        (qv_staged, kx_ready, scored, maxed, shift_ready, exp_ready, summed, inv_ready, probs_ready, probs_turned,
         probsT_ready, mixed_ready, mixed_kept, mixed_turned, mixedT_ready, out_ready, added) = s.sems(
            "qv_staged", "kx_ready", "scored", "maxed", "shift_ready", "exp_ready", "summed", "inv_ready", "probs_ready",
            "probs_turned", "probsT_ready", "mixed_ready", "mixed_kept", "mixed_turned", "mixedT_ready", "out_ready",
            "added")
        block = s.block()
        S_BANK = k.psum[:, 0:4, 0:W]
        PT_BANK = k.psum[:, 4:6, :].rearrange("p b c -> p (b c)")

        def pe_scores(pe, t, u):
            k.hold(pe)
            pe.wait_ge(qv_staged, t + 1)
            pe.wait_ge(kx_ready, t + 1)
            for b in range(2):
                for h2 in range(2):
                    for j in range(2):
                        for g in range(XG):
                            r = slice(32 * g, 32 * g + 32)
                            last = nc.tensor.matmul(k.psum[j * T:(j + 1) * T, g, h2 * TT + b * T:h2 * TT + (b + 1) * T],
                                                    q_t[u][r, b * T:(b + 1) * T], kx[u][r, 2 * h2 + j, b * T:(b + 1) * T],
                                                    start=True, stop=True)
            last.then_inc(scored, 1)

        def pe_turn(pe, t):
            pe.wait_ge(probs_ready, t + 1)
            for g in range(XG):
                for h2 in range(2):
                    last = nc.tensor.transpose(PT_BANK[:, (2 * g + h2) * TT:(2 * g + h2 + 1) * TT],
                                               probs[:, g, h2 * TT:(h2 + 1) * TT], k.eye[:, :])
            last.then_inc(probs_turned, 1)

        def pe_values(pe, t, u):
            k.hold(pe)
            pe.wait_ge(probsT_ready, t + 1)
            for g in range(XG):
                for h2 in range(2):
                    for j in range(2):
                        for b in range(2):
                            r, h = slice(b * T, (b + 1) * T), 4 * g + 2 * h2 + j
                            last = nc.tensor.matmul(k.bank[6][r, h * XK:(h + 1) * XK],
                                                    probsT[r, g, h2 * TT + j * T:h2 * TT + (j + 1) * T],
                                                    v_t[u][r, h * XK:(h + 1) * XK], start=True, stop=True)
            last.then_inc(mixed_ready, 1)
            pe.wait_ge(mixed_kept, t + 1)
            nc.tensor.transpose(k.bank[7][:, 0:TT], mixed[:, :], k.eye[:, :]).then_inc(mixed_turned, 1)
            pe.wait_ge(mixedT_ready, t + 1)
            nc.tensor.matmul(k.bank[7][:, TT:2 * TT], wT[:, 3, :], mixedT[:, :], start=True, stop=True
                             ).then_inc(out_ready, 1)

        def dve_spread(dve, t, u):
            dve.tensor_tensor(kx[u][:, :, :], kT[:, ds(t * TT, TT)].unsqueeze(1).to_broadcast([P, 4, TT]),
                              head_mask[:, :].unsqueeze(2).to_broadcast([P, 4, TT]), ALU.mult).then_inc(kx_ready, 1)

        def dve_shift(dve, t):
            dve.wait_ge(scored, t + 1)
            sc = S_BANK.rearrange("p g (h k) -> p g h k", k=T)
            dve.tensor_reduce(top[:, :].rearrange("p (g h) -> p g h", g=XG), sc, AX_X, ALU.max).then_inc(maxed, 1)
            dve.wait_ge(maxed, t + 1)
            dve.tensor_tensor(shifted[:, :, :].rearrange("p g (h k) -> p g h k", k=T), sc,
                              top[:, :].rearrange("p (g h) -> p g h", g=XG).unsqueeze(3).to_broadcast([P, XG, 4, T]),
                              ALU.subtract).then_inc(shift_ready, 1)

        def rows_of(ap):
            return ap.rearrange("p g (h k) -> p (g h) k", k=T)

        def dve_sum(dve, t):
            dve.wait_ge(exp_ready, t + 1)
            dve.tensor_reduce(total[:, :], rows_of(expd[:, :, :]), AX_X, ALU.add).then_inc(summed, 1)
            dve.wait_ge(summed, t + 1)
            dve.reciprocal(inv[:, :], total[:, :]).then_inc(inv_ready, 1)

        def dve_add(dve, t):
            dve.wait_ge(out_ready, t + 1)
            x = k.X[:, ds(t * TT, TT)]
            dve.scalar_tensor_tensor(x, k.bank[7][:, TT:2 * TT], o_bias[:, :], x, ALU.add, ALU.add).then_inc(added, 1)

        def act_stage(act, t, u):
            act.activation(q_t[u][:, :], qT[:, ds(t * TT, TT)], ACT.Copy)
            act.activation(v_t[u][:, :], v[:, ds(t, 1), :], ACT.Copy).then_inc(qv_staged, 1)

        def tiles(eng, body):
            with eng.Fori(0, NT // 2 - 1) as i:
                for u in range(2):
                    body(i * 2 + u, u, True)
            body(NT - 2, 0, True)
            body(NT - 1, 1, False)

        @block.tensor
        def _(pe):
            pe_scores(pe, 0, 0)

            def body(t, u, more):
                pe_turn(pe, t)
                if more:
                    pe_scores(pe, t + 1, 1 - u)
                pe_values(pe, t, u)
            tiles(pe, body)

        @block.vector
        def _(dve):
            dve_spread(dve, 0, 0)
            dve_shift(dve, 0)

            def body(t, u, more):
                if more:
                    dve_spread(dve, t + 1, 1 - u)
                dve_sum(dve, t)
                if more:
                    dve_shift(dve, t + 1)
                dve_add(dve, t)
            tiles(dve, body)

        @block.gpsimd
        def _(pool):
            def body(t, u, more):
                pool.wait_ge(inv_ready, t + 1)
                pool.tensor_tensor(rows_of(probs[:, :, :]), rows_of(expd[:, :, :]),
                                   inv[:, :].unsqueeze(2).to_broadcast([P, XG * 4, T]), ALU.mult
                                   ).then_inc(probs_ready, 1)
            tiles(pool, body)

        @block.scalar
        def _(act):
            act_stage(act, 0, 0)

            def body(t, u, more):
                act.wait_ge(shift_ready, t + 1)
                act.activation(expd[:, :, :], shifted[:, :, :], ACT.Exp).then_inc(exp_ready, 1)
                if more:
                    act_stage(act, t + 1, 1 - u)
                act.wait_ge(probs_turned, t + 1)
                act.activation(probsT[:, :, :].rearrange("p g c -> p (g c)"), PT_BANK, ACT.Copy
                               ).then_inc(probsT_ready, 1)
                act.wait_ge(mixed_ready, t + 1)
                act.activation(mixed[:, :], k.bank[6][:, 0:D], ACT.Copy).then_inc(mixed_kept, 1)
                act.wait_ge(mixed_turned, t + 1)
                act.activation(mixedT[:, :], k.bank[7][:, 0:TT], ACT.Copy).then_inc(mixedT_ready, 1)
            tiles(act, body)


ME, MS, MH = 16, 16, 32
SLOTS = ME * MS
MG = 4
UNIT_SHIFT = 30


def mixture_inputs(k, s):
    nc = k.nc
    f = Core()
    f.xn, f.xs = s.sb("xn", [P, N]), s.sb("xs", [P, N])
    f.mu = s.sb("mu_unit", [P, SLOTS])
    with Stage(k, "mixin") as t:
        cols = t.sb("cols", [P, 3])
        mu, mu_n2 = t.sb("mu", [P, SLOTS]), t.sb("mu_n2", [P, SLOTS])
        unit_bias = t.sb("unit_bias", [P, 1])
        sq, n2, log, inv, xc = ([t.sb(f"{n}{u}", [P, G]) for u in range(2)] for n in ("sq", "n2", "log", "inv", "xc"))
        (cols_loaded, mu_loaded, const_ready, mean_ready, centred, squared, var_ready, log_ready, rstd_ready, scaled,
         xn_ready, sq2_ready, n2_ready, n2_kept, log2_ready, inv_ready, xs_ready) = t.sems(
            "cols_loaded", "mu_loaded", "const_ready", "mean_ready", "centred", "squared", "var_ready", "log_ready",
            "rstd_ready", "scaled", "xn_ready", "sq2_ready", "n2_ready", "n2_kept", "log2_ready", "inv_ready", "xs_ready")
        block = t.block()
        mean, var, norm = k.bank[0:2], k.bank[2:4], k.bank[4:6]

        @block.sync
        def _(sync):
            with nc.allow_non_contiguous_dma(reason="three columns"):
                sync.dma_start(cols[:, 0:1], column(k.a["L0_ffn_ln_gamma"])).then_inc(cols_loaded, 16)
                sync.dma_start(cols[:, 1:2], column(k.a["L0_ffn_ln_beta"])).then_inc(cols_loaded, 16)
                sync.dma_start(cols[:, 2:3], k.a["L0_ffn_scale"].partition_broadcast(P)).then_inc(cols_loaded, 16)
            sync.dma_start(mu[:, :], k.a["L0_ffn_mu"].rearrange("d e s -> d (e s)")).then_inc(mu_loaded, 16)

        @block.tensor
        def _(pe):
            pe.wait_ge(sq2_ready, 1)
            nc.tensor.matmul(norm[1][:, 0:SLOTS], k.ones_mean[:, :], sq[1][:, 0:SLOTS], start=True, stop=True
                             ).then_inc(n2_ready, 1)
            with pe.Fori(0, NG // 2) as i:
                for u in range(2):
                    nc.tensor.matmul(mean[u][:, :], k.ones_mean[:, :], k.X[:, ds(i * (2 * G) + u * G, G)],
                                     start=True, stop=True).then_inc(mean_ready, 1)
                for u in range(2):
                    pe.wait_ge(squared, i * 2 + (u + 1))
                    nc.tensor.matmul(var[u][:, :], k.ones_mean[:, :], sq[u][:, :],
                                     start=True, stop=True).then_inc(var_ready, 1)
                for u in range(2):
                    pe.wait_ge(sq2_ready, i * 2 + (u + 2))
                    nc.tensor.matmul(norm[u][:, :], k.ones_mean[:, :], sq[u][:, :],
                                     start=True, stop=True).then_inc(n2_ready, 1)

        @block.vector
        def _(dve):
            dve.memset(unit_bias[:, :], 0.5 * UNIT_SHIFT * float(np.log(2.0))).then_inc(const_ready, 1)
            dve.wait_ge(n2_ready, 1)
            dve.tensor_scalar(n2[1][:, 0:SLOTS], norm[1][:, 0:SLOTS], float(D), 1e-24, ALU.mult, ALU.max
                              ).then_inc(n2_kept, 1)
            dve.wait_ge(inv_ready, 1)
            dve.tensor_tensor(f.mu[:, :], mu[:, :], inv[1][:, 0:SLOTS], ALU.mult).then_inc(xs_ready, 1)
            dve.wait_ge(cols_loaded, 48)
            with dve.Fori(0, NG // 2) as i:
                for u in range(2):
                    dve.wait_ge(mean_ready, i * 2 + (u + 1))
                    dve.tensor_tensor(xc[u][:, :], k.X[:, ds(i * (2 * G) + u * G, G)], mean[u][:, :], ALU.subtract
                                      ).then_inc(centred, 1)
                for u in range(2):
                    dve.wait_ge(rstd_ready, i * 2 + (u + 1))
                    xn = f.xn[:, ds(i * (2 * G) + u * G, G)]
                    dve.tensor_tensor(xn, xc[u][:, :], inv[u][:, :], ALU.mult).then_inc(scaled, 1)
                    dve.wait_ge(scaled, i * 2 + (u + 1))
                    dve.tensor_scalar(xn, xn, cols[:, 0:1], cols[:, 1:2], ALU.mult, ALU.add).then_inc(xn_ready, 1)
                for u in range(2):
                    dve.wait_ge(n2_ready, i * 2 + (u + 2))
                    dve.tensor_scalar(n2[u][:, :], norm[u][:, :], float(D), 1e-24, ALU.mult, ALU.max
                                      ).then_inc(n2_kept, 1)
                for u in range(2):
                    dve.wait_ge(inv_ready, i * 2 + (u + 2))
                    g_at = ds(i * (2 * G) + u * G, G)
                    dve.scalar_tensor_tensor(f.xs[:, g_at], f.xn[:, g_at], cols[:, 2:3], inv[u][:, :], ALU.mult,
                                             ALU.mult).then_inc(xs_ready, 1)

        @block.scalar
        def _(act):
            act.preload_act_table_set(LOG_EXP)
            act.wait_ge(mu_loaded, 16)
            act.activation(sq[1][:, 0:SLOTS], mu[:, :], ACT.Square).then_inc(sq2_ready, 1)
            act.wait_ge(const_ready, 1)

            def inverse_norm(u, cols, step):
                act.wait_ge(n2_kept, step)
                act.activation(log[u][:, 0:cols], n2[u][:, 0:cols], ACT.Ln, scale=2.0 ** UNIT_SHIFT
                               ).then_inc(log2_ready, 1)
                act.wait_ge(log2_ready, step)
                act.activation(inv[u][:, 0:cols], log[u][:, 0:cols], ACT.Exp, scale=-0.5, bias=unit_bias[:, :]
                               ).then_inc(inv_ready, 1)
            inverse_norm(1, SLOTS, 1)
            act.wait_ge(xs_ready, 1)
            with act.Fori(0, NG // 2) as i:
                for u in range(2):
                    act.wait_ge(centred, i * 2 + (u + 1))
                    act.activation(sq[u][:, :], xc[u][:, :], ACT.Square).then_inc(squared, 1)
                for u in range(2):
                    act.wait_ge(var_ready, i * 2 + (u + 1))
                    act.activation(log[u][:, :], var[u][:, :], ACT.Ln, bias=k.ln_eps[:, :]).then_inc(log_ready, 1)
                    act.wait_ge(log_ready, i * 2 + (u + 1))
                    act.activation(inv[u][:, :], log[u][:, :], ACT.Exp, scale=-0.5).then_inc(rstd_ready, 1)
                for u in range(2):
                    act.wait_ge(xn_ready, i * 2 + (u + 1))
                    act.activation(sq[u][:, :], f.xn[:, ds(i * (2 * G) + u * G, G)], ACT.Square
                                   ).then_inc(sq2_ready, 1)
                for u in range(2):
                    inverse_norm(u, G, i * 2 + (u + 2))
    return f


def soft_mixture(k):
    nc = k.nc
    with Stage(k, "moe") as s:
        slot_in = s.sb("slot_in", [P, B, SLOTS])
        combine = s.sb("combine", [P, 2, N])
        w1, w2 = s.sb("w1", [P, ME, MH]), s.sb("w2", [P, MG, D])
        b1, b2 = s.sb("b1", [P, MG]), s.sb("b2", [P, 2, D])
        own = s.sb("own_expert", [P, 4])
        (w_loaded,) = s.sems("w_loaded")
        with Stage(k, "route") as r:
            f = mixture_inputs(k, r)
            xs, xn = ([r.sb(f"{n}{u}", [P, TT]) for u in range(2)] for n in ("xs", "xn"))
            xr = r.sb("x_rows", [P, D])
            e1, p1 = r.sb("e1", [P, SLOTS]), r.sb("p1", [P, SLOTS])
            sh2, e2, p2, p2T = (r.sb(n, [P, 2 * TT]) for n in ("sh2", "e2", "p2", "p2T"))
            ntop1, sum1, inv1 = (r.sb(n, [P, 1]) for n in ("ntop1", "sum1", "inv1"))
            top2, sum2, inv2 = (r.sb(n, [P, 4]) for n in ("top2", "sum2", "inv2"))
            (staged, routed, xr_ready, ntop1_ready, e1_ready, inv1_ready, p1_ready, top2_ready, sh2_ready, e2_ready,
             sum2_ready, inv2_ready, p2_ready, p_turned, combine_ready, p2T_ready, slots_ready, slots_kept) = r.sems(
                "staged", "routed", "xr_ready", "ntop1_ready", "e1_ready", "inv1_ready", "p1_ready", "top2_ready",
                "sh2_ready", "e2_ready", "sum2_ready", "inv2_ready", "p2_ready", "p_turned", "combine_ready", "p2T_ready",
                "slots_ready", "slots_kept")
            block = r.block()
            row_bank, l1_bank, l2_bank = k.bank[0][:, 0:D], k.bank[1][:, 0:SLOTS], k.bank[2][:, 0:2 * TT]
            c_bank, d_bank = k.bank[3][:, 0:2 * TT], k.bank[4][:, 0:SLOTS]

            @block.sync
            def _(sync):
                a = k.a
                with nc.allow_non_contiguous_dma(reason="128-byte rows"):
                    sync.dma_start(w1[:, :, :], a["L0_ffn_w1"].rearrange("e d h -> d e h")).then_inc(w_loaded, 16)
                    sync.dma_start(b1[:, :], a["L0_ffn_b1"].rearrange("(g e) h -> (e h) g", e=4)
                                   ).then_inc(w_loaded, 16)
                for g in range(MG):
                    sync.dma_start(w2[:, g, :], a["L0_ffn_w2"][4 * g:4 * g + 4, :, :].rearrange("e h d -> (e h) d")
                                   ).then_inc(w_loaded, 16)
                for e in range(ME):
                    sync.dma_start(b2[MS * (e % 8):MS * (e % 8 + 1), e // 8, :],
                                   a["L0_ffn_b2"][e, :].partition_broadcast(MS)).then_inc(w_loaded, 16)

            def pe_route(pe, t, u):
                pe.wait_ge(staged, t + 1)
                if not isinstance(t, int) or t > 0:
                    pe.wait_ge(xr_ready, t)
                    pe.wait_ge(e1_ready, t)
                    pe.wait_ge(sh2_ready, t)
                nc.tensor.transpose(row_bank, xn[u][:, :], k.eye[:, :])
                nc.tensor.matmul(l1_bank, xs[u][:, :], f.mu[:, :], start=True, stop=True)
                for h in range(2):
                    last = nc.tensor.matmul(l2_bank[:, h * TT:(h + 1) * TT], f.mu[:, h * P:(h + 1) * P], xs[u][:, :],
                                            start=True, stop=True)
                last.then_inc(routed, 1)

            def pe_dispatch(pe, t):
                pe.wait_ge(p1_ready, t + 1)
                pe.wait_ge(p2_ready, t + 1)
                for h in range(2):
                    nc.tensor.transpose(c_bank[:, h * TT:(h + 1) * TT], p1[:, h * P:(h + 1) * P], k.eye[:, :])
                for h in range(2):
                    last = nc.tensor.transpose(d_bank[:, h * P:(h + 1) * P], p2[:, h * TT:(h + 1) * TT], k.eye[:, :])
                last.then_inc(p_turned, 1)

            def pe_slots(pe, t):
                pe.wait_ge(p2T_ready, t + 1)
                for b in range(2):
                    rows = slice(b * T, (b + 1) * T)
                    last = nc.tensor.matmul(k.bank[5 + b][:, 0:SLOTS], xr[rows, :], p2T[rows, :], start=True, stop=True)
                last.then_inc(slots_ready, 1)

            def dve_stage(dve, t, u):
                dve.tensor_copy(xn[u][:, :], f.xn[:, ds(t * TT, TT)])
                dve.tensor_copy(xs[u][:, :], f.xs[:, ds(t * TT, TT)]).then_inc(staged, 1)

            def dve_shift(dve, t):
                dve.wait_ge(routed, t + 1)
                dve.tensor_reduce(ntop1[:, :], l1_bank, AX_X, ALU.max, negate=True).then_inc(ntop1_ready, 1)
                l2 = l2_bank.rearrange("p (h t) -> p h t", t=T)
                dve.tensor_reduce(top2[:, :], l2, AX_X, ALU.max).then_inc(top2_ready, 1)
                dve.wait_ge(top2_ready, t + 1)
                dve.tensor_tensor(sh2[:, :].rearrange("p (h t) -> p h t", t=T), l2,
                                  top2[:, :].unsqueeze(2).to_broadcast([P, 4, T]), ALU.subtract).then_inc(sh2_ready, 1)

            def dve_scale(dve, t):
                dve.wait_ge(e1_ready, t + 1)
                dve.reciprocal(inv1[:, :], sum1[:, :]).then_inc(inv1_ready, 1)
                dve.wait_ge(inv1_ready, t + 1)
                dve.tensor_scalar(p1[:, :], e1[:, :], inv1[:, :], None, ALU.mult).then_inc(p1_ready, 1)
                dve.wait_ge(e2_ready, t + 1)
                dve.tensor_reduce(sum2[:, :], e2[:, :].rearrange("p (h t) -> p h t", t=T), AX_X, ALU.add
                                  ).then_inc(sum2_ready, 1)
                dve.wait_ge(sum2_ready, t + 1)
                dve.reciprocal(inv2[:, :], sum2[:, :]).then_inc(inv2_ready, 1)
                dve.wait_ge(inv2_ready, t + 1)
                dve.tensor_tensor(p2[:, :].rearrange("p (h t) -> p h t", t=T),
                                  e2[:, :].rearrange("p (h t) -> p h t", t=T),
                                  inv2[:, :].unsqueeze(2).to_broadcast([P, 4, T]), ALU.mult).then_inc(p2_ready, 1)

            def dve_keep(dve, t):
                dve.wait_ge(slots_ready, t + 1)
                dve.tensor_copy(slot_in[:, ds(t * 2, 2), :], k.psum[:, 5:7, 0:SLOTS]).then_inc(slots_kept, 1)

            def tiles(eng, body):
                with eng.Fori(0, NT // 2 - 1) as i:
                    for u in range(2):
                        body(i * 2 + u, u, True)
                body(NT - 2, 0, True)
                body(NT - 1, 1, False)

            @block.tensor
            def _(pe):
                pe_route(pe, 0, 0)

                def body(t, u, more):
                    pe_dispatch(pe, t)
                    if more:
                        pe_route(pe, t + 1, 1 - u)
                    pe_slots(pe, t)
                tiles(pe, body)

            @block.vector
            def _(dve):
                dve_stage(dve, 0, 0)
                dve_shift(dve, 0)

                def body(t, u, more):
                    dve_scale(dve, t)
                    if more:
                        dve_stage(dve, t + 1, 1 - u)
                        dve_shift(dve, t + 1)
                    dve_keep(dve, t)
                tiles(dve, body)

            @block.scalar
            def _(act):
                def front(t):
                    act.wait_ge(routed, t + 1)
                    if not isinstance(t, int) or t > 0:
                        act.wait_ge(slots_ready, t)
                    act.activation(xr[:, :], row_bank, ACT.Copy).then_inc(xr_ready, 1)
                    act.wait_ge(ntop1_ready, t + 1)
                    act.activation(e1[:, :], l1_bank, ACT.Exp, bias=ntop1[:, :], accum_out=sum1[:, :]
                                   ).then_inc(e1_ready, 1)
                    act.wait_ge(sh2_ready, t + 1)
                    act.activation(e2[:, :], sh2[:, :], ACT.Exp).then_inc(e2_ready, 1)
                front(0)

                def body(t, u, more):
                    act.wait_ge(p_turned, t + 1)
                    act.activation(p2T[:, :], d_bank, ACT.Copy).then_inc(p2T_ready, 1)
                    act.activation(combine[:, :, ds(t * TT, TT)], c_bank.rearrange("p (h t) -> p h t", h=2), ACT.Copy
                                   ).then_inc(combine_ready, 1)
                    if more:
                        front(t + 1)
                tiles(act, body)

        UB = 4
        NU = B // UB
        hid = [s.sb(f"hid{u}", [P, MG, UB, 4, MS]) for u in range(2)]
        slot_out = [s.sb(f"slot_out{u}", [P, UB, 2, D]) for u in range(2)]
        own_ready, h_ready, gelu_ready, masked, o_ready, o_kept, out_ready, added = s.sems(
            "own_ready", "h_ready", "gelu_ready", "masked", "o_ready", "o_kept", "out_ready", "added")
        block = s.block()

        @block.gpsimd
        def _(pool):
            pool.memset(own[:, :], 0.0).then_inc(own_ready, 1)
            pool.wait_ge(own_ready, 1)
            for e in range(4):
                last = pool.memset(own[MH * e:MH * (e + 1), e:e + 1], 1.0)
            last.then_inc(own_ready, 1)

        @block.tensor
        def _(pe):
            pe.wait_ge(w_loaded, 16 * (2 + MG + ME))
            with pe.Fori(0, NU // 2) as i:
                for u in range(2):
                    for g in range(MG):
                        last = nc.tensor.matmul(k.psum[:, 4 * u + g // 2, (g % 2) * 256:(g % 2) * 256 + 256],
                                                w1[:, 4 * g:4 * g + 4, :].rearrange("p e h -> p (e h)"),
                                                slot_in[:, ds(i * (2 * UB) + u * UB, UB), g * 64:(g + 1) * 64],
                                                start=True, stop=True)
                    last.then_inc(h_ready, 1)
                for u in range(2):
                    pe.wait_ge(masked, i * 2 + (u + 1))
                    for b in range(UB):
                        for g in range(MG):
                            last = nc.tensor.matmul(
                                k.psum[(g % 2) * 64:(g % 2) * 64 + 64, 4 * u + 2 + b // 2,
                                       (b % 2) * 256 + (g // 2) * D:(b % 2) * 256 + (g // 2) * D + D],
                                hid[u][:, g, b, :, :].rearrange("p e s -> p (e s)"), w2[:, g, :], start=True, stop=True)
                    last.then_inc(o_ready, 1)
                for u in range(2):
                    pe.wait_ge(o_kept, i * 2 + (u + 1))
                    for b in range(UB):
                        for h in range(2):
                            last = nc.tensor.matmul(k.bank[4 * u][:, b * T:(b + 1) * T], slot_out[u][:, b, h, :],
                                                    combine[:, h, ds(i * (2 * UB * T) + (u * UB + b) * T, T)],
                                                    start=(h == 0), stop=(h == 1))
                    last.then_inc(out_ready, 1)
                pe.wait_ge(added, i * 2 + 2)

        @block.scalar
        def _(act):
            act.preload_act_table(ACT.Gelu)
            act.wait_ge(w_loaded, 16 * (2 + MG + ME))
            with act.Fori(0, NU // 2) as i:
                for u in range(2):
                    act.wait_ge(h_ready, i * 2 + (u + 1))
                    for g in range(MG):
                        last = act.activation(hid[u][:, g, :, :, :].rearrange("p b e s -> p (b e s)"),
                                              k.psum[:, 4 * u + g // 2, (g % 2) * 256:(g % 2) * 256 + 256], ACT.Gelu,
                                              bias=b1[:, g:g + 1])
                    last.then_inc(gelu_ready, 1)

        @block.vector
        def _(dve):
            dve.wait_ge(own_ready, 2)
            dve.wait_ge(w_loaded, 16 * (2 + MG + ME))
            with dve.Fori(0, NU // 2) as i:
                for u in range(2):
                    dve.wait_ge(gelu_ready, i * 2 + (u + 1))
                    h = hid[u][:, :, :, :, :].rearrange("p g b e s -> p (g b) e s")
                    dve.tensor_tensor(h, h, own[:, :].unsqueeze(1).unsqueeze(3).to_broadcast([P, MG * UB, 4, MS]),
                                      ALU.mult).then_inc(masked, 1)
                for u in range(2):
                    dve.wait_ge(o_ready, i * 2 + (u + 1))
                    dve.tensor_tensor(slot_out[u][:, :, :, :].rearrange("p b h d -> p b (h d)"),
                                      k.psum[:, 4 * u + 2:4 * u + 4, :].rearrange("p n (b c) -> p (n b) c", b=2),
                                      b2[:, :, :].rearrange("p h d -> p (h d)").unsqueeze(1).to_broadcast([P, UB, 2 * D]),
                                      ALU.add).then_inc(o_kept, 1)
                for u in range(2):
                    dve.wait_ge(out_ready, i * 2 + (u + 1))
                    x = k.X[:, ds(i * (2 * UB * T) + u * UB * T, UB * T)]
                    dve.tensor_tensor(x, x, k.bank[4 * u][:, 0:UB * T], ALU.add).then_inc(added, 1)


DH, DK = 8, 64
DP = DH * DK // P
HB = 2 * DP
LEVELS = 6
DECAY, THRESHOLD = 0.9, 0.5
NORM_FLOOR = 2.0 ** -62


def delta_inputs(k, s, hT, uT):
    nc = k.nc
    a = k.a
    with Stage(k, "din") as t:
        cols = t.sb("cols", [P, 6])
        bau, w_au = t.sb("bau", [DK, 1]), t.sb("w_au", [P, DK])
        rms_eps = t.sb("rms_eps", [P, 1])
        sq, log, rstd, conv = ([t.sb(f"{n}{u}", [P, G]) for u in range(2)] for n in ("sq", "log", "rstd", "conv"))
        xn = t.sb("xn", [P, N])
        loaded, eps_ready, squared, mean_ready, log_ready, rstd_ready, normed = t.sems(
            "loaded", "eps_ready", "squared", "mean_ready", "log_ready", "rstd_ready", "normed")
        with Stage(k, "rms") as r:
            block = r.block()

            @block.sync
            def _(sync):
                with nc.allow_non_contiguous_dma(reason="columns"):
                    sync.dma_start(cols[:, 0:1], column(a["L1_attn_norm_in_w"])).then_inc(loaded, 16)
                    sync.dma_start(cols[:, 1:2], column(a["L1_attn_conv_b"])).then_inc(loaded, 16)
                    sync.dma_start(cols[:, 2:6], a["L1_attn_conv_w"].rearrange("d o j -> d (o j)")).then_inc(loaded, 16)
                    sync.dma_start(bau[:, :], column(a["L1_attn_bau"])).then_inc(loaded, 16)
                sync.dma_start(w_au[:, :], a["L1_attn_Wau"]).then_inc(loaded, 16)

            @block.scalar
            def _(act):
                act.preload_act_table_set(LOG_EXP)
                act.wait_ge(eps_ready, 1)
                with act.Fori(0, NG // 2) as i:
                    for u in range(2):
                        act.activation(sq[u][:, :], k.X[:, ds(i * (2 * G) + u * G, G)], ACT.Square).then_inc(squared, 1)
                    for u in range(2):
                        act.wait_ge(mean_ready, i * 2 + (u + 1))
                        act.activation(log[u][:, :], k.bank[u][:, :], ACT.Ln, bias=rms_eps[:, :]).then_inc(log_ready, 1)
                        act.wait_ge(log_ready, i * 2 + (u + 1))
                        act.activation(rstd[u][:, :], log[u][:, :], ACT.Exp, scale=-0.5).then_inc(rstd_ready, 1)
                    act.wait_ge(normed, i * 2 + 2)

            @block.tensor
            def _(pe):
                with pe.Fori(0, NG // 2) as i:
                    for u in range(2):
                        pe.wait_ge(squared, i * 2 + (u + 1))
                        nc.tensor.matmul(k.bank[u][:, :], k.ones_mean[:, :], sq[u][:, :], start=True, stop=True
                                         ).then_inc(mean_ready, 1)

            @block.vector
            def _(dve):
                dve.memset(rms_eps[:, :], RMS_EPS).then_inc(eps_ready, 1)
                dve.wait_ge(loaded, 80)
                with dve.Fori(0, NG // 2) as i:
                    for u in range(2):
                        dve.wait_ge(rstd_ready, i * 2 + (u + 1))
                        g_at = ds(i * (2 * G) + u * G, G)
                        dve.scalar_tensor_tensor(xn[:, g_at], k.X[:, g_at], cols[:, 0:1], rstd[u][:, :], ALU.mult,
                                                 ALU.mult).then_inc(normed, 1)
        with Stage(k, "conv") as r:
            taps, h_ready, u_ready, u_kept = r.sems("taps", "h_ready", "u_ready", "u_kept")
            block = r.block()

            @block.vector
            def _(dve):
                with dve.Fori(0, NG // 2) as i:
                    for u in range(2):
                        x = xn[:, ds(i * (2 * G) + u * G, G)].rearrange("p (b t) -> p b t", t=T)
                        c = conv[u][:, :].rearrange("p (b t) -> p b t", t=T)
                        dve.tensor_scalar(c, x, cols[:, 5:6], cols[:, 1:2], ALU.mult, ALU.add).then_inc(taps, 1)
                        for j in (1, 2, 3):
                            dve.wait_ge(taps, i * 8 + (4 * u + j))
                            dve.scalar_tensor_tensor(c[:, :, j:T], x[:, :, 0:T - j], cols[:, 5 - j:6 - j], c[:, :, j:T],
                                                     ALU.mult, ALU.add).then_inc(taps, 1)
                    dve.wait_ge(h_ready, i * 2 + 2)

            @block.scalar
            def _(act):
                act.preload_act_table(ACT.Silu)
                with act.Fori(0, NG // 2) as i:
                    for u in range(2):
                        act.wait_ge(taps, i * 8 + 4 * (u + 1))
                        act.activation(hT[:, ds(i * (2 * G) + u * G, G)], conv[u][:, :], ACT.Silu).then_inc(h_ready, 1)
                    for u in range(2):
                        act.wait_ge(u_ready, i * 2 + (u + 1))
                        act.activation(uT[:, ds(i * (2 * G) + u * G, G)], k.bank[u][0:DK, :], ACT.Silu, bias=bau[:, :]
                                       ).then_inc(u_kept, 1)

            @block.tensor
            def _(pe):
                with pe.Fori(0, NG // 2) as i:
                    for u in range(2):
                        pe.wait_ge(h_ready, i * 2 + (u + 1))
                        nc.tensor.matmul(k.bank[u][0:DK, :], w_au[:, :], hT[:, ds(i * (2 * G) + u * G, G)],
                                         start=True, stop=True).then_inc(u_ready, 1)


def delta_spikes(k, s, hT, spikes):
    nc = k.nc
    with Stage(k, "spk") as t:
        drive = t.sb("drive", [P, DP, N])
        w = t.sb("w", [P, DP * P])
        charge, left = t.sb("charge", [P, DP * B]), t.sb("left", [P, DP * B])
        loaded, driven, kept, cleared, charged, fired, spent = t.sems(
            "loaded", "driven", "kept", "cleared", "charged", "fired", "spent")
        block = t.block()

        @block.sync
        def _(sync):
            sync.dma_start(w[:, :], k.a["L1_attn_Wspike"]).then_inc(loaded, 16)

        @block.tensor
        def _(pe):
            pe.wait_ge(loaded, 16)
            with pe.Fori(0, NG // 2) as i:
                for u in range(2):
                    for hp in range(DP):
                        last = nc.tensor.matmul(k.bank[4 * u + hp][:, :], w[:, hp * P:(hp + 1) * P],
                                                hT[:, ds(i * (2 * G) + u * G, G)], start=True, stop=True)
                    last.then_inc(driven, 1)
                pe.wait_ge(kept, i * 2 + 2)

        @block.scalar
        def _(act):
            with act.Fori(0, NG // 2) as i:
                for u in range(2):
                    act.wait_ge(driven, i * 2 + (u + 1))
                    act.activation(drive[:, :, ds(i * (2 * G) + u * G, G)], k.psum[:, 4 * u:4 * u + 4, :], ACT.Copy
                                   ).then_inc(kept, 1)

        @block.vector
        def _(dve):
            dve.memset(left[:, :], 0.0).then_inc(spent, 1)
            dve.wait_ge(kept, NG)
            with dve.Fori(0, T) as pos:
                at = lambda ap: ap[:, :, :].rearrange("p h (b t) -> p (h b) t", t=T)[:, :, ds(pos, 1)].rearrange(
                    "p n o -> p (n o)")
                dve.wait_ge(spent, pos + 1)
                dve.scalar_tensor_tensor(charge[:, :], left[:, :], DECAY, at(drive), ALU.mult, ALU.add
                                         ).then_inc(charged, 1)
                dve.wait_ge(charged, pos + 1)
                dve.tensor_scalar(at(spikes), charge[:, :], THRESHOLD, None, ALU.is_gt).then_inc(fired, 1)
                dve.wait_ge(fired, pos + 1)
                dve.scalar_tensor_tensor(left[:, :], at(spikes), -THRESHOLD, charge[:, :], ALU.mult, ALU.add
                                         ).then_inc(spent, 1)


def delta_weights(k, s):
    nc = k.nc
    a = k.a
    w = Core()
    w.q, w.k, w.v = (s.sb(n, [P, DP * P]) for n in ("wq", "wk", "wv"))
    w.alpha = s.sb("w_alpha", [DK, DP * P])
    w.beta = s.sb("w_beta", [P, DP, P])
    w.o = s.sb("wo", [P, DP, D])
    w.alpha_spike = s.sb("alpha_spike", [P, 3, DP, P], BF16)
    w.beta_spike = s.sb("beta_spike", [P, 3, DP, P], BF16)
    w.head_ones = s.sb("head_ones_bf16", [P, P], BF16)
    w.bias = s.sb("bias", [P, 2, DP])
    w.levels = s.sb("level_masks", [P, LEVELS, T // 2])
    w.eye2 = s.sb("eye2", [P, T])
    w.head_sum, w.head_mean = s.sb("head_sum", [P, P]), s.sb("head_mean", [P, P])
    with Stage(k, "dw") as t:
        raw_beta, cols = t.sb("raw_beta", [P, DH]), t.sb("cols", [P, 3, DP])
        wide = t.sb("wide", [P, 2, DP, P])
        left = t.sb("left", [P, 2, DP, P])
        loaded, step = t.sems("loaded", "dve_step")
        block = t.block()

        @block.sync
        def _(sync):
            loads = [(w.q[:, :], a["L1_attn_Wq"]), (w.k[:, :], a["L1_attn_Wk"]), (w.v[:, :], a["L1_attn_Wv"]),
                     (w.alpha[:, :], a["L1_attn_Wad"]), (raw_beta[:, :], a["L1_attn_Wbeta"]),
                     (w.o[:, :, :], a["L1_attn_Wo"].rearrange("(n p) o -> p n o", p=P)),
                     (w.levels[:, :, :], a["level_masks"]), (w.eye2[:, :], a["eye2"]), (w.head_sum[:, :], a["head_sum"])]
            for dst, src in loads:
                sync.dma_start(dst, src).then_inc(loaded, 16)
            with nc.allow_non_contiguous_dma(reason="columns"):
                for c, name in enumerate(("alpha_spike", "beta_spike")):
                    sync.dma_start(cols[:, c, :], a[f"L1_attn_{name}"].rearrange("o (n j) d -> (o j d) n", j=2)
                                   ).then_inc(loaded, 16)
                sync.dma_start(cols[:, 2, :], a["L1_attn_head_norm_w"].rearrange("(n j) d -> (j d) n", j=2)
                               ).then_inc(loaded, 16)
                sync.dma_start(w.bias[:, 0, :], a["L1_attn_bad"].rearrange("(n p) -> p n", p=P)).then_inc(loaded, 16)
                for j in range(2):
                    sync.dma_start(w.bias[j * DK:(j + 1) * DK, 1, :],
                                   a["L1_attn_bbeta"].rearrange("(n j) -> j n", j=2)[j, :].partition_broadcast(DK)
                                   ).then_inc(loaded, 16)

        @block.vector
        def _(dve):
            dve.wait_ge(loaded, 16 * 15)
            dve.tensor_copy(w.head_ones[:, :], w.head_sum[:, :])
            dve.tensor_scalar(w.head_mean[:, :], w.head_sum[:, :], 1.0 / DK, None, ALU.mult)
            dve.tensor_copy(w.beta[:, :, :].rearrange("p n (j c) -> p (n j) c", j=2),
                            raw_beta[:, :].unsqueeze(2).to_broadcast([P, DH, DK]))
            over = lambda ap: ap.unsqueeze(2).to_broadcast([P, DP, P])
            dve.tensor_tensor(w.o[:, :, :], w.o[:, :, :], over(cols[:, 2, :]), ALU.mult)
            for c, base in enumerate((k.eye, w.head_sum)):
                last = dve.tensor_tensor(wide[:, c, :, :], base[:, :].unsqueeze(1).to_broadcast([P, DP, P]),
                                         over(cols[:, c, :]), ALU.mult)
            last.then_inc(step, 1)
            n = 1
            for c, dst in enumerate((w.alpha_spike, w.beta_spike)):
                src = wide[:, c, :, :]
                for part in range(3):
                    dve.wait_ge(step, n)
                    dve.tensor_copy(dst[:, part, :, :], src).then_inc(step, 1)
                    n += 1
                    if part < 2:
                        dve.wait_ge(step, n)
                        dve.tensor_tensor(left[:, part, :, :], src, dst[:, part, :, :], ALU.subtract).then_inc(step, 1)
                        n += 1
                        src = left[:, part, :, :]
    return w


def delta_rule(k, s, hT, uT, spikes, yT):
    nc = k.nc
    w = delta_weights(k, s)
    two = lambda name, shape, dt=F32: [s.sb(f"{name}{u}", shape, dt) for u in range(2)]
    h_t = two("h", [P, TT])
    raw, kq, kS = two("raw", [P, HB, 2, T]), two("kq", [P, HB, 2, T]), two("kS", [P, HB, T])
    inv = two("inv", [P, 2, 512])
    alpha, beta, v = two("alpha", [P, HB, T]), two("beta", [P, HB, T]), two("v", [P, 2, DP, DK])
    blocks = [[alpha[u]] + [s.sb(f"decay{2 ** l}_{u}", [P, HB, T >> l]) for l in range(1, LEVELS - 1)] for u in range(2)]
    CT = [[s.sb(f"CT{l}_{u}", [P, HB, T]) for l in range(LEVELS)] for u in range(2)]
    PT = two("PT", [P, HB, T])
    r_rt, z_u = two("R_RT", [P, 2, HB * T]), two("Z_U", [P, 2, HB * T])
    sq, log = r_rt, z_u
    (R, RT), (Z, U) = ([[m[u][:, c, :].rearrange("p (n t) -> p n t", t=T) for u in range(2)] for c in range(2)]
                       for m in (r_rt, z_u))
    ysq, yn = ([kq[u][:, :, :, :].rearrange("p (c n) w t -> p c (n w t)", c=2)[:, c, :] for u in range(2)]
               for c in range(2))
    ylog, yinv = ([inv[u][:, c, :] for u in range(2)] for c in range(2))
    floor, small, rms_eps = s.sb("floor", [P, 1]), s.sb("small", [P, 1]), s.sb("rms_eps2", [P, 1])
    (h_staged, logits, raw_ready, sq_ready, sig_ready, counted, v_ready, gates_ready, v_kept, n2_ready, ln1, ex1, ln2,
     inv_ready, normed, kS_ready, kq_ready, diag_ready, y_ready, ysq_ready, yms_ready, ylog_ready, yinv_ready, yn_ready,
     out_ready, out_kept, cleared) = s.sems(
        "h_staged", "logits_ready", "raw_ready", "sq_ready", "sig_ready", "counted", "v_ready", "gates_ready", "v_kept",
        "n2_ready", "ln1", "ex1", "ln2", "inv_ready", "normed", "kS_ready", "kq_ready", "diag_ready", "y_ready",
        "ysq_ready", "yms_ready", "ylog_ready", "yinv_ready", "yn_ready", "out_ready", "out_kept", "cleared")
    level_ready, level_kept, scaled, kS_scaled, decays_ready, z_ready, z_kept, r_ready, r_kept = (
        s.sems(*[f"{name}{l}" for l in range(LEVELS)]) for name in (
            "level_ready", "level_kept", "scaled", "kS_scaled", "decays_ready", "z_ready", "z_kept", "r_ready", "r_kept"))
    block = s.block()
    BOTH = range(2)

    def bank(u, n):
        return k.bank[4 * u + n]

    def hb(ap):
        return ap.rearrange("p (n t) -> p n t", t=T)

    def product(out, lhsT, rhs):
        for n in range(HB):
            for j in range(2):
                r = slice(j * DK, (j + 1) * DK)
                last = nc.tensor.matmul(out[r, n * T:(n + 1) * T], lhsT[r, n, :], rhs(r, n), start=True, stop=True)
        return last

    def right(ap, l):
        return ap.rearrange("p n w (c two l) -> p n w c two l", two=2, l=1 << l)[:, :, :, :, 1, :]

    def upto(i, u):
        return i * 2 + (u + 1)

    @block.tensor
    def _(pe):
        pe.wait_ge(cleared, 1)
        with pe.Fori(0, NT // 2) as i:
            for u in BOTH:
                tile = ds(i * (2 * TT) + u * TT, TT)
                pe.wait_ge(h_staged, upto(i, u))
                for hp in range(DP):
                    c, hc = slice(hp * TT, (hp + 1) * TT), slice(hp * P, (hp + 1) * P)
                    nc.tensor.matmul(bank(u, 0)[:, c], w.k[:, hc], h_t[u][:, :], start=True, stop=True)
                    nc.tensor.matmul(bank(u, 1)[:, c], w.q[:, hc], h_t[u][:, :], start=True, stop=True)
                    nc.tensor.matmul(bank(u, 2)[:, c], w.alpha[:, hc], uT[:, tile], start=True, stop=False)
                    for part in range(3):
                        nc.tensor.matmul(bank(u, 2)[:, c], w.alpha_spike[:, part, hp, :],
                                         spikes[:, hp, tile], start=False, stop=(part == 2))
                    nc.tensor.matmul(bank(u, 3)[:, c], w.beta[:, hp, :], h_t[u][:, :], start=True, stop=False)
                    for part in range(3):
                        last = nc.tensor.matmul(bank(u, 3)[:, c], w.beta_spike[:, part, hp, :],
                                                spikes[:, hp, tile], start=False, stop=(part == 2))
                last.then_inc(logits, 1)
            for u in BOTH:
                tile = ds(i * (2 * TT) + u * TT, TT)
                pe.wait_ge(raw_ready, upto(i, u))
                pe.wait_ge(sq_ready, upto(i, u))
                for hp in range(DP):
                    last = nc.tensor.matmul(bank(u, 0)[:, hp * TT:(hp + 1) * TT], w.head_ones[:, :],
                                            spikes[:, hp, tile], start=True, stop=True)
                last.then_inc(counted, 1)
                pe.wait_ge(sig_ready, upto(i, u))
                for c in range(2):
                    last = nc.tensor.matmul(bank(u, 2 + c)[:, :], w.head_sum[:, :], sq[u][:, c, :], start=True, stop=True)
                last.then_inc(n2_ready, 1)
                wv = w.v[:, :].rearrange("p (n j v) -> p j n v", j=2, v=DK)
                for b in range(2):
                    for j in range(2):
                        last = nc.tensor.matmul(
                            bank(u, 1)[j * DK:(j + 1) * DK, b * 256:(b + 1) * 256].rearrange("p (n v) -> p n v", v=DK),
                            h_t[u][:, b * T:(b + 1) * T], wv[:, j, :, :], start=True, stop=True)
                last.then_inc(v_ready, 1)
            for u in BOTH:
                k.hold(pe)
                pe.wait_ge(gates_ready, upto(i, u))
                pe.wait_ge(inv_ready, upto(i, u))
                pe.wait_ge(v_kept, upto(i, u))
                pe.wait_ge(kS_ready, upto(i, u))
                product(bank(u, 2), kS[u], lambda r, n: raw[u][r, n, 1, :]).then_inc(diag_ready, 1)

            def level(l):
                for u in BOTH:
                    if l == 0:
                        k.hold(pe)
                        pe.wait_ge(kq_ready, upto(i, u))
                    else:
                        k.hold(pe)
                        pe.wait_ge(scaled[l - 1], upto(i, u))
                        pe.wait_ge(kS_scaled[l - 1], upto(i, u))
                    product(bank(u, l % 2), kS[u], lambda r, n: right(kq[u][r, :, :, :], l)[:, n, :, :, :]
                            ).then_inc(level_ready[l], 1)
            level(0)
            for l in range(LEVELS - 1):
                level(l + 1)
                if l == 0:
                    for u in BOTH:
                        k.hold(pe)
                        pe.wait_ge(level_kept[0], upto(i, u))
                        product(bank(u, 3), CT[u][0], lambda r, n: w.eye2[r, :]).then_inc(r_ready[0], 1)
                    continue
                for u in BOTH:
                    k.hold(pe)
                    pe.wait_ge(level_kept[l], upto(i, u))
                    pe.wait_ge(r_kept[l - 1], upto(i, u))
                    product(bank(u, 2), CT[u][l], lambda r, n: R[u][r, n, :]).then_inc(z_ready[l - 1], 1)
                for u in BOTH:
                    k.hold(pe)
                    pe.wait_ge(z_kept[l - 1], upto(i, u))
                    if l < LEVELS - 2:
                        product(bank(u, 3), RT[u], lambda r, n: Z[u][r, n, :])
                    product(bank(u, 2), Z[u], lambda r, n: RT[u][r, n, :]).then_inc(r_ready[l], 1)
            for u in BOTH:
                k.hold(pe)
                pe.wait_ge(r_kept[LEVELS - 2], upto(i, u))
                product(bank(u, 2), RT[u], lambda r, n: v[u][r, n % 2, n // 2, :]).then_inc(z_ready[LEVELS - 2], 1)
            for u in BOTH:
                k.hold(pe)
                pe.wait_ge(level_kept[LEVELS - 1], upto(i, u))
                pe.wait_ge(z_kept[LEVELS - 2], upto(i, u))
                product(bank(u, 3), CT[u][LEVELS - 1], lambda r, n: U[u][r, n, :]).then_inc(z_ready[LEVELS - 1], 1)
            for u in BOTH:
                k.hold(pe)
                pe.wait_ge(z_kept[LEVELS - 1], upto(i, u))
                product(bank(u, 2), RT[u], lambda r, n: Z[u][r, n, :]).then_inc(r_ready[LEVELS - 1], 1)
            for u in BOTH:
                k.hold(pe)
                pe.wait_ge(r_kept[LEVELS - 1], upto(i, u))
                product(bank(u, 0), U[u], lambda r, n: PT[u][r, n, :]).then_inc(y_ready, 1)
            for u in BOTH:
                pe.wait_ge(ysq_ready, upto(i, u))
                nc.tensor.matmul(bank(u, 1)[:, :], w.head_mean[:, :], ysq[u][:, :], start=True, stop=True
                                 ).then_inc(yms_ready, 1)
            for u in BOTH:
                pe.wait_ge(yn_ready, upto(i, u))
                for hp in range(DP):
                    last = nc.tensor.matmul(bank(u, 3)[:, 0:TT], w.o[:, hp, :], yn[u][:, hp * TT:(hp + 1) * TT],
                                            start=(hp == 0), stop=(hp == DP - 1))
                last.then_inc(out_ready, 1)
            pe.wait_ge(out_kept, i * 2 + 2)

    @block.scalar
    def _(act):
        act.wait_ge(cleared, 1)
        with act.Fori(0, NT // 2) as i:
            for u in BOTH:
                act.wait_ge(logits, upto(i, u))
                for g, dst in enumerate((alpha[u], beta[u])):
                    for hp in range(DP):
                        last = act.activation(dst[:, 2 * hp:2 * hp + 2, :].rearrange("p n t -> p (n t)"),
                                              bank(u, 2 + g)[:, hp * TT:(hp + 1) * TT], ACT.Sigmoid,
                                              bias=w.bias[:, g, hp:hp + 1])
                last.then_inc(sig_ready, 1)
                act.wait_ge(raw_ready, upto(i, u))
                act.activation(sq[u][:, :, :].rearrange("p w (n t) -> p w n t", t=T),
                               raw[u][:, :, :, :].rearrange("p n w t -> p w n t"), ACT.Square).then_inc(sq_ready, 1)
            act.preload_act_table_set(LOG_EXP)
            for u in BOTH:
                act.wait_ge(n2_ready, upto(i, u))
                act.activation(log[u][:, :, :], k.psum[:, 4 * u + 2:4 * u + 4, :], ACT.Ln, bias=floor[:, :]).then_inc(ln1, 1)
                act.wait_ge(ln1, upto(i, u))
                act.activation(inv[u][:, :, :], log[u][:, :, :], ACT.Exp, scale=0.5).then_inc(ex1, 1)
                act.wait_ge(ex1, upto(i, u))
                act.activation(log[u][:, :, :], inv[u][:, :, :], ACT.Ln, bias=small[:, :]).then_inc(ln2, 1)
                act.wait_ge(ln2, upto(i, u))
                act.activation(inv[u][:, :, :], log[u][:, :, :], ACT.Exp, scale=-1.0).then_inc(inv_ready, 1)
            for l in range(1, LEVELS - 1):
                for u in BOTH:
                    act.wait_ge(z_ready[l - 1], upto(i, u))
                    act.activation(Z[u][:, :, :].rearrange("p n t -> p (n t)"), bank(u, 2), ACT.Copy).then_inc(z_kept[l - 1], 1)
            for u in BOTH:
                act.wait_ge(z_ready[LEVELS - 2], upto(i, u))
                act.activation(U[u][:, :, :].rearrange("p n t -> p (n t)"), bank(u, 2), ACT.Copy).then_inc(z_kept[LEVELS - 2], 1)
            for u in BOTH:
                act.wait_ge(z_ready[LEVELS - 1], upto(i, u))
                act.activation(Z[u][:, :, :].rearrange("p n t -> p (n t)"), bank(u, 3), ACT.Copy).then_inc(z_kept[LEVELS - 1], 1)
            for u in BOTH:
                act.wait_ge(y_ready, upto(i, u))
                act.activation(ysq[u][:, :], bank(u, 0), ACT.Square).then_inc(ysq_ready, 1)
            for u in BOTH:
                act.wait_ge(yms_ready, upto(i, u))
                act.activation(ylog[u][:, :], bank(u, 1), ACT.Ln, bias=rms_eps[:, :]).then_inc(ylog_ready, 1)
                act.wait_ge(ylog_ready, upto(i, u))
                act.activation(yinv[u][:, :], ylog[u][:, :], ACT.Exp, scale=-0.5).then_inc(yinv_ready, 1)

    @block.gpsimd
    def _(pool):
        with pool.Fori(0, NT // 2) as i:
            for u in BOTH:
                pool.wait_ge(raw_ready, upto(i, u))
                pool.wait_ge(inv_ready, upto(i, u))
                pool.tensor_tensor(raw[u][:, :, :, :], raw[u][:, :, :, :],
                                   inv[u][:, :, :].rearrange("p w (n t) -> p n w t", t=T), ALU.mult).then_inc(normed, 1)
            for l in range(LEVELS - 1):
                for u in BOTH:
                    pool.wait_ge(level_ready[l], upto(i, u))
                    if l > 0:
                        pool.wait_ge(decays_ready[l - 1], upto(i, u))
                    L = 1 << l
                    ks = kS[u][:, :, :].rearrange("p n (c two l) -> p n c two l", two=2, l=L)[:, :, :, 0, :]
                    total = blocks[u][l][:, :, :].rearrange("p n (c two) -> p n c two", two=2)[:, :, :, 1]
                    pool.tensor_tensor(ks, ks, total.unsqueeze(3).to_broadcast([P, HB, T // (2 * L), L]), ALU.mult
                                       ).then_inc(kS_scaled[l], 1)

    @block.vector
    def _(dve):
        for u in BOTH:
            for l in range(LEVELS):
                dve.memset(CT[u][l][:, :, :], 0.0)
        dve.memset(floor[:, :], NORM_FLOOR)
        dve.memset(rms_eps[:, :], RMS_EPS)
        dve.memset(small[:, :], 1e-6).then_inc(cleared, 1)
        with dve.Fori(0, NT // 2) as i:
            for u in BOTH:
                dve.tensor_copy(h_t[u][:, :], hT[:, ds(i * (2 * TT) + u * TT, TT)]).then_inc(h_staged, 1)
            for u in BOTH:
                dve.wait_ge(logits, upto(i, u))
                for c in range(2):
                    last = dve.tensor_copy(raw[u][:, :, c, :], hb(bank(u, c)))
                last.then_inc(raw_ready, 1)
            for u in BOTH:
                dve.wait_ge(counted, upto(i, u))
                dve.wait_ge(sig_ready, upto(i, u))
                count = hb(bank(u, 0))
                dve.scalar_tensor_tensor(alpha[u][:, :, :], count, 0.5, alpha[u][:, :, :], ALU.is_lt, ALU.max)
                dve.scalar_tensor_tensor(beta[u][:, :, :], count, 1.0, beta[u][:, :, :], ALU.min, ALU.min
                                         ).then_inc(gates_ready, 1)
                dve.wait_ge(v_ready, upto(i, u))
                dve.tensor_copy(v[u][:, :, :, :].rearrange("p b n v -> p (b n v)"), bank(u, 1)).then_inc(v_kept, 1)
            for u in BOTH:
                dve.wait_ge(normed, upto(i, u))
                dve.wait_ge(gates_ready, upto(i, u))
                dve.tensor_tensor(kS[u][:, :, :], raw[u][:, :, 0, :], beta[u][:, :, :], ALU.mult).then_inc(kS_ready, 1)
                dve.tensor_tensor(kq[u][:, :, :, :], raw[u][:, :, :, :],
                                  alpha[u][:, :, :].unsqueeze(2).to_broadcast([P, HB, 2, T]), ALU.mult
                                  ).then_inc(kq_ready, 1)
            for u in BOTH:
                dve.wait_ge(diag_ready, upto(i, u))
                dve.tensor_tensor(PT[u][:, :, :], hb(bank(u, 2)), w.eye2[:, :].unsqueeze(1).to_broadcast([P, HB, T]),
                                  ALU.mult).then_inc(cleared, 1)

            def level(l):
                L = 1 << l
                for u in BOTH:
                    dve.wait_ge(level_ready[l], upto(i, u))
                    if l < LEVELS - 1:
                        pair = blocks[u][l][:, :, :].rearrange("p n (c two) -> p n c two", two=2)
                        if l > 0:
                            dve.wait_ge(decays_ready[l - 1], upto(i, u))
                            dve.wait_ge(scaled[l - 1], upto(i, u))
                        if l < LEVELS - 2:
                            dve.tensor_tensor(blocks[u][l + 1][:, :, :], pair[:, :, :, 0], pair[:, :, :, 1], ALU.mult
                                              ).then_inc(decays_ready[l], 1)
                        for c in range(2):
                            x = right(kq[u][:, :, :, :], l)[:, :, c, :, :]
                            last = dve.tensor_tensor(x, x, pair[:, :, :, 0].unsqueeze(3).to_broadcast(
                                [P, HB, T // (2 * L), L]), ALU.mult)
                        last.then_inc(scaled[l], 1)
                    out = bank(u, l % 2).rearrange("p (n w c l) -> p n w c l", n=HB, w=2, l=L)
                    mask = w.levels[:, l:l + 1, :].rearrange("p o (c l) -> p o c l", l=L)
                    shape = [P, HB, T // (2 * L), L]
                    ct = CT[u][l][:, :, :].rearrange("p n (c two l) -> p n c two l", two=2, l=L)[:, :, :, 1, :]
                    pt = PT[u][:, :, :].rearrange("p n (c two l) -> p n c two l", two=2, l=L)[:, :, :, 1, :]
                    if l == 0:
                        dve.wait_ge(cleared, upto(i, u) + 1)
                    else:
                        dve.wait_ge(level_kept[l - 1], upto(i, u))
                    dve.tensor_tensor(ct, out[:, :, 0, :, :], mask.to_broadcast(shape), ALU.mult)
                    dve.copy_predicated(pt, mask.bitcast(U32).to_broadcast(shape), out[:, :, 1, :, :]
                                        ).then_inc(level_kept[l], 1)

            def flat(ap):
                return ap[:, :, :].rearrange("p n t -> p (n t)")
            level(0)
            for l in range(LEVELS - 1):
                level(l + 1)
                for u in BOTH:
                    dve.wait_ge(r_ready[l], upto(i, u))
                    if l == 0:
                        eye = w.eye2[:, :].unsqueeze(1).to_broadcast([P, HB, T])
                        dve.tensor_tensor(R[u][:, :, :], eye, hb(bank(u, 3)), ALU.subtract)
                        dve.tensor_tensor(RT[u][:, :, :], eye, CT[u][0][:, :, :], ALU.subtract).then_inc(r_kept[l], 1)
                        continue
                    if l < LEVELS - 2:
                        dve.wait_ge(r_kept[l - 1], upto(i, u))
                        dve.tensor_tensor(flat(R[u]), flat(R[u]), bank(u, 3), ALU.subtract)
                    dve.tensor_tensor(flat(RT[u]), flat(RT[u]), bank(u, 2), ALU.subtract).then_inc(r_kept[l], 1)
            for u in BOTH:
                dve.wait_ge(r_ready[LEVELS - 1], upto(i, u))
                dve.tensor_tensor(flat(U[u]), flat(U[u]), bank(u, 2), ALU.subtract).then_inc(r_kept[LEVELS - 1], 1)
            for u in BOTH:
                dve.wait_ge(yinv_ready, upto(i, u))
                dve.tensor_tensor(yn[u][:, :], yinv[u][:, :], bank(u, 0), ALU.mult).then_inc(yn_ready, 1)
            for u in BOTH:
                dve.wait_ge(out_ready, upto(i, u))
                dve.tensor_scalar(yT[:, ds(i * (2 * TT) + u * TT, TT)], bank(u, 3)[:, 0:TT], 1.0, None, ALU.mult
                                  ).then_inc(out_kept, 1)


def delta_output(k, s, yT):
    nc = k.nc
    a = k.a
    FF = 512
    with Stage(k, "dout") as t:
        w_u1, w_u2 = t.sb("w_u1", [P, DK]), t.sb("w_u2", [DK, D])
        w_1, w_3, w_2 = t.sb("w_1", [P, FF]), t.sb("w_3", [P, FF]), t.sb("w_2", [P, FF // P, D])
        bu1, bu2, ff_norm = t.sb("bu1", [DK, 1]), t.sb("bu2", [P, 1]), t.sb("ff_norm", [P, 1])
        rms_eps = t.sb("rms_eps", [P, 1])
        u1 = t.sb("u1", [DK, N])
        two = lambda name, shape: [t.sb(f"{name}{u}", shape) for u in range(2)]
        gate, sq, log, rstd, gated, z = (two(n, [P, G]) for n in ("gate", "sq", "log", "rstd", "gated", "z"))
        act1, hid = two("act1", [P, G]), two("hid", [P, G])
        (loaded,) = t.sems("loaded")
        with Stage(k, "dg1") as r:
            u_ready, u_kept = r.sems("u_ready", "u_kept")
            block = r.block()

            @block.sync
            def _(sync):
                for dst, src in ((w_u1[:, :], a["L1_attn_Wu1"]), (w_u2[:, :], a["L1_attn_Wu2"]),
                                 (w_1[:, :], a["L1_attn_Wff1"]), (w_3[:, :], a["L1_attn_Wff3"]),
                                 (w_2[:, :, :], a["L1_attn_Wff2"].rearrange("(c p) d -> p c d", p=P))):
                    sync.dma_start(dst, src).then_inc(loaded, 16)
                with nc.allow_non_contiguous_dma(reason="columns"):
                    for dst, name in ((bu1, "bu1"), (bu2, "bu2"), (ff_norm, "ff_norm_w")):
                        sync.dma_start(dst[:, :], column(a[f"L1_attn_{name}"])).then_inc(loaded, 16)

            @block.tensor
            def _(pe):
                pe.wait_ge(loaded, 128)
                with pe.Fori(0, NG // 2) as i:
                    for u in range(2):
                        nc.tensor.matmul(k.bank[u][0:DK, :], w_u1[:, :], k.X[:, ds(i * (2 * G) + u * G, G)],
                                         start=True, stop=True).then_inc(u_ready, 1)
                    pe.wait_ge(u_kept, i * 2 + 2)

            @block.scalar
            def _(act):
                act.preload_act_table(ACT.Silu)
                act.wait_ge(loaded, 128)
                with act.Fori(0, NG // 2) as i:
                    for u in range(2):
                        act.wait_ge(u_ready, i * 2 + (u + 1))
                        act.activation(u1[:, ds(i * (2 * G) + u * G, G)], k.bank[u][0:DK, :], ACT.Silu, bias=bu1[:, :]
                                       ).then_inc(u_kept, 1)
        with Stage(k, "dg2") as r:
            g_ready, gate_ready, gated_ready, y1_ready = r.sems("g_ready", "gate_ready", "gated_ready", "y1_ready")
            block = r.block()

            @block.tensor
            def _(pe):
                with pe.Fori(0, NG // 2) as i:
                    for u in range(2):
                        nc.tensor.matmul(k.bank[u][:, :], w_u2[:, :], u1[:, ds(i * (2 * G) + u * G, G)],
                                         start=True, stop=True).then_inc(g_ready, 1)
                    pe.wait_ge(gate_ready, i * 2 + 2)

            @block.scalar
            def _(act):
                act.preload_act_table(ACT.Sigmoid)
                with act.Fori(0, NG // 2) as i:
                    for u in range(2):
                        act.wait_ge(g_ready, i * 2 + (u + 1))
                        act.activation(gate[u][:, :], k.bank[u][:, :], ACT.Sigmoid, bias=bu2[:, :]
                                       ).then_inc(gate_ready, 1)
                    act.wait_ge(gated_ready, i * 2 + 2)

            @block.vector
            def _(dve):
                dve.memset(rms_eps[:, :], RMS_EPS)
                with dve.Fori(0, NG // 2) as i:
                    for u in range(2):
                        dve.wait_ge(gate_ready, i * 2 + (u + 1))
                        y = yT[:, ds(i * (2 * G) + u * G, G)]
                        dve.tensor_tensor(gated[u][:, :], y, gate[u][:, :], ALU.mult).then_inc(gated_ready, 1)
                        dve.wait_ge(gated_ready, i * 2 + (u + 1))
                        dve.tensor_tensor(y, gated[u][:, :], k.X[:, ds(i * (2 * G) + u * G, G)], ALU.add
                                          ).then_inc(y1_ready, 1)
        with Stage(k, "dff") as r:
            zT = r.sb("zT", [P, N])
            with Stage(k, "drms") as q:
                squared, mean_ready, log_ready, rstd_ready, z_ready = q.sems(
                    "squared", "mean_ready", "log_ready", "rstd_ready", "z_ready")
                block = q.block()

                @block.scalar
                def _(act):
                    act.preload_act_table_set(LOG_EXP)
                    with act.Fori(0, NG // 2) as i:
                        for u in range(2):
                            act.activation(sq[u][:, :], yT[:, ds(i * (2 * G) + u * G, G)], ACT.Square
                                           ).then_inc(squared, 1)
                        for u in range(2):
                            act.wait_ge(mean_ready, i * 2 + (u + 1))
                            act.activation(log[u][:, :], k.bank[u][:, :], ACT.Ln, bias=rms_eps[:, :]
                                           ).then_inc(log_ready, 1)
                            act.wait_ge(log_ready, i * 2 + (u + 1))
                            act.activation(rstd[u][:, :], log[u][:, :], ACT.Exp, scale=-0.5).then_inc(rstd_ready, 1)
                        act.wait_ge(z_ready, i * 2 + 2)

                @block.tensor
                def _(pe):
                    with pe.Fori(0, NG // 2) as i:
                        for u in range(2):
                            pe.wait_ge(squared, i * 2 + (u + 1))
                            nc.tensor.matmul(k.bank[u][:, :], k.ones_mean[:, :], sq[u][:, :], start=True, stop=True
                                             ).then_inc(mean_ready, 1)

                @block.vector
                def _(dve):
                    with dve.Fori(0, NG // 2) as i:
                        for u in range(2):
                            dve.wait_ge(rstd_ready, i * 2 + (u + 1))
                            g_at = ds(i * (2 * G) + u * G, G)
                            dve.scalar_tensor_tensor(zT[:, g_at], yT[:, g_at], ff_norm[:, :], rstd[u][:, :], ALU.mult,
                                                     ALU.mult).then_inc(z_ready, 1)
            up1_ready, up3_ready, silu_ready, hid_ready, down_ready, summed, added = r.sems(
                "up1_ready", "up3_ready", "silu_ready", "hid_ready", "down_ready", "summed", "added")
            block = r.block()
            C = FF // P
            UNITS = 2 * C

            @block.tensor
            def _(pe):
                with pe.Fori(0, NG // 2) as i:
                    def up(n):
                        if n >= 2:
                            pe.wait_ge(hid_ready, i * UNITS + (n - 1))
                        f = slice((n % C) * P, (n % C + 1) * P)
                        for m, (wt, ready) in enumerate(((w_1, up1_ready), (w_3, up3_ready))):
                            nc.tensor.matmul(k.bank[2 * (n % 2) + m][:, :], wt[:, f],
                                             zT[:, ds(i * (2 * G) + (n // C) * G, G)], start=True, stop=True
                                             ).then_inc(ready, 1)

                    def down(n):
                        pe.wait_ge(hid_ready, i * UNITS + (n + 1))
                        last = nc.tensor.matmul(k.bank[4 + n // C][:, :], w_2[:, n % C, :], hid[n % 2][:, :],
                                                start=(n % C == 0), stop=(n % C == C - 1))
                        if n % C == C - 1:
                            last.then_inc(down_ready, 1)
                    up(0)
                    for n in range(1, UNITS):
                        up(n)
                        down(n - 1)
                    down(UNITS - 1)
                    pe.wait_ge(added, i * 2 + 2)

            @block.scalar
            def _(act):
                act.preload_act_table(ACT.Silu)
                with act.Fori(0, NG // 2) as i:
                    for n in range(UNITS):
                        act.wait_ge(up1_ready, i * UNITS + (n + 1))
                        act.activation(act1[n % 2][:, :], k.bank[2 * (n % 2)][:, :], ACT.Silu).then_inc(silu_ready, 1)

            @block.vector
            def _(dve):
                with dve.Fori(0, NG // 2) as i:
                    for u in range(2):
                        g_at = ds(i * (2 * G) + u * G, G)
                        dve.tensor_tensor(k.X[:, g_at], k.X[:, g_at], yT[:, g_at], ALU.add).then_inc(summed, 1)
                        for c in range(C):
                            n = u * C + c
                            dve.wait_ge(silu_ready, i * UNITS + (n + 1))
                            dve.wait_ge(up3_ready, i * UNITS + (n + 1))
                            dve.tensor_tensor(hid[n % 2][:, :], act1[n % 2][:, :], k.bank[2 * (n % 2) + 1][:, :], ALU.mult
                                              ).then_inc(hid_ready, 1)
                        dve.wait_ge(down_ready, i * 2 + (u + 1))
                        dve.wait_ge(summed, i * 2 + (u + 1))
                        dve.tensor_tensor(k.X[:, g_at], k.X[:, g_at], k.bank[4 + u][:, :], ALU.add).then_inc(added, 1)


def delta_stage(k):
    with Stage(k, "delta") as s:
        hT = s.sb("hT", [P, N])
        with Stage(k, "dr") as r:
            uT, spikes = r.sb("uT", [DK, N]), r.sb("spikes", [P, DP, N], BF16)
            delta_inputs(k, r, hT, uT)
            delta_spikes(k, r, hT, spikes)
            delta_rule(k, r, hT, uT, spikes, hT)
        delta_output(k, s, hT)


def context_mlp(k):
    nc = k.nc
    H = BG // 2
    with Stage(k, "cmlp") as s:
        turn_context(k, s, "cmlp_ctx")
        hid = [s.sb(f"hid{u}", [P, H, T]) for u in range(2)]
        ctx_g = [s.sb(f"ctxT{u}", [P, G]) for u in range(2)]
        x_g = [s.sb(f"x{u}", [P, G]) for u in range(2)]
        row_g = [s.sb(f"rows{u}", [P, H, D]) for u in range(2)]
        staged, h_ready, gelu_ready, y_ready, added = s.sems("operands_staged", "h_ready", "gelu_ready",
                                                             "y_ready", "added")
        block = s.block()
        h_bank, y_bank = k.bank[0:2], k.bank[2:6]

        @block.vector
        def _(dve):
            with dve.Fori(0, NG // 2) as i:
                for u in range(2):
                    dve.tensor_copy(ctx_g[u][:, :], k.ctxT[:, ds(i * (2 * G) + u * G, G)])
                    dve.tensor_copy(row_g[u][:, :, :], k.ctx_rows[:, ds(i * (2 * H) + u * H, H), :])
                    dve.tensor_copy(x_g[u][:, :], k.X[:, ds(i * (2 * G) + u * G, G)]).then_inc(staged, 1)
                for u in range(2):
                    dve.wait_ge(y_ready, i * 2 + (u + 1))
                    for half in range(2):
                        x = k.X[:, ds(i * (2 * G) + u * G, G)].rearrange("p (n c t) -> p n c t", c=2, t=T)[:, :, half, :]
                        y = y_bank[2 * u + half][:, 0:G // 2].rearrange("p (n t) -> p n t", t=T)
                        dve.tensor_tensor(x, x, y, ALU.add).then_inc(added, 1)

        @block.tensor
        def _(pe):
            with pe.Fori(0, NG // 2) as i:
                for u in range(2):
                    pe.wait_ge(staged, i * 2 + (u + 1))
                    for n in range(H):
                        for half in range(2):
                            c = (2 * n + half) * T
                            last = nc.tensor.matmul(h_bank[u][half * T:half * T + T, n * T:(n + 1) * T],
                                                    ctx_g[u][:, c:c + T], x_g[u][:, c:c + T],
                                                    start=True, stop=True)
                    last.then_inc(h_ready, 1)
                for u in range(2):
                    pe.wait_ge(gelu_ready, i * 2 + (u + 1))
                    for n in range(H):
                        for half in range(2):
                            r = slice(half * T, half * T + T)
                            last = nc.tensor.matmul(y_bank[2 * u + half][:, n * T:(n + 1) * T],
                                                    row_g[u][r, n, :], hid[u][r, n, :], start=True, stop=True)
                    last.then_inc(y_ready, 1)

        @block.scalar
        def _(act):
            with act.Fori(0, NG // 2) as i:
                for u in range(2):
                    act.wait_ge(h_ready, i * 2 + (u + 1))
                    act.activation(hid[u][:, :, :].rearrange("p n t -> p (n t)"), h_bank[u][:, 0:H * T],
                                   ACT.Gelu_apprx_tanh).then_inc(gelu_ready, 1)


FE, FK, FH = 8, 16, 512
FC = FH // P
EK = FE * FK


def pick_tokens(k, s):
    nc = k.nc
    f = Core()
    f.picks = s.sb("picks", [P, 2, 2, 2, NT // 2])
    with Stage(k, "gate") as t:
        gate_rows, gateT = t.sb("gate_rows", [FE, D]), t.sb("gateT", [P, FE])
        x_g = [t.sb(f"x{u}", [P, G]) for u in range(2)]
        shifted, expd, probs = (t.sb(n, [P, NT, FE]) for n in ("shifted", "exp", "probs"))
        top, total, inv = (t.sb(n, [P, NT]) for n in ("top", "total", "inv"))
        probsT = t.sb("probsT", [P, 4, T])
        rest = t.sb("rest", [P, 4, T])
        values, places_u, places = t.sb("values", [P, 4, FK]), t.sb("places_u", [P, 4, FK], U32), t.sb("places", [P, 4, FK])
        is_expert, is_tile = t.sb("is_expert", [P, FE]), t.sb("is_tile", [P, NT // 2])
        spread = t.sb("spread", [P, 2, 4, FE, FK])
        (gate_loaded, gate_turned, gateT_ready, staged, scored, step, exp_ready, turned, spread_ready, moved) = t.sems(
            "gate_loaded", "gate_turned", "gateT_ready", "staged", "scored", "dve_step", "exp_ready", "turned",
            "spread_ready", "moved")
        block = t.block()
        GATE = k.bank[0][:, 0:NT * FE]
        TURNED = k.bank[1][:, 0:4 * T]

        @block.sync
        def _(sync):
            sync.dma_start(gate_rows[:, :], k.a["L1_ffn_gate_w"]).then_inc(gate_loaded, 16)

        @block.tensor
        def _(pe):
            pe.wait_ge(gate_loaded, 16)
            nc.tensor.transpose(k.bank[2][:, 0:FE], gate_rows[:, :], k.eye[0:FE, 0:FE]).then_inc(gate_turned, 1)
            pe.wait_ge(gateT_ready, 1)
            with pe.Fori(0, NG // 2) as i:
                for u in range(2):
                    pe.wait_ge(staged, i * 2 + (u + 1))
                    for n in range(4):
                        last = nc.tensor.matmul(k.bank[0][:, ds(i * (8 * FE) + (u * 4 + n) * FE, FE)],
                                                x_g[u][:, n * D:(n + 1) * D], gateT[:, :], start=True, stop=True)
                    last.then_inc(scored, 1)
            pe.wait_ge(step, 6)
            for h in range(2):
                last = nc.tensor.transpose(TURNED[:, h * TT:(h + 1) * TT],
                                           probs[:, h * 16:(h + 1) * 16, :].rearrange("p n e -> p (n e)"), k.eye[:, :])
            last.then_inc(turned, 1)
            pe.wait_ge(spread_ready, 2)
            for w in range(2):
                for c in range(4):
                    last = nc.tensor.matmul(k.bank[2][:, (4 * w + c) * 16:(4 * w + c + 1) * 16],
                                            spread[:, w, c, :, :].rearrange("p e r -> p (e r)"), is_tile[:, :],
                                            start=True, stop=True)
            last.then_inc(moved, 1)

        @block.vector
        def _(dve):
            eye = k.eye[:, :]
            dve.tensor_reduce(is_expert[:, :], eye.rearrange("p (n e) -> p e n", e=FE), AX_X, ALU.add).then_inc(step, 1)
            dve.tensor_reduce(is_tile[:, :], eye.rearrange("p (n e) -> p n e", e=FE), AX_X, ALU.add).then_inc(step, 1)
            dve.wait_ge(gate_turned, 1)
            dve.tensor_copy(gateT[:, :], k.bank[2][:, 0:FE]).then_inc(gateT_ready, 1)
            dve.tensor_copy(x_g[0][:, :], k.X[:, 0:G]).then_inc(staged, 1)
            dve.tensor_copy(x_g[1][:, :], k.X[:, G:2 * G]).then_inc(staged, 1)
            with dve.Fori(0, NG // 2 - 1) as i:
                for u in range(2):
                    dve.wait_ge(scored, i * 2 + (u + 1))
                    dve.tensor_copy(x_g[u][:, :], k.X[:, ds(i * (2 * G) + (u + 2) * G, G)]).then_inc(staged, 1)
            dve.wait_ge(scored, NG)
            sc = GATE.rearrange("p (n e) -> p n e", e=FE)
            over = lambda ap: ap.unsqueeze(2).to_broadcast([P, NT, FE])
            dve.tensor_reduce(top[:, :], sc, AX_X, ALU.max).then_inc(step, 1)
            dve.wait_ge(step, 3)
            dve.tensor_tensor(shifted[:, :, :], sc, over(top[:, :]), ALU.subtract).then_inc(spread_ready, 1)
            dve.wait_ge(exp_ready, 1)
            dve.tensor_reduce(total[:, :], expd[:, :, :], AX_X, ALU.add).then_inc(step, 1)
            dve.wait_ge(step, 4)
            dve.reciprocal(inv[:, :], total[:, :]).then_inc(step, 1)
            dve.wait_ge(step, 5)
            dve.tensor_tensor(probs[:, :, :], expd[:, :, :], over(inv[:, :]), ALU.mult).then_inc(step, 1)
            dve.wait_ge(turned, 1)
            dve.tensor_copy(probsT[:, :, :].rearrange("p c t -> p (c t)"), TURNED).then_inc(step, 1)
            n = 7
            for c in range(4):
                first, second = slice(0, 8), slice(8, 16)
                dve.wait_ge(step, n)
                dve.max(values[:, c, first], probsT[:, c, :]).then_inc(step, 1)
                dve.wait_ge(step, n + 1)
                dve.max_index(places_u[:, c, first], values[:, c, first], probsT[:, c, :]).then_inc(step, 1)
                dve.match_replace(rest[:, c, :], values[:, c, first], probsT[:, c, :], -1.0).then_inc(step, 1)
                dve.wait_ge(step, n + 3)
                dve.max(values[:, c, second], rest[:, c, :]).then_inc(step, 1)
                dve.wait_ge(step, n + 4)
                dve.max_index(places_u[:, c, second], values[:, c, second], rest[:, c, :]).then_inc(step, 1)
                n += 5
            dve.wait_ge(step, n)
            dve.tensor_copy(places[:, :, :], places_u[:, :, :]).then_inc(step, 1)
            dve.wait_ge(step, n + 1)
            for w, src in enumerate((places, values)):
                for c in range(4):
                    last = dve.tensor_tensor(spread[:, w, c, :, :], src[:, c, :].unsqueeze(1).to_broadcast([P, FE, FK]),
                                             is_expert[:, :].unsqueeze(2).to_broadcast([P, FE, FK]), ALU.mult)
            last.then_inc(spread_ready, 1)
            dve.wait_ge(moved, 1)
            dve.tensor_copy(f.picks[:, :, :, :, :].rearrange("p w h b n -> p (w h b n)"), k.bank[2][:, 0:P]
                            ).then_inc(step, 1)

        @block.scalar
        def _(act):
            act.wait_ge(spread_ready, 1)
            act.activation(expd[:, :, :], shifted[:, :, :], ACT.Exp).then_inc(exp_ready, 1)
    return f


def picked_experts(k):
    nc = k.nc
    with Stage(k, "topk") as s:
        picked = s.sb("picked", [P, FE, B, FK])
        scatter = s.sb("scatter", [P, B, T])
        outs = s.sb("outs", [P, FE, B, FK])
        with Stage(k, "gather") as r:
            f = pick_tokens(k, r)
            tokens = r.sb("token_number", [P, T])
            place, gate = r.sb("place", [P, B]), r.sb("gate_of", [P, B])
            one_hot = [r.sb(f"one_hot{u}", [P, 4, T]) for u in range(2)]
            x_t = [r.sb(f"x{u}", [P, 2 * TT]) for u in range(2)]
            rows, hot_rows = ([r.sb(f"{n}{u}", [P, 2, P]) for u in range(2)] for n in ("rows", "hot_rows"))
            numbered, ordered, hot_ready, staged, scatter_ready, turned, turned_kept, gathered, kept = r.sems(
                "numbered", "ordered", "hot_ready", "staged", "scatter_ready", "turned", "turned_kept", "gathered", "kept")
            block = r.block()
            NQ = NT // 2

            @block.gpsimd
            def _(pool):
                pool.iota(tokens[:, :], pattern=[[1, T]], base=0, channel_multiplier=0,
                          allow_small_or_imprecise_dtypes=True).then_inc(numbered, 1)

            @block.vector
            def _(dve):
                for w, dst in enumerate((place, gate)):
                    last = dve.tensor_copy(dst[:, :].rearrange("p (h n b) -> p h b n", h=2, b=2), f.picks[:, w, :, :, :])
                last.then_inc(ordered, 1)
                dve.wait_ge(numbered, 1)
                dve.wait_ge(ordered, 1)
                with dve.Fori(0, NQ // 2) as i:
                    for u in range(2):
                        dve.tensor_tensor(one_hot[u][:, :, :], tokens[:, :].unsqueeze(1).to_broadcast([P, 4, T]),
                                          place[:, ds(i * 8 + u * 4, 4)].unsqueeze(2).to_broadcast([P, 4, T]),
                                          ALU.is_equal).then_inc(hot_ready, 1)
                        dve.tensor_copy(x_t[u][:, :], k.X[:, ds(i * (4 * TT) + u * 2 * TT, 2 * TT)]).then_inc(staged, 1)
                        dve.wait_ge(hot_ready, i * 2 + (u + 1))
                        dve.tensor_tensor(scatter[:, ds(i * 8 + u * 4, 4), :], one_hot[u][:, :, :],
                                          gate[:, ds(i * 8 + u * 4, 4)].unsqueeze(2).to_broadcast([P, 4, T]),
                                          ALU.mult).then_inc(scatter_ready, 1)
                    for u in range(2):
                        dve.wait_ge(gathered, i * 2 + (u + 1))
                        for b in range(2):
                            for j in range(2):
                                last = dve.tensor_copy(picked[:, :, ds(i * 8 + (u * 4 + 2 * j + b), 1), :],
                                                       k.bank[2 + 2 * u + b][:, j * EK:(j + 1) * EK].rearrange(
                                                           "p (e n r) -> p e n r", n=1, r=FK))
                        last.then_inc(kept, 1)

            @block.tensor
            def _(pe):
                with pe.Fori(0, NQ // 2) as i:
                    for u in range(2):
                        pe.wait_ge(staged, i * 2 + (u + 1))
                        for j in range(2):
                            nc.tensor.transpose(k.bank[u][:, j * P:(j + 1) * P], x_t[u][:, j * TT:(j + 1) * TT], k.eye[:, :])
                            last = nc.tensor.transpose(
                                k.bank[u][:, (2 + j) * P:(3 + j) * P],
                                one_hot[u][:, 2 * j:2 * j + 2, :].rearrange("p b t -> p (b t)"), k.eye[:, :])
                        last.then_inc(turned, 1)
                    for u in range(2):
                        k.hold(pe)
                        pe.wait_ge(turned_kept, i * 2 + (u + 1))
                        for j in range(2):
                            for b in range(2):
                                r = slice(b * T, (b + 1) * T)
                                last = nc.tensor.matmul(k.bank[2 + 2 * u + b][:, j * EK:(j + 1) * EK], rows[u][r, j, :],
                                                        hot_rows[u][r, j, :], start=True, stop=True)
                        last.then_inc(gathered, 1)

            @block.scalar
            def _(act):
                with act.Fori(0, NQ // 2) as i:
                    for u in range(2):
                        act.wait_ge(turned, i * 2 + (u + 1))
                        act.activation(rows[u][:, :, :].rearrange("p j d -> p (j d)"), k.bank[u][:, 0:2 * P], ACT.Copy)
                        act.activation(hot_rows[u][:, :, :].rearrange("p j d -> p (j d)"), k.bank[u][:, 2 * P:4 * P],
                                       ACT.Copy).then_inc(turned_kept, 1)

        with Stage(k, "experts") as e:
            w1 = [e.sb(f"w1_{u}", [P, FH]) for u in range(2)]
            w2 = [e.sb(f"w2_{u}", [P, FC, D]) for u in range(2)]
            hid = [e.sb(f"hid{u}", [P, 2, 512]) for u in range(3)]
            w_loaded = e.sems("w_loaded0", "w_loaded1")
            h_ready, gelu_ready, y_ready, y_kept = e.sems("h_ready", "gelu_ready", "y_ready", "y_kept")
            block = e.block()
            picks2 = picked[:, :, :, :].rearrange("p e (h n) r -> p (e h) (n r)", h=2)
            outs2 = outs[:, :, :, :].rearrange("p e (h n) r -> p (e h) (n r)", h=2)
            a1, a2 = k.a["L1_ffn_w1"], k.a["L1_ffn_w2"]

            @block.sync
            def _(sync):
                def load(expert, u):
                    sync.dma_start(w1[u][:, :], a1[ds(expert, 1), :, :].rearrange("o d f -> d (o f)")).then_inc(w_loaded[u], 16)
                    sync.dma_start(w2[u][:, :, :], a2[ds(expert, 1), :, :].rearrange("o (c p) d -> p (o c) d", p=P)
                                   ).then_inc(w_loaded[u], 16)
                for u in range(2):
                    load(u, u)
                with sync.Fori(0, FE // 2 - 1) as i:
                    for u in range(2):
                        sync.wait_ge(y_ready, i * 4 + (2 * u + 2))
                        load(i * 2 + (u + 2), u)

            @block.tensor
            def _(pe):
                with pe.Fori(0, FE // 2) as i:
                    def hidden(n):
                        u, half, pair = n // 4, (n // 2) % 2, n % 2
                        if n % 4 == 0:
                            pe.wait_ge(w_loaded[u], i * 32 + 32)
                        for c in range(2):
                            f0 = (2 * pair + c) * P
                            last = nc.tensor.matmul(k.bank[2 * (n % 3) + c][:, :], w1[u][:, f0:f0 + P],
                                                    picks2[:, ds(i * 4 + (n // 2), 1), :].rearrange("p o c -> p (o c)"),
                                                    start=True, stop=True)
                        last.then_inc(h_ready, 1)

                    def output(n):
                        u, half, pair = n // 4, (n // 2) % 2, n % 2
                        pe.wait_ge(gelu_ready, i * 8 + (n + 1))
                        if n >= 4 and pair == 0:
                            pe.wait_ge(y_kept, i * 4 + (n // 2 - 1))
                        for c in range(2):
                            last = nc.tensor.matmul(k.bank[6 + half][:, :], w2[u][:, 2 * pair + c, :], hid[n % 3][:, c, :],
                                                    start=(pair == 0 and c == 0), stop=(pair == 1 and c == 1))
                        if pair == 1:
                            last.then_inc(y_ready, 1)
                    hidden(0)
                    for n in range(8):
                        if n < 7:
                            hidden(n + 1)
                        output(n)
                    pe.wait_ge(y_kept, i * 4 + 4)

            @block.scalar
            def _(act):
                act.preload_act_table(ACT.Gelu)
                with act.Fori(0, FE // 2) as i:
                    for n in range(8):
                        act.wait_ge(h_ready, i * 8 + (n + 1))
                        act.activation(hid[n % 3][:, :, :], k.psum[:, 2 * (n % 3):2 * (n % 3) + 2, :], ACT.Gelu
                                       ).then_inc(gelu_ready, 1)

            @block.vector
            def _(dve):
                with dve.Fori(0, FE // 2) as i:
                    for m in range(4):
                        dve.wait_ge(y_ready, i * 4 + (m + 1))
                        dve.tensor_copy(outs2[:, ds(i * 4 + m, 1), :].rearrange("p o c -> p (o c)"), k.bank[6 + m % 2][:, :]
                                        ).then_inc(y_kept, 1)

        with Stage(k, "scatter") as r:
            y_t = [r.sb(f"y{u}", [P, 4, EK]) for u in range(2)]
            rows = [r.sb(f"rows{u}", [P, 4, D]) for u in range(2)]
            staged, turned, rows_ready, out_ready, added = r.sems("staged", "turned", "rows_ready", "out_ready", "added")
            block = r.block()
            NU = B // 4

            @block.vector
            def _(dve):
                with dve.Fori(0, NU // 2) as i:
                    for u in range(2):
                        dve.tensor_copy(y_t[u][:, :, :].rearrange("p n (e r) -> p e n r", e=FE),
                                        outs[:, :, ds(i * 8 + u * 4, 4), :]).then_inc(staged, 1)
                    for u in range(2):
                        dve.wait_ge(out_ready, i * 2 + (u + 1))
                        x = k.X[:, ds(i * (8 * T) + u * 4 * T, 4 * T)]
                        dve.tensor_tensor(x, x, k.bank[2 + u][:, 0:4 * T], ALU.add).then_inc(added, 1)

            @block.tensor
            def _(pe):
                with pe.Fori(0, NU // 2) as i:
                    for u in range(2):
                        pe.wait_ge(staged, i * 2 + (u + 1))
                        for b in range(4):
                            last = nc.tensor.transpose(k.bank[u][:, b * D:(b + 1) * D], y_t[u][:, b, :], k.eye[:, :])
                        last.then_inc(turned, 1)
                    for u in range(2):
                        pe.wait_ge(rows_ready, i * 2 + (u + 1))
                        for b in range(4):
                            last = nc.tensor.matmul(k.bank[2 + u][:, b * T:(b + 1) * T], rows[u][:, b, :],
                                                    scatter[:, ds(i * 8 + (u * 4 + b), 1), :].rearrange("p o t -> p (o t)"),
                                                    start=True, stop=True)
                        last.then_inc(out_ready, 1)

            @block.scalar
            def _(act):
                with act.Fori(0, NU // 2) as i:
                    for u in range(2):
                        act.wait_ge(turned, i * 2 + (u + 1))
                        act.activation(rows[u][:, :, :].rearrange("p b d -> p (b d)"), k.bank[u][:, :], ACT.Copy
                                       ).then_inc(rows_ready, 1)


def store_tokens(k):
    nc = k.nc
    with Stage(k, "store") as s:
        rows = s.sb("rows", [P, NT, D])
        turned, kept, stored = s.sems("turned", "kept", "stored")
        block = s.block()
        out = k.out.rearrange("(n u) t d -> (u t) n d", u=2)

        @block.tensor
        def _(pe):
            for g in range(NG):
                for j in range(4):
                    last = nc.tensor.transpose(k.bank[g][:, j * D:(j + 1) * D], k.X[:, g * G + j * D:g * G + (j + 1) * D],
                                               k.eye[:, :])
                last.then_inc(turned, 1)

        @block.vector
        def _(dve):
            for g in range(NG):
                dve.wait_ge(turned, g + 1)
                dve.tensor_copy(rows[:, 4 * g:4 * g + 4, :].rearrange("p n d -> p (n d)"),
                                k.bank[g][:, :]).then_inc(kept, 1)

        @block.sync
        def _(sync):
            for g in range(0, NG, 2):
                sync.wait_ge(kept, g + 2)
                sync.dma_start(out[:, 4 * g:4 * g + 8, :], rows[:, 4 * g:4 * g + 8, :]).then_inc(stored, 16)
            sync.wait_ge(stored, 16 * NG // 2)


def host_constants():
    inv_freq = (1.0 / 10000.0 ** (np.arange(0, AK, 2, dtype=np.float32) / AK)).astype(np.float32)
    angle = (np.arange(T, dtype=np.float32)[None, :] * inv_freq[:, None]).astype(np.float32)
    cos, sin = np.cos(angle), np.sin(angle)
    table = np.stack([np.concatenate([cos, cos, cos, cos]), np.concatenate([-sin, sin, -sin, sin])], axis=1)
    s = np.arange(P) % T
    levels = np.zeros((P, LEVELS, T // 2), np.float32)
    for l in range(LEVELS):
        half = 1 << l
        block = np.arange(T // 2) // half
        levels[:, l, :] = (s[:, None] // (2 * half) == block[None, :]) & (s[:, None] % (2 * half) < half)
    head = np.arange(P) // DK
    return {"level_masks": levels, "eye2": np.tile(np.eye(T, dtype=np.float32), (2, 1)),
            "head_sum": (head[:, None] == head[None, :]).astype(np.float32),
            "rope_q": (table * np.float32(AK ** -0.5)).astype(np.float32), "rope_k": table.astype(np.float32)}


STAGES = ["attn", "ln1", "xattn", "ln2", "moe", "ln3", "delta", "ln4", "cmlp", "ln5", "topk", "ln6"]


def decoder(nc, a, out):
    k = Core()
    k.nc, k.a, k.out = nc, a, out
    with ExitStack() as stack:
        def sb(name, shape, dt=F32):
            return stack.enter_context(nc.sbuf_tensor(name, shape, dt))
        k.X = sb("X", [P, N])
        k.ctx_rows = sb("ctx_rows", [P, NT, D])
        k.eye = sb("eye", [P, P])
        k.ones_mean = sb("ones_mean", [P, P])
        k.ln_eps = sb("ln_eps", [P, 1])
        k.psum = stack.enter_context(nc.psum_tensor("psum", [P, 8, 512], F32))
        k.bank = [k.psum[:, i, :] for i in range(8)]
        k.ln_sems = [stack.enter_context(nc.semaphore(f"ln_{n}")) for n in (
            "mean_ready", "centred", "squared", "var_ready", "log_ready", "rstd_ready", "normed")]
        k.ln_calls = 0
        k.ctx_loaded = stack.enter_context(nc.semaphore("ctx_loaded"))
        k.eye_made = stack.enter_context(nc.semaphore("eye_made"))
        load_tokens(k)
        for st in STAGES:
            if st.startswith("ln"):
                layer_norm(k, k.ln_calls)
                k.ln_calls += 1
            else:
                {"attn": rope_attention, "xattn": cross_attention, "moe": soft_mixture, "delta": delta_stage,
                 "cmlp": context_mlp, "topk": picked_experts}[st](k)
        store_tokens(k)


INPUTS = ["x", "ctx_1024"] + [f"L0_attn_{n}" for n in ("Wq", "bq", "Wk", "bk", "Wv", "bv", "Wo", "bo")] + [
    f"L0_xattn_{n}" for n in ("wq_w", "wq_b", "wk_w", "wk_b", "wv_w", "wv_b", "wo_w", "wo_b")] + [
    f"L0_ffn_{n}" for n in ("ln_gamma", "ln_beta", "mu", "scale", "w1", "b1", "w2", "b2")] + [
    f"L1_attn_{n}" for n in ("norm_in_w", "conv_w", "conv_b", "Wq", "Wk", "Wv", "Wo", "Wspike", "Wau", "bau", "Wad", "bad",
                             "alpha_spike", "Wbeta", "bbeta", "beta_spike", "head_norm_w", "Wu1", "bu1", "Wu2", "bu2",
                             "ff_norm_w", "Wff1", "Wff3", "Wff2")] + [
    f"L1_ffn_{n}" for n in ("gate_w", "w1", "w2")]


def kernel(**inputs):
    import concourse.bacc as bacc
    from concourse.bass_utils import run_bass_kernel_spmd

    nc = bacc.Bacc("TRN2", target_bir_lowering=False, num_devices=1)
    operands = {name: np.ascontiguousarray(inputs[name]) for name in INPUTS}
    operands.update(host_constants())
    arrays, args = {}, {}
    for name, array in operands.items():
        arrays[f"in_{name}_dram"] = array
        args[name] = nc.dram_tensor(f"in_{name}_dram", array.shape, mybir.dt.from_np(array.dtype),
                                    kind="ExternalInput").ap()
    out = nc.dram_tensor("out_0_dram", (B, T, D), F32, kind="ExternalOutput").ap()
    decoder(nc, args, out)
    r = run_bass_kernel_spmd(nc, [arrays], core_ids=[0])
    return r.results[0]["out_0_dram"]
```

```python
from contextlib import ExitStack

import numpy as np

import concourse.bass as bass
from concourse import mybir

ALU = mybir.AluOpType
ACT = mybir.ActivationFunctionType
F32 = mybir.dt.float32
BF16 = mybir.dt.bfloat16
U32 = mybir.dt.uint32
AX_X = mybir.AxisListType.X
ds = bass.ds

P = 128
B, T, D = 64, 64, 128
N = B * T
TT = 2 * T
NT = N // TT
G = 512
NG = N // G
BG = G // T
LN_EPS = 1e-5
LOG_EXP = "natural_log_exp_and_others"
RMS_EPS = 1e-6


class Core:

    def hold(self, pe):
        pe.wait_ge(self.eye_made, 2)


class Stage:

    def __init__(self, k, name):
        self.nc, self.name, self.stack, self.own = k.nc, name, ExitStack(), []

    def __enter__(self):
        self.stack.__enter__()
        return self

    def __exit__(self, *e):
        done = self.stack.__exit__(*e)
        if self.own:
            self.nc.clear_and_free_semaphores(self.own)
            self.nc.all_engine_barrier()
        return done

    def sb(self, name, shape, dt=F32):
        return self.stack.enter_context(self.nc.sbuf_tensor(f"{self.name}_{name}", shape, dt))

    def sems(self, *names):
        new = [self.nc.alloc_semaphore(f"{self.name}_{n}") for n in names]
        self.own += new
        return new

    def block(self):
        return self.stack.enter_context(self.nc.Block())


def load_tokens(k):
    nc = k.nc
    with Stage(k, "load") as s:
        rows = s.sb("rows", [P, NT, D])
        eye_ready = k.eye_made
        loaded, ones_ready, turned, kept = s.sems("x_loaded", "ones_ready", "turned", "kept")
        block = s.block()
        NB = 8

        @block.sync
        def _(sync):
            sync.dma_start(rows[:, :, :], k.a["x"].rearrange("(n u) t d -> (u t) n d", u=2)).then_inc(loaded, 16)
            sync.dma_start(k.ctx_rows[:, :, :],
                           k.a["ctx_1024"].rearrange("(n u) t d -> (u t) n d", u=2)).then_inc(k.ctx_loaded, 16)

        @block.gpsimd
        def _(pool):
            pool.memset(k.eye[:, :], 0.0).then_inc(eye_ready, 1)
            pool.wait_ge(eye_ready, 1)
            pool.affine_select(out=k.eye[:, :], in_=k.eye[:, :], compare_op=ALU.not_equal, fill=1.0, base=0,
                               pattern=[[-1, P]], channel_multiplier=1).then_inc(eye_ready, 1)

        @block.tensor
        def _(pe):
            pe.wait_ge(eye_ready, 2)
            pe.wait_ge(loaded, 16)
            for g in range(NB):
                for j in range(4):
                    last = nc.tensor.transpose(k.bank[g][:, j * D:(j + 1) * D], rows[:, 4 * g + j, :], k.eye[:, :])
                last.then_inc(turned, 1)

        @block.vector
        def _(dve):
            dve.memset(k.ones_mean[:, :], 1.0 / D).then_inc(ones_ready, 1)
            dve.memset(k.ln_eps[:, :], LN_EPS).then_inc(ones_ready, 1)
            for g in range(NB):
                dve.wait_ge(turned, g + 1)
                dve.tensor_copy(k.X[:, g * G:(g + 1) * G], k.bank[g][:, :]).then_inc(kept, 1)


def turn_context(k, s, name):
    nc = k.nc
    k.ctxT = s.sb("ctxT", [P, N])
    with Stage(k, name) as t:
        turned, kept = t.sems("turned", "kept")
        block = t.block()

        @block.tensor
        def _(pe):
            pe.wait_ge(k.ctx_loaded, 16)
            for g in range(NG):
                for j in range(4):
                    last = nc.tensor.transpose(k.bank[g][:, j * D:(j + 1) * D], k.ctx_rows[:, 4 * g + j, :], k.eye[:, :])
                last.then_inc(turned, 1)

        @block.vector
        def _(dve):
            for g in range(NG):
                dve.wait_ge(turned, g + 1)
                dve.tensor_copy(k.ctxT[:, g * G:(g + 1) * G], k.bank[g][:, :]).then_inc(kept, 1)


def layer_norm(k, call):
    nc = k.nc
    base = call * NG
    with Stage(k, f"ln{call}") as s:
        sq = [s.sb(f"sq{u}", [P, G]) for u in range(2)]
        log_var = [s.sb(f"log_var{u}", [P, G]) for u in range(2)]
        rstd = [s.sb(f"rstd{u}", [P, G]) for u in range(2)]
        mean_ready, centred, squared, var_ready, log_ready, rstd_ready, normed = k.ln_sems
        block = s.block()
        mean, var = k.bank[0:2], k.bank[2:4]

        @block.tensor
        def _(pe):
            with pe.Fori(0, NG // 2) as i:
                for u in range(2):
                    nc.tensor.matmul(mean[u][:, :], k.ones_mean[:, :], k.X[:, ds(i * (2 * G) + u * G, G)],
                                     start=True, stop=True).then_inc(mean_ready, 1)
                for u in range(2):
                    pe.wait_ge(squared, i * 2 + (base + u + 1))
                    nc.tensor.matmul(var[u][:, :], k.ones_mean[:, :], sq[u][:, :],
                                     start=True, stop=True).then_inc(var_ready, 1)

        @block.vector
        def _(dve):
            with dve.Fori(0, NG // 2) as i:
                for u in range(2):
                    dve.wait_ge(mean_ready, i * 2 + (base + u + 1))
                    x = k.X[:, ds(i * (2 * G) + u * G, G)]
                    dve.tensor_tensor(x, x, mean[u][:, :], ALU.subtract).then_inc(centred, 1)
                for u in range(2):
                    dve.wait_ge(rstd_ready, i * 2 + (base + u + 1))
                    x = k.X[:, ds(i * (2 * G) + u * G, G)]
                    dve.tensor_tensor(x, x, rstd[u][:, :], ALU.mult).then_inc(normed, 1)

        @block.scalar
        def _(act):
            act.preload_act_table_set(LOG_EXP)
            with act.Fori(0, NG // 2) as i:
                for u in range(2):
                    act.wait_ge(centred, i * 2 + (base + u + 1))
                    act.activation(sq[u][:, :], k.X[:, ds(i * (2 * G) + u * G, G)], ACT.Square).then_inc(squared, 1)
                for u in range(2):
                    act.wait_ge(var_ready, i * 2 + (base + u + 1))
                    act.activation(log_var[u][:, :], var[u][:, :], ACT.Ln, bias=k.ln_eps[:, :]).then_inc(log_ready, 1)
                    act.wait_ge(log_ready, i * 2 + (base + u + 1))
                    act.activation(rstd[u][:, :], log_var[u][:, :], ACT.Exp, scale=-0.5).then_inc(rstd_ready, 1)


def attention_weights(k, s):
    nc = k.nc
    AD = AH * AK
    NR = AD // P
    w = Core()
    w.q, w.k, w.q_rot, w.k_rot, w.v = (s.sb(n, [P, AD], BF16) for n in ("wqT", "wkT", "wqT_rot", "wkT_rot", "wvT"))
    w.o = s.sb("woT", [P, NR, D])
    w.bq, w.bk, w.bq_rot, w.bk_rot = (s.sb(n, [1, AD], BF16) for n in ("bq", "bk", "bq_rot", "bk_rot"))
    w.ones = s.sb("ones", [1, TT], BF16)
    w.o_bias = s.sb("o_bias", [P, 1])
    w.rope_q, w.rope_k = s.sb("rope_q", [P, 2, T]), s.sb("rope_k", [P, 2, T])
    w.parts = s.sb("x_parts", [P, 3, N], BF16)
    with Stage(k, "attn_w") as t:
        rows = t.sb("rows", [P, 4, NR, P], BF16)
        eye = t.sb("eye", [P, P], BF16)
        left = t.sb("left", [P, 2, N // 2])
        bv_col, bo_col = t.sb("bv_col", [P, NR], BF16), t.sb("bo_col", [P, 1], BF16)
        bv, bo = t.sb("bv", [P, NR]), t.sb("bo", [P, 1])
        rows_loaded, small_loaded, eye_ready, turned, kept, part_ready, bias_ready, wobv_ready, small_ready = t.sems(
            "rows_loaded", "small_loaded", "eye_ready", "turned", "kept", "part_ready", "bias_ready", "wobv_ready",
            "small_ready")
        block = t.block()
        half_bank = [k.bank[i].bitcast(BF16) for i in range(8)]
        rotated = lambda ap: ap.rearrange("p (h c e) -> p h c e", c=2, e=AK // 2)

        @block.sync
        def _(sync):
            for n, name in enumerate(("Wq", "Wk", "Wv")):
                sync.dma_start(rows[:, n, :, :], k.a[f"L0_attn_{name}"].rearrange("(r p) i -> p r i", p=P)
                               ).then_inc(rows_loaded, 16)
            sync.dma_start(rows[:, 3, :, :], k.a["L0_attn_Wo"].rearrange("o (r p) -> o r p", p=P)
                           ).then_inc(rows_loaded, 16)

        @block.gpsimd
        def _(pool):
            flat = lambda name: k.a[name].rearrange("(o n) -> o n", o=1)
            with nc.allow_non_contiguous_dma(reason="biases: 2 KB"):
                pool.dma_start(w.bq[:, :], flat("L0_attn_bq")).then_inc(small_loaded, 16)
                pool.dma_start(w.bk[:, :], flat("L0_attn_bk")).then_inc(small_loaded, 16)
                for c in range(2):
                    pool.dma_start(rotated(w.bq_rot[:, :])[:, :, c, :], rotated(flat("L0_attn_bq"))[:, :, 1 - c, :]
                                   ).then_inc(small_loaded, 16)
                    pool.dma_start(rotated(w.bk_rot[:, :])[:, :, c, :], rotated(flat("L0_attn_bk"))[:, :, 1 - c, :]
                                   ).then_inc(small_loaded, 16)
                pool.dma_start(bv_col[:, :], k.a["L0_attn_bv"].rearrange("(r p) -> p r", p=P)).then_inc(small_loaded, 16)
                pool.dma_start(bo_col[:, :], k.a["L0_attn_bo"].rearrange("(p o) -> p o", o=1)).then_inc(small_loaded, 16)
                pool.dma_start(w.rope_q[:, :, :], k.a["rope_q"]).then_inc(small_loaded, 16)
                pool.dma_start(w.rope_k[:, :, :], k.a["rope_k"]).then_inc(small_loaded, 16)

        @block.tensor
        def _(pe):
            pe.wait_ge(rows_loaded, 64)
            pe.wait_ge(eye_ready, 2)
            for n in range(4):
                for r in range(NR):
                    last = nc.tensor.transpose(half_bank[n][:, r * P:(r + 1) * P], rows[:, n, r, :], eye[:, :])
                last.then_inc(turned, 1)
            pe.wait_ge(kept, 6)
            pe.wait_ge(bias_ready, 2)
            for r in range(NR):
                last = nc.tensor.matmul(k.bank[4][:, 0:1], w.o[:, r, :], bv[:, r:r + 1], start=(r == 0),
                                        stop=(r == NR - 1))
            last.then_inc(wobv_ready, 1)

        @block.vector
        def _(dve):
            dve.memset(w.ones[:, :], 1.0).then_inc(eye_ready, 1)
            dve.tensor_copy(eye[:, :], k.eye[:, :]).then_inc(eye_ready, 1)
            for c in range(2):
                cols = slice(c * N // 2, (c + 1) * N // 2)
                for part in range(3):
                    src = k.X[:, cols] if part == 0 else left[:, part - 1, :]
                    if part:
                        dve.wait_ge(part_ready, 5 * c + 2 * part)
                    dve.tensor_copy(w.parts[:, part, cols], src).then_inc(part_ready, 1)
                    if part < 2:
                        dve.wait_ge(part_ready, 5 * c + 2 * part + 1)
                        dve.tensor_tensor(left[:, part, :], src, w.parts[:, part, cols], ALU.subtract
                                          ).then_inc(part_ready, 1)
            for n, (plain, rot) in enumerate(((w.q, w.q_rot), (w.k, w.k_rot), (w.v, None), (w.o, None))):
                dve.wait_ge(turned, n + 1)
                dst = plain[:, :] if n < 3 else plain[:, :, :].rearrange("p r o -> p (r o)")
                dve.tensor_copy(dst, half_bank[n][:, 0:AD]).then_inc(kept, 1)
                if rot is not None:
                    for c in range(2):
                        last = dve.tensor_copy(rotated(rot[:, :])[:, :, c, :],
                                               rotated(half_bank[n][:, 0:AD])[:, :, 1 - c, :])
                    last.then_inc(kept, 1)
            dve.wait_ge(small_loaded, 16 * 10)
            dve.tensor_copy(bv[:, :], bv_col[:, :]).then_inc(bias_ready, 1)
            dve.tensor_copy(bo[:, :], bo_col[:, :]).then_inc(bias_ready, 1)
            dve.wait_ge(bias_ready, 2)
            dve.wait_ge(wobv_ready, 1)
            dve.tensor_tensor(w.o_bias[:, :], k.bank[4][:, 0:1], bo[:, :], ALU.add).then_inc(small_ready, 1)
    return w


AH, AK = 16, 64
HP = AH * AK // P


def rope_attention(k):
    nc = k.nc
    with Stage(k, "attn") as s:
        w = attention_weights(k, s)
        HG = HP // 2
        qk = [s.sb(n, [P, HP, TT]) for n in ("q", "k")]
        by_cos = [s.sb(f"by_cos{r}", [P, G]) for r in range(2)]
        by_sin = [s.sb(f"by_sin{r}", [P, G]) for r in range(2)]
        v = [s.sb(f"v{u}", [P, AH * AK]) for u in range(2)]
        shifted, expd, probs = (s.sb(n, [P, HP, TT]) for n in ("shifted", "exp", "probs"))
        probsT = s.sb("probsT", [P, HP, TT])
        heads = s.sb("heads", [P, 2, HP, T])
        top, total, inv = (s.sb(n, [P, AH]) for n in ("row_max", "row_sum", "row_inv"))
        (projected, turned, roped, v_kept, scored, maxed, shift_ready, exp_ready, summed, inv_ready, probs_ready,
         probs_turned, probsT_ready, attended, heads_ready, out_ready, added) = s.sems(
            "projected", "cos_sin_ready", "roped", "v_kept", "scored", "maxed", "shift_ready", "exp_ready", "summed",
            "inv_ready", "probs_ready", "probs_turned", "probsT_ready", "attended", "heads_ready", "out_ready", "added")
        block = s.block()
        PROJ = 5
        S_BANK = k.psum[:, 4:6, :].rearrange("p b c -> p (b c)")
        O_BANK = k.psum[:, 6:8, :]
        Y_BANK = k.bank[3][:, 0:TT]
        KINDS = [(w.q, w.q_rot, w.bq, w.bq_rot), (w.k, w.k_rot, w.bk, w.bk_rot)]

        def pe_project(pe, t):
            for st in range(4):
                if st >= 2:
                    pe.wait_ge(turned, t * 4 + (st - 1))
                elif st == 1 and (not isinstance(t, int) or t > 1):
                    pe.wait_ge(added, t)
                elif st == 0 and not isinstance(t, int):
                    pe.wait_ge(v_kept, t)
                c0 = (st // 2) * HG
                for wt, bias, bank in zip(KINDS[st % 2][0:2], KINDS[st % 2][2:4], (2 * (st % 2), 2 * (st % 2) + 1)):
                    for c in range(HG):
                        out = k.bank[bank][:, c * TT:(c + 1) * TT]
                        cols = slice((c0 + c) * P, (c0 + c + 1) * P)
                        for part in range(3):
                            nc.tensor.matmul(out, wt[:, cols], w.parts[:, part, ds(t * TT, TT)],
                                             start=(part == 0), stop=False)
                        last = nc.tensor.matmul(out, bias[:, cols], w.ones[:, :], start=False, stop=True)
                last.then_inc(projected, 1)
            pe.wait_ge(turned, t * 4 + 3)
            for half in range(2):
                for part in range(3):
                    last = nc.tensor.matmul(k.bank[half][:, :], w.parts[:, part, ds(t * TT, TT)],
                                            w.v[:, half * G:(half + 1) * G], start=(part == 0), stop=(part == 2))
            last.then_inc(projected, 1)

        def pe_scores(pe, t):
            for hp in range(HP):
                for b in range(2):
                    for j in range(2):
                        r, cols = slice(j * AK, (j + 1) * AK), slice(b * T, (b + 1) * T)
                        last = nc.tensor.matmul(S_BANK[r, hp * TT + b * T:hp * TT + (b + 1) * T],
                                                qk[0][r, hp, cols], qk[1][r, hp, cols], start=True, stop=True)
            last.then_inc(scored, 1)

        def pe_values(pe, t, u, more):
            pe.wait_ge(probs_ready, t + 1)
            for hp in range(HP):
                last = nc.tensor.transpose(S_BANK[:, hp * TT:(hp + 1) * TT], probs[:, hp, :], k.eye[:, :])
            last.then_inc(probs_turned, 1)
            k.hold(pe)
            pe.wait_ge(probsT_ready, t + 1)
            pe.wait_ge(v_kept, t + 1)
            for hp in range(HP):
                for j in range(2):
                    for b in range(2):
                        r, h = slice(b * T, (b + 1) * T), 2 * hp + j
                        last = nc.tensor.matmul(O_BANK[j * AK:(j + 1) * AK, b, hp * T:(hp + 1) * T],
                                                v[u][r, h * AK:(h + 1) * AK], probsT[r, hp, j * T:(j + 1) * T],
                                                start=True, stop=True)
            last.then_inc(attended, 1)
            pe.wait_ge(heads_ready, t + 1)
            if more:
                pe.wait_ge(roped, t * 4 + 8)
            for hp in range(HP):
                last = nc.tensor.matmul(Y_BANK, w.o[:, hp, :], heads[:, :, hp, :], start=(hp == 0),
                                        stop=(hp == HP - 1))
            last.then_inc(out_ready, 1)

        def dve_rope(dve, t, st):
            dve.wait_ge(projected, t * PROJ + (st + 1))
            if not isinstance(t, int) or st >= 2:
                dve.wait_ge(roped, t * 4 + (st - 1))
            tab, r = (w.rope_q, w.rope_k)[st % 2], st % 2
            for part, dst in enumerate((by_cos[r], by_sin[r])):
                last = dve.tensor_tensor(dst[:, :].rearrange("p (n t) -> p n t", t=T),
                                         k.bank[2 * r + part][:, :].rearrange("p (n t) -> p n t", t=T),
                                         tab[:, part:part + 1, :].to_broadcast([P, 2 * HG, T]), ALU.mult)
            last.then_inc(turned, 1)

        def rows_of(ap):
            return ap.rearrange("p h (b t) -> p (h b) t", b=2)

        def dve_shift(dve, t):
            dve.wait_ge(scored, t + 1)
            sc = S_BANK.rearrange("p (h t) -> p h t", t=T)
            dve.tensor_reduce(top[:, :], sc, AX_X, ALU.max).then_inc(maxed, 1)
            dve.wait_ge(maxed, t + 1)
            dve.tensor_tensor(rows_of(shifted[:, :, :]), sc, top[:, :].unsqueeze(2).to_broadcast([P, AH, T]),
                              ALU.subtract).then_inc(shift_ready, 1)

        def dve_sum(dve, t):
            dve.wait_ge(exp_ready, t + 1)
            dve.tensor_reduce(total[:, :], rows_of(expd[:, :, :]), AX_X, ALU.add).then_inc(summed, 1)
            dve.wait_ge(summed, t + 1)
            dve.reciprocal(inv[:, :], total[:, :]).then_inc(inv_ready, 1)

        def dve_add(dve, t):
            dve.wait_ge(out_ready, t + 1)
            x = k.X[:, ds(t * TT, TT)]
            dve.scalar_tensor_tensor(x, Y_BANK, w.o_bias[:, :], x, ALU.add, ALU.add).then_inc(added, 1)

        def pool_rope(pool, t, st):
            pool.wait_ge(turned, t * 4 + (st + 1))
            if not isinstance(t, int):
                pool.wait_ge(scored, t)
            c0 = (st // 2) * HG
            pool.tensor_tensor(qk[st % 2][:, c0:c0 + HG, :].rearrange("p h t -> p (h t)"), by_cos[st % 2][:, :],
                               by_sin[st % 2][:, :], ALU.add).then_inc(roped, 1)

        def pool_norm(pool, t):
            pool.wait_ge(inv_ready, t + 1)
            pool.tensor_tensor(rows_of(probs[:, :, :]), rows_of(expd[:, :, :]),
                               inv[:, :].unsqueeze(2).to_broadcast([P, AH, T]), ALU.mult).then_inc(probs_ready, 1)

        def act_v(act, t, u):
            act.wait_ge(projected, t * PROJ + PROJ)
            act.activation(v[u][:, :], k.psum[:, 0:2, :].rearrange("p b c -> p (b c)"), ACT.Copy).then_inc(v_kept, 1)

        def act_exp(act, t):
            act.wait_ge(shift_ready, t + 1)
            act.activation(expd[:, :, :], shifted[:, :, :], ACT.Exp).then_inc(exp_ready, 1)

        def act_values(act, t):
            act.wait_ge(probs_turned, t + 1)
            act.activation(probsT[:, :, :].rearrange("p h t -> p (h t)"), S_BANK, ACT.Copy).then_inc(probsT_ready, 1)
            act.wait_ge(attended, t + 1)
            act.activation(heads[:, :, :, :].rearrange("p b h t -> p b (h t)"), O_BANK, ACT.Copy
                           ).then_inc(heads_ready, 1)

        def tiles(eng, body):
            with eng.Fori(0, NT // 2 - 1) as i:
                for u in range(2):
                    body(i * 2 + u, u, True)
            body(NT - 2, 0, True)
            body(NT - 1, 1, False)

        @block.tensor
        def _(pe):
            pe_project(pe, 0)
            pe.wait_ge(roped, 4)

            def body(t, u, more):
                pe_scores(pe, t)
                if more:
                    pe_project(pe, t + 1)
                pe_values(pe, t, u, more)
            tiles(pe, body)

        @block.vector
        def _(dve):
            dve.memset(top[:, :], 0.0).then_inc(added, 1)
            for st in range(4):
                dve_rope(dve, 0, st)

            def body(t, u, more):
                dve_shift(dve, t)
                for st in range(4):
                    if st == 2:
                        dve_sum(dve, t)
                    if more:
                        dve_rope(dve, t + 1, st)
                dve_add(dve, t)
            tiles(dve, body)

        @block.gpsimd
        def _(pool):
            for st in range(4):
                pool_rope(pool, 0, st)

            def body(t, u, more):
                for st in range(4):
                    if st == 2:
                        pool_norm(pool, t)
                    if more:
                        pool_rope(pool, t + 1, st)
            tiles(pool, body)

        @block.scalar
        def _(act):
            act_v(act, 0, 0)

            def body(t, u, more):
                act_exp(act, t)
                if more:
                    act_v(act, t + 1, 1 - u)
                act_values(act, t)
            tiles(act, body)


XH, XK = 16, 8
XG = 4


def turn_square(k, name, loads, out, bank0=0):
    nc = k.nc
    with Stage(k, name) as s:
        rows = s.sb("rows", [P, len(loads), D])
        loaded, turned, kept = s.sems("loaded", "turned", "kept")
        block = s.block()

        @block.sync
        def _(sync):
            for i, w in enumerate(loads):
                sync.dma_start(rows[:, i, :], w).then_inc(loaded, 16)

        @block.tensor
        def _(pe):
            pe.wait_ge(loaded, 16 * len(loads))
            for i in range(len(loads)):
                last = nc.tensor.transpose(k.bank[bank0][:, i * D:(i + 1) * D], rows[:, i, :], k.eye[:, :])
            last.then_inc(turned, 1)

        @block.vector
        def _(dve):
            dve.wait_ge(turned, 1)
            dve.tensor_copy(out.rearrange("p n d -> p (n d)"), k.bank[bank0][:, 0:len(loads) * D]).then_inc(kept, 1)


def column(ap):
    return ap.rearrange("(p o) -> p o", o=1)


def cross_attention(k):
    nc = k.nc
    with Stage(k, "xattn") as s:
        wT = s.sb("wT", [P, 4, D])
        turn_context(k, s, "xattn_ctx")
        turn_square(k, "xattn_w", [k.a[f"L0_xattn_{n}_w"] for n in ("wq", "wk", "wv", "wo")], wT[:, :, :])
        qT, kT = s.sb("qT", [P, N]), s.sb("kT", [P, N])
        v = s.sb("v", [P, NT, D])
        bias = s.sb("bias", [P, 4])
        bq, o_bias, head_mask = s.sb("bq_scaled", [P, 1]), s.sb("o_bias", [P, 1]), s.sb("head_mask", [P, 4])
        scale = float(XK) ** -0.5
        with Stage(k, "xproj") as t:
            ctx_g = [t.sb(f"ctx{u}", [P, G]) for u in range(2)]
            bias_loaded, masked, staged, projected, kept, small_ready, wobv_ready, scaled_ready, ob_ready = t.sems(
                "bias_loaded", "masked", "ctx_staged", "projected", "kept", "small_ready", "wobv_ready", "scaled_ready",
                "o_bias_ready")
            block = t.block()

            @block.sync
            def _(sync):
                with nc.allow_non_contiguous_dma(reason="four columns of biases"):
                    for i, n in enumerate(("wq", "wk", "wv", "wo")):
                        sync.dma_start(bias[:, i:i + 1], column(k.a[f"L0_xattn_{n}_b"])).then_inc(bias_loaded, 16)

            @block.gpsimd
            def _(pool):
                pool.memset(head_mask[:, :], 1.0).then_inc(masked, 1)
                for g in range(XG):
                    m = head_mask[32 * g:32 * g + 32, :]
                    pool.wait_ge(masked, 2 * g + 1)
                    pool.affine_select(out=m, in_=m, compare_op=ALU.is_ge, fill=0.0, base=0,
                                       pattern=[[-XK, 4]], channel_multiplier=1).then_inc(masked, 1)
                    pool.wait_ge(masked, 2 * g + 2)
                    pool.affine_select(out=m, in_=m, compare_op=ALU.is_ge, fill=0.0, base=XK - 1,
                                       pattern=[[XK, 4]], channel_multiplier=-1).then_inc(masked, 1)

            @block.tensor
            def _(pe):
                pe.wait_ge(bias_loaded, 64)
                nc.tensor.matmul(k.bank[6][:, 0:1], wT[:, 3, :], bias[:, 2:3], start=True, stop=True
                                 ).then_inc(wobv_ready, 1)
                with pe.Fori(0, NG // 2) as i:
                    for u in range(2):
                        g_at = ds(i * (2 * G) + u * G, G)
                        nc.tensor.matmul(k.bank[3 * u][:, :], wT[:, 0, :], k.X[:, g_at], start=True, stop=True)
                        nc.tensor.matmul(k.bank[3 * u + 1][:, :], wT[:, 1, :], k.ctxT[:, g_at], start=True, stop=True)
                        pe.wait_ge(staged, i * 2 + (u + 1))
                        for n in range(4):
                            last = nc.tensor.matmul(k.bank[3 * u + 2][:, n * D:(n + 1) * D],
                                                    ctx_g[u][:, n * D:(n + 1) * D], wT[:, 2, :], start=True, stop=True)
                        last.then_inc(projected, 1)
                    pe.wait_ge(kept, i * 2 + 2)
                    pe.wait_ge(small_ready, i * 2 + 2)

            @block.vector
            def _(dve):
                dve.wait_ge(bias_loaded, 64)
                dve.tensor_scalar(bq[:, :], bias[:, 0:1], scale, None, ALU.mult).then_inc(scaled_ready, 1)
                dve.wait_ge(wobv_ready, 1)
                dve.tensor_tensor(o_bias[:, :], k.bank[6][:, 0:1], bias[:, 3:4], ALU.add).then_inc(ob_ready, 1)
                with dve.Fori(0, NG // 2) as i:
                    for u in range(2):
                        dve.tensor_copy(ctx_g[u][:, :], k.ctxT[:, ds(i * (2 * G) + u * G, G)]).then_inc(staged, 1)
                    for u in range(2):
                        dve.wait_ge(projected, i * 2 + (u + 1))
                        dve.tensor_copy(v[:, ds(i * 8 + u * 4, 4), :].rearrange("p n d -> p (n d)"),
                                        k.bank[3 * u + 2][:, :]).then_inc(kept, 1)

            @block.scalar
            def _(act):
                act.wait_ge(scaled_ready, 1)
                with act.Fori(0, NG // 2) as i:
                    for u in range(2):
                        g_at = ds(i * (2 * G) + u * G, G)
                        act.wait_ge(projected, i * 2 + (u + 1))
                        act.activation(qT[:, g_at], k.bank[3 * u][:, :], ACT.Identity, scale=scale, bias=bq[:, :])
                        act.activation(kT[:, g_at], k.bank[3 * u + 1][:, :], ACT.Identity, bias=bias[:, 1:2]
                                       ).then_inc(small_ready, 1)

        q_t = [s.sb(f"q{u}", [P, TT]) for u in range(2)]
        v_t = [s.sb(f"v{u}", [P, D]) for u in range(2)]
        kx = [s.sb(f"kx{u}", [P, 4, TT]) for u in range(2)]
        W = 4 * TT // 2
        shifted, expd, probs, probsT = (s.sb(n, [P, XG, W]) for n in ("shifted", "exp", "probs", "probsT"))
        top, total, inv = (s.sb(n, [P, XG * 4]) for n in ("row_max", "row_sum", "row_inv"))
        mixed, mixedT = s.sb("mixed", [P, D]), s.sb("mixedT", [P, TT])
        (qv_staged, kx_ready, scored, maxed, shift_ready, exp_ready, summed, inv_ready, probs_ready, probs_turned,
         probsT_ready, mixed_ready, mixed_kept, mixed_turned, mixedT_ready, out_ready, added) = s.sems(
            "qv_staged", "kx_ready", "scored", "maxed", "shift_ready", "exp_ready", "summed", "inv_ready", "probs_ready",
            "probs_turned", "probsT_ready", "mixed_ready", "mixed_kept", "mixed_turned", "mixedT_ready", "out_ready",
            "added")
        block = s.block()
        S_BANK = k.psum[:, 0:4, 0:W]
        PT_BANK = k.psum[:, 4:6, :].rearrange("p b c -> p (b c)")

        def pe_scores(pe, t, u):
            k.hold(pe)
            pe.wait_ge(qv_staged, t + 1)
            pe.wait_ge(kx_ready, t + 1)
            for b in range(2):
                for h2 in range(2):
                    for j in range(2):
                        for g in range(XG):
                            r = slice(32 * g, 32 * g + 32)
                            last = nc.tensor.matmul(k.psum[j * T:(j + 1) * T, g, h2 * TT + b * T:h2 * TT + (b + 1) * T],
                                                    q_t[u][r, b * T:(b + 1) * T], kx[u][r, 2 * h2 + j, b * T:(b + 1) * T],
                                                    start=True, stop=True)
            last.then_inc(scored, 1)

        def pe_turn(pe, t):
            pe.wait_ge(probs_ready, t + 1)
            for g in range(XG):
                for h2 in range(2):
                    last = nc.tensor.transpose(PT_BANK[:, (2 * g + h2) * TT:(2 * g + h2 + 1) * TT],
                                               probs[:, g, h2 * TT:(h2 + 1) * TT], k.eye[:, :])
            last.then_inc(probs_turned, 1)

        def pe_values(pe, t, u):
            k.hold(pe)
            pe.wait_ge(probsT_ready, t + 1)
            for g in range(XG):
                for h2 in range(2):
                    for j in range(2):
                        for b in range(2):
                            r, h = slice(b * T, (b + 1) * T), 4 * g + 2 * h2 + j
                            last = nc.tensor.matmul(k.bank[6][r, h * XK:(h + 1) * XK],
                                                    probsT[r, g, h2 * TT + j * T:h2 * TT + (j + 1) * T],
                                                    v_t[u][r, h * XK:(h + 1) * XK], start=True, stop=True)
            last.then_inc(mixed_ready, 1)
            pe.wait_ge(mixed_kept, t + 1)
            nc.tensor.transpose(k.bank[7][:, 0:TT], mixed[:, :], k.eye[:, :]).then_inc(mixed_turned, 1)
            pe.wait_ge(mixedT_ready, t + 1)
            nc.tensor.matmul(k.bank[7][:, TT:2 * TT], wT[:, 3, :], mixedT[:, :], start=True, stop=True
                             ).then_inc(out_ready, 1)

        def dve_spread(dve, t, u):
            dve.tensor_tensor(kx[u][:, :, :], kT[:, ds(t * TT, TT)].unsqueeze(1).to_broadcast([P, 4, TT]),
                              head_mask[:, :].unsqueeze(2).to_broadcast([P, 4, TT]), ALU.mult).then_inc(kx_ready, 1)

        def dve_shift(dve, t):
            dve.wait_ge(scored, t + 1)
            sc = S_BANK.rearrange("p g (h k) -> p g h k", k=T)
            dve.tensor_reduce(top[:, :].rearrange("p (g h) -> p g h", g=XG), sc, AX_X, ALU.max).then_inc(maxed, 1)
            dve.wait_ge(maxed, t + 1)
            dve.tensor_tensor(shifted[:, :, :].rearrange("p g (h k) -> p g h k", k=T), sc,
                              top[:, :].rearrange("p (g h) -> p g h", g=XG).unsqueeze(3).to_broadcast([P, XG, 4, T]),
                              ALU.subtract).then_inc(shift_ready, 1)

        def rows_of(ap):
            return ap.rearrange("p g (h k) -> p (g h) k", k=T)

        def dve_sum(dve, t):
            dve.wait_ge(exp_ready, t + 1)
            dve.tensor_reduce(total[:, :], rows_of(expd[:, :, :]), AX_X, ALU.add).then_inc(summed, 1)
            dve.wait_ge(summed, t + 1)
            dve.reciprocal(inv[:, :], total[:, :]).then_inc(inv_ready, 1)

        def dve_add(dve, t):
            dve.wait_ge(out_ready, t + 1)
            x = k.X[:, ds(t * TT, TT)]
            dve.scalar_tensor_tensor(x, k.bank[7][:, TT:2 * TT], o_bias[:, :], x, ALU.add, ALU.add).then_inc(added, 1)

        def act_stage(act, t, u):
            act.activation(q_t[u][:, :], qT[:, ds(t * TT, TT)], ACT.Copy)
            act.activation(v_t[u][:, :], v[:, ds(t, 1), :], ACT.Copy).then_inc(qv_staged, 1)

        def tiles(eng, body):
            with eng.Fori(0, NT // 2 - 1) as i:
                for u in range(2):
                    body(i * 2 + u, u, True)
            body(NT - 2, 0, True)
            body(NT - 1, 1, False)

        @block.tensor
        def _(pe):
            pe_scores(pe, 0, 0)

            def body(t, u, more):
                pe_turn(pe, t)
                if more:
                    pe_scores(pe, t + 1, 1 - u)
                pe_values(pe, t, u)
            tiles(pe, body)

        @block.vector
        def _(dve):
            dve_spread(dve, 0, 0)
            dve_shift(dve, 0)

            def body(t, u, more):
                if more:
                    dve_spread(dve, t + 1, 1 - u)
                dve_sum(dve, t)
                if more:
                    dve_shift(dve, t + 1)
                dve_add(dve, t)
            tiles(dve, body)

        @block.gpsimd
        def _(pool):
            def body(t, u, more):
                pool.wait_ge(inv_ready, t + 1)
                pool.tensor_tensor(rows_of(probs[:, :, :]), rows_of(expd[:, :, :]),
                                   inv[:, :].unsqueeze(2).to_broadcast([P, XG * 4, T]), ALU.mult
                                   ).then_inc(probs_ready, 1)
            tiles(pool, body)

        @block.scalar
        def _(act):
            act_stage(act, 0, 0)

            def body(t, u, more):
                act.wait_ge(shift_ready, t + 1)
                act.activation(expd[:, :, :], shifted[:, :, :], ACT.Exp).then_inc(exp_ready, 1)
                if more:
                    act_stage(act, t + 1, 1 - u)
                act.wait_ge(probs_turned, t + 1)
                act.activation(probsT[:, :, :].rearrange("p g c -> p (g c)"), PT_BANK, ACT.Copy
                               ).then_inc(probsT_ready, 1)
                act.wait_ge(mixed_ready, t + 1)
                act.activation(mixed[:, :], k.bank[6][:, 0:D], ACT.Copy).then_inc(mixed_kept, 1)
                act.wait_ge(mixed_turned, t + 1)
                act.activation(mixedT[:, :], k.bank[7][:, 0:TT], ACT.Copy).then_inc(mixedT_ready, 1)
            tiles(act, body)


ME, MS, MH = 16, 16, 32
SLOTS = ME * MS
MG = 4
UNIT_SHIFT = 30


def mixture_inputs(k, s):
    nc = k.nc
    f = Core()
    f.xn, f.xs = s.sb("xn", [P, N]), s.sb("xs", [P, N])
    f.mu = s.sb("mu_unit", [P, SLOTS])
    with Stage(k, "mixin") as t:
        cols = t.sb("cols", [P, 3])
        mu, mu_n2 = t.sb("mu", [P, SLOTS]), t.sb("mu_n2", [P, SLOTS])
        unit_bias = t.sb("unit_bias", [P, 1])
        sq, n2, log, inv, xc = ([t.sb(f"{n}{u}", [P, G]) for u in range(2)] for n in ("sq", "n2", "log", "inv", "xc"))
        (cols_loaded, mu_loaded, const_ready, mean_ready, centred, squared, var_ready, log_ready, rstd_ready, scaled,
         xn_ready, sq2_ready, n2_ready, n2_kept, log2_ready, inv_ready, xs_ready) = t.sems(
            "cols_loaded", "mu_loaded", "const_ready", "mean_ready", "centred", "squared", "var_ready", "log_ready",
            "rstd_ready", "scaled", "xn_ready", "sq2_ready", "n2_ready", "n2_kept", "log2_ready", "inv_ready", "xs_ready")
        block = t.block()
        mean, var, norm = k.bank[0:2], k.bank[2:4], k.bank[4:6]

        @block.sync
        def _(sync):
            with nc.allow_non_contiguous_dma(reason="three columns"):
                sync.dma_start(cols[:, 0:1], column(k.a["L0_ffn_ln_gamma"])).then_inc(cols_loaded, 16)
                sync.dma_start(cols[:, 1:2], column(k.a["L0_ffn_ln_beta"])).then_inc(cols_loaded, 16)
                sync.dma_start(cols[:, 2:3], k.a["L0_ffn_scale"].partition_broadcast(P)).then_inc(cols_loaded, 16)
            sync.dma_start(mu[:, :], k.a["L0_ffn_mu"].rearrange("d e s -> d (e s)")).then_inc(mu_loaded, 16)

        @block.tensor
        def _(pe):
            pe.wait_ge(sq2_ready, 1)
            nc.tensor.matmul(norm[1][:, 0:SLOTS], k.ones_mean[:, :], sq[1][:, 0:SLOTS], start=True, stop=True
                             ).then_inc(n2_ready, 1)
            with pe.Fori(0, NG // 2) as i:
                for u in range(2):
                    nc.tensor.matmul(mean[u][:, :], k.ones_mean[:, :], k.X[:, ds(i * (2 * G) + u * G, G)],
                                     start=True, stop=True).then_inc(mean_ready, 1)
                for u in range(2):
                    pe.wait_ge(squared, i * 2 + (u + 1))
                    nc.tensor.matmul(var[u][:, :], k.ones_mean[:, :], sq[u][:, :],
                                     start=True, stop=True).then_inc(var_ready, 1)
                for u in range(2):
                    pe.wait_ge(sq2_ready, i * 2 + (u + 2))
                    nc.tensor.matmul(norm[u][:, :], k.ones_mean[:, :], sq[u][:, :],
                                     start=True, stop=True).then_inc(n2_ready, 1)

        @block.vector
        def _(dve):
            dve.memset(unit_bias[:, :], 0.5 * UNIT_SHIFT * float(np.log(2.0))).then_inc(const_ready, 1)
            dve.wait_ge(n2_ready, 1)
            dve.tensor_scalar(n2[1][:, 0:SLOTS], norm[1][:, 0:SLOTS], float(D), 1e-24, ALU.mult, ALU.max
                              ).then_inc(n2_kept, 1)
            dve.wait_ge(inv_ready, 1)
            dve.tensor_tensor(f.mu[:, :], mu[:, :], inv[1][:, 0:SLOTS], ALU.mult).then_inc(xs_ready, 1)
            dve.wait_ge(cols_loaded, 48)
            with dve.Fori(0, NG // 2) as i:
                for u in range(2):
                    dve.wait_ge(mean_ready, i * 2 + (u + 1))
                    dve.tensor_tensor(xc[u][:, :], k.X[:, ds(i * (2 * G) + u * G, G)], mean[u][:, :], ALU.subtract
                                      ).then_inc(centred, 1)
                for u in range(2):
                    dve.wait_ge(rstd_ready, i * 2 + (u + 1))
                    xn = f.xn[:, ds(i * (2 * G) + u * G, G)]
                    dve.tensor_tensor(xn, xc[u][:, :], inv[u][:, :], ALU.mult).then_inc(scaled, 1)
                    dve.wait_ge(scaled, i * 2 + (u + 1))
                    dve.tensor_scalar(xn, xn, cols[:, 0:1], cols[:, 1:2], ALU.mult, ALU.add).then_inc(xn_ready, 1)
                for u in range(2):
                    dve.wait_ge(n2_ready, i * 2 + (u + 2))
                    dve.tensor_scalar(n2[u][:, :], norm[u][:, :], float(D), 1e-24, ALU.mult, ALU.max
                                      ).then_inc(n2_kept, 1)
                for u in range(2):
                    dve.wait_ge(inv_ready, i * 2 + (u + 2))
                    g_at = ds(i * (2 * G) + u * G, G)
                    dve.scalar_tensor_tensor(f.xs[:, g_at], f.xn[:, g_at], cols[:, 2:3], inv[u][:, :], ALU.mult,
                                             ALU.mult).then_inc(xs_ready, 1)

        @block.scalar
        def _(act):
            act.preload_act_table_set(LOG_EXP)
            act.wait_ge(mu_loaded, 16)
            act.activation(sq[1][:, 0:SLOTS], mu[:, :], ACT.Square).then_inc(sq2_ready, 1)
            act.wait_ge(const_ready, 1)

            def inverse_norm(u, cols, step):
                act.wait_ge(n2_kept, step)
                act.activation(log[u][:, 0:cols], n2[u][:, 0:cols], ACT.Ln, scale=2.0 ** UNIT_SHIFT
                               ).then_inc(log2_ready, 1)
                act.wait_ge(log2_ready, step)
                act.activation(inv[u][:, 0:cols], log[u][:, 0:cols], ACT.Exp, scale=-0.5, bias=unit_bias[:, :]
                               ).then_inc(inv_ready, 1)
            inverse_norm(1, SLOTS, 1)
            act.wait_ge(xs_ready, 1)
            with act.Fori(0, NG // 2) as i:
                for u in range(2):
                    act.wait_ge(centred, i * 2 + (u + 1))
                    act.activation(sq[u][:, :], xc[u][:, :], ACT.Square).then_inc(squared, 1)
                for u in range(2):
                    act.wait_ge(var_ready, i * 2 + (u + 1))
                    act.activation(log[u][:, :], var[u][:, :], ACT.Ln, bias=k.ln_eps[:, :]).then_inc(log_ready, 1)
                    act.wait_ge(log_ready, i * 2 + (u + 1))
                    act.activation(inv[u][:, :], log[u][:, :], ACT.Exp, scale=-0.5).then_inc(rstd_ready, 1)
                for u in range(2):
                    act.wait_ge(xn_ready, i * 2 + (u + 1))
                    act.activation(sq[u][:, :], f.xn[:, ds(i * (2 * G) + u * G, G)], ACT.Square
                                   ).then_inc(sq2_ready, 1)
                for u in range(2):
                    inverse_norm(u, G, i * 2 + (u + 2))
    return f


def soft_mixture(k):
    nc = k.nc
    with Stage(k, "moe") as s:
        slot_in = s.sb("slot_in", [P, B, SLOTS])
        combine = s.sb("combine", [P, 2, N])
        w1, w2 = s.sb("w1", [P, ME, MH]), s.sb("w2", [P, MG, D])
        b1, b2 = s.sb("b1", [P, MG]), s.sb("b2", [P, 2, D])
        own = s.sb("own_expert", [P, 4])
        (w_loaded,) = s.sems("w_loaded")
        with Stage(k, "route") as r:
            f = mixture_inputs(k, r)
            xs, xn = ([r.sb(f"{n}{u}", [P, TT]) for u in range(2)] for n in ("xs", "xn"))
            xr = r.sb("x_rows", [P, D])
            e1, p1 = r.sb("e1", [P, SLOTS]), r.sb("p1", [P, SLOTS])
            sh2, e2, p2, p2T = (r.sb(n, [P, 2 * TT]) for n in ("sh2", "e2", "p2", "p2T"))
            ntop1, sum1, inv1 = (r.sb(n, [P, 1]) for n in ("ntop1", "sum1", "inv1"))
            top2, sum2, inv2 = (r.sb(n, [P, 4]) for n in ("top2", "sum2", "inv2"))
            (staged, routed, xr_ready, ntop1_ready, e1_ready, inv1_ready, p1_ready, top2_ready, sh2_ready, e2_ready,
             sum2_ready, inv2_ready, p2_ready, p_turned, combine_ready, p2T_ready, slots_ready, slots_kept) = r.sems(
                "staged", "routed", "xr_ready", "ntop1_ready", "e1_ready", "inv1_ready", "p1_ready", "top2_ready",
                "sh2_ready", "e2_ready", "sum2_ready", "inv2_ready", "p2_ready", "p_turned", "combine_ready", "p2T_ready",
                "slots_ready", "slots_kept")
            block = r.block()
            row_bank, l1_bank, l2_bank = k.bank[0][:, 0:D], k.bank[1][:, 0:SLOTS], k.bank[2][:, 0:2 * TT]
            c_bank, d_bank = k.bank[3][:, 0:2 * TT], k.bank[4][:, 0:SLOTS]

            @block.sync
            def _(sync):
                a = k.a
                with nc.allow_non_contiguous_dma(reason="128-byte rows"):
                    sync.dma_start(w1[:, :, :], a["L0_ffn_w1"].rearrange("e d h -> d e h")).then_inc(w_loaded, 16)
                    sync.dma_start(b1[:, :], a["L0_ffn_b1"].rearrange("(g e) h -> (e h) g", e=4)
                                   ).then_inc(w_loaded, 16)
                for g in range(MG):
                    sync.dma_start(w2[:, g, :], a["L0_ffn_w2"][4 * g:4 * g + 4, :, :].rearrange("e h d -> (e h) d")
                                   ).then_inc(w_loaded, 16)
                for e in range(ME):
                    sync.dma_start(b2[MS * (e % 8):MS * (e % 8 + 1), e // 8, :],
                                   a["L0_ffn_b2"][e, :].partition_broadcast(MS)).then_inc(w_loaded, 16)

            def pe_route(pe, t, u):
                pe.wait_ge(staged, t + 1)
                if not isinstance(t, int) or t > 0:
                    pe.wait_ge(xr_ready, t)
                    pe.wait_ge(e1_ready, t)
                    pe.wait_ge(sh2_ready, t)
                nc.tensor.transpose(row_bank, xn[u][:, :], k.eye[:, :])
                nc.tensor.matmul(l1_bank, xs[u][:, :], f.mu[:, :], start=True, stop=True)
                for h in range(2):
                    last = nc.tensor.matmul(l2_bank[:, h * TT:(h + 1) * TT], f.mu[:, h * P:(h + 1) * P], xs[u][:, :],
                                            start=True, stop=True)
                last.then_inc(routed, 1)

            def pe_dispatch(pe, t):
                pe.wait_ge(p1_ready, t + 1)
                pe.wait_ge(p2_ready, t + 1)
                for h in range(2):
                    nc.tensor.transpose(c_bank[:, h * TT:(h + 1) * TT], p1[:, h * P:(h + 1) * P], k.eye[:, :])
                for h in range(2):
                    last = nc.tensor.transpose(d_bank[:, h * P:(h + 1) * P], p2[:, h * TT:(h + 1) * TT], k.eye[:, :])
                last.then_inc(p_turned, 1)

            def pe_slots(pe, t):
                pe.wait_ge(p2T_ready, t + 1)
                for b in range(2):
                    rows = slice(b * T, (b + 1) * T)
                    last = nc.tensor.matmul(k.bank[5 + b][:, 0:SLOTS], xr[rows, :], p2T[rows, :], start=True, stop=True)
                last.then_inc(slots_ready, 1)

            def dve_stage(dve, t, u):
                dve.tensor_copy(xn[u][:, :], f.xn[:, ds(t * TT, TT)])
                dve.tensor_copy(xs[u][:, :], f.xs[:, ds(t * TT, TT)]).then_inc(staged, 1)

            def dve_shift(dve, t):
                dve.wait_ge(routed, t + 1)
                dve.tensor_reduce(ntop1[:, :], l1_bank, AX_X, ALU.max, negate=True).then_inc(ntop1_ready, 1)
                l2 = l2_bank.rearrange("p (h t) -> p h t", t=T)
                dve.tensor_reduce(top2[:, :], l2, AX_X, ALU.max).then_inc(top2_ready, 1)
                dve.wait_ge(top2_ready, t + 1)
                dve.tensor_tensor(sh2[:, :].rearrange("p (h t) -> p h t", t=T), l2,
                                  top2[:, :].unsqueeze(2).to_broadcast([P, 4, T]), ALU.subtract).then_inc(sh2_ready, 1)

            def dve_scale(dve, t):
                dve.wait_ge(e1_ready, t + 1)
                dve.reciprocal(inv1[:, :], sum1[:, :]).then_inc(inv1_ready, 1)
                dve.wait_ge(inv1_ready, t + 1)
                dve.tensor_scalar(p1[:, :], e1[:, :], inv1[:, :], None, ALU.mult).then_inc(p1_ready, 1)
                dve.wait_ge(e2_ready, t + 1)
                dve.tensor_reduce(sum2[:, :], e2[:, :].rearrange("p (h t) -> p h t", t=T), AX_X, ALU.add
                                  ).then_inc(sum2_ready, 1)
                dve.wait_ge(sum2_ready, t + 1)
                dve.reciprocal(inv2[:, :], sum2[:, :]).then_inc(inv2_ready, 1)
                dve.wait_ge(inv2_ready, t + 1)
                dve.tensor_tensor(p2[:, :].rearrange("p (h t) -> p h t", t=T),
                                  e2[:, :].rearrange("p (h t) -> p h t", t=T),
                                  inv2[:, :].unsqueeze(2).to_broadcast([P, 4, T]), ALU.mult).then_inc(p2_ready, 1)

            def dve_keep(dve, t):
                dve.wait_ge(slots_ready, t + 1)
                dve.tensor_copy(slot_in[:, ds(t * 2, 2), :], k.psum[:, 5:7, 0:SLOTS]).then_inc(slots_kept, 1)

            def tiles(eng, body):
                with eng.Fori(0, NT // 2 - 1) as i:
                    for u in range(2):
                        body(i * 2 + u, u, True)
                body(NT - 2, 0, True)
                body(NT - 1, 1, False)

            @block.tensor
            def _(pe):
                pe_route(pe, 0, 0)

                def body(t, u, more):
                    pe_dispatch(pe, t)
                    if more:
                        pe_route(pe, t + 1, 1 - u)
                    pe_slots(pe, t)
                tiles(pe, body)

            @block.vector
            def _(dve):
                dve_stage(dve, 0, 0)
                dve_shift(dve, 0)

                def body(t, u, more):
                    dve_scale(dve, t)
                    if more:
                        dve_stage(dve, t + 1, 1 - u)
                        dve_shift(dve, t + 1)
                    dve_keep(dve, t)
                tiles(dve, body)

            @block.scalar
            def _(act):
                def front(t):
                    act.wait_ge(routed, t + 1)
                    if not isinstance(t, int) or t > 0:
                        act.wait_ge(slots_ready, t)
                    act.activation(xr[:, :], row_bank, ACT.Copy).then_inc(xr_ready, 1)
                    act.wait_ge(ntop1_ready, t + 1)
                    act.activation(e1[:, :], l1_bank, ACT.Exp, bias=ntop1[:, :], accum_out=sum1[:, :]
                                   ).then_inc(e1_ready, 1)
                    act.wait_ge(sh2_ready, t + 1)
                    act.activation(e2[:, :], sh2[:, :], ACT.Exp).then_inc(e2_ready, 1)
                front(0)

                def body(t, u, more):
                    act.wait_ge(p_turned, t + 1)
                    act.activation(p2T[:, :], d_bank, ACT.Copy).then_inc(p2T_ready, 1)
                    act.activation(combine[:, :, ds(t * TT, TT)], c_bank.rearrange("p (h t) -> p h t", h=2), ACT.Copy
                                   ).then_inc(combine_ready, 1)
                    if more:
                        front(t + 1)
                tiles(act, body)

        UB = 4
        NU = B // UB
        hid = [s.sb(f"hid{u}", [P, MG, UB, 4, MS]) for u in range(2)]
        slot_out = [s.sb(f"slot_out{u}", [P, UB, 2, D]) for u in range(2)]
        own_ready, h_ready, gelu_ready, masked, o_ready, o_kept, out_ready, added = s.sems(
            "own_ready", "h_ready", "gelu_ready", "masked", "o_ready", "o_kept", "out_ready", "added")
        block = s.block()

        @block.gpsimd
        def _(pool):
            pool.memset(own[:, :], 0.0).then_inc(own_ready, 1)
            pool.wait_ge(own_ready, 1)
            for e in range(4):
                last = pool.memset(own[MH * e:MH * (e + 1), e:e + 1], 1.0)
            last.then_inc(own_ready, 1)

        @block.tensor
        def _(pe):
            pe.wait_ge(w_loaded, 16 * (2 + MG + ME))
            with pe.Fori(0, NU // 2) as i:
                for u in range(2):
                    for g in range(MG):
                        last = nc.tensor.matmul(k.psum[:, 4 * u + g // 2, (g % 2) * 256:(g % 2) * 256 + 256],
                                                w1[:, 4 * g:4 * g + 4, :].rearrange("p e h -> p (e h)"),
                                                slot_in[:, ds(i * (2 * UB) + u * UB, UB), g * 64:(g + 1) * 64],
                                                start=True, stop=True)
                    last.then_inc(h_ready, 1)
                for u in range(2):
                    pe.wait_ge(masked, i * 2 + (u + 1))
                    for b in range(UB):
                        for g in range(MG):
                            last = nc.tensor.matmul(
                                k.psum[(g % 2) * 64:(g % 2) * 64 + 64, 4 * u + 2 + b // 2,
                                       (b % 2) * 256 + (g // 2) * D:(b % 2) * 256 + (g // 2) * D + D],
                                hid[u][:, g, b, :, :].rearrange("p e s -> p (e s)"), w2[:, g, :], start=True, stop=True)
                    last.then_inc(o_ready, 1)
                for u in range(2):
                    pe.wait_ge(o_kept, i * 2 + (u + 1))
                    for b in range(UB):
                        for h in range(2):
                            last = nc.tensor.matmul(k.bank[4 * u][:, b * T:(b + 1) * T], slot_out[u][:, b, h, :],
                                                    combine[:, h, ds(i * (2 * UB * T) + (u * UB + b) * T, T)],
                                                    start=(h == 0), stop=(h == 1))
                    last.then_inc(out_ready, 1)
                pe.wait_ge(added, i * 2 + 2)

        @block.scalar
        def _(act):
            act.preload_act_table(ACT.Gelu)
            act.wait_ge(w_loaded, 16 * (2 + MG + ME))
            with act.Fori(0, NU // 2) as i:
                for u in range(2):
                    act.wait_ge(h_ready, i * 2 + (u + 1))
                    for g in range(MG):
                        last = act.activation(hid[u][:, g, :, :, :].rearrange("p b e s -> p (b e s)"),
                                              k.psum[:, 4 * u + g // 2, (g % 2) * 256:(g % 2) * 256 + 256], ACT.Gelu,
                                              bias=b1[:, g:g + 1])
                    last.then_inc(gelu_ready, 1)

        @block.vector
        def _(dve):
            dve.wait_ge(own_ready, 2)
            dve.wait_ge(w_loaded, 16 * (2 + MG + ME))
            with dve.Fori(0, NU // 2) as i:
                for u in range(2):
                    dve.wait_ge(gelu_ready, i * 2 + (u + 1))
                    h = hid[u][:, :, :, :, :].rearrange("p g b e s -> p (g b) e s")
                    dve.tensor_tensor(h, h, own[:, :].unsqueeze(1).unsqueeze(3).to_broadcast([P, MG * UB, 4, MS]),
                                      ALU.mult).then_inc(masked, 1)
                for u in range(2):
                    dve.wait_ge(o_ready, i * 2 + (u + 1))
                    dve.tensor_tensor(slot_out[u][:, :, :, :].rearrange("p b h d -> p b (h d)"),
                                      k.psum[:, 4 * u + 2:4 * u + 4, :].rearrange("p n (b c) -> p (n b) c", b=2),
                                      b2[:, :, :].rearrange("p h d -> p (h d)").unsqueeze(1).to_broadcast([P, UB, 2 * D]),
                                      ALU.add).then_inc(o_kept, 1)
                for u in range(2):
                    dve.wait_ge(out_ready, i * 2 + (u + 1))
                    x = k.X[:, ds(i * (2 * UB * T) + u * UB * T, UB * T)]
                    dve.tensor_tensor(x, x, k.bank[4 * u][:, 0:UB * T], ALU.add).then_inc(added, 1)


DH, DK = 8, 64
DP = DH * DK // P
HB = 2 * DP
LEVELS = 6
DECAY, THRESHOLD = 0.9, 0.5
NORM_FLOOR = 2.0 ** -62


def delta_inputs(k, s, hT, uT):
    nc = k.nc
    a = k.a
    with Stage(k, "din") as t:
        cols = t.sb("cols", [P, 6])
        bau, w_au = t.sb("bau", [DK, 1]), t.sb("w_au", [P, DK])
        rms_eps = t.sb("rms_eps", [P, 1])
        sq, log, rstd, conv = ([t.sb(f"{n}{u}", [P, G]) for u in range(2)] for n in ("sq", "log", "rstd", "conv"))
        xn = t.sb("xn", [P, N])
        loaded, eps_ready, squared, mean_ready, log_ready, rstd_ready, normed = t.sems(
            "loaded", "eps_ready", "squared", "mean_ready", "log_ready", "rstd_ready", "normed")
        with Stage(k, "rms") as r:
            block = r.block()

            @block.sync
            def _(sync):
                with nc.allow_non_contiguous_dma(reason="columns"):
                    sync.dma_start(cols[:, 0:1], column(a["L1_attn_norm_in_w"])).then_inc(loaded, 16)
                    sync.dma_start(cols[:, 1:2], column(a["L1_attn_conv_b"])).then_inc(loaded, 16)
                    sync.dma_start(cols[:, 2:6], a["L1_attn_conv_w"].rearrange("d o j -> d (o j)")).then_inc(loaded, 16)
                    sync.dma_start(bau[:, :], column(a["L1_attn_bau"])).then_inc(loaded, 16)
                sync.dma_start(w_au[:, :], a["L1_attn_Wau"]).then_inc(loaded, 16)

            @block.scalar
            def _(act):
                act.preload_act_table_set(LOG_EXP)
                act.wait_ge(eps_ready, 1)
                with act.Fori(0, NG // 2) as i:
                    for u in range(2):
                        act.activation(sq[u][:, :], k.X[:, ds(i * (2 * G) + u * G, G)], ACT.Square).then_inc(squared, 1)
                    for u in range(2):
                        act.wait_ge(mean_ready, i * 2 + (u + 1))
                        act.activation(log[u][:, :], k.bank[u][:, :], ACT.Ln, bias=rms_eps[:, :]).then_inc(log_ready, 1)
                        act.wait_ge(log_ready, i * 2 + (u + 1))
                        act.activation(rstd[u][:, :], log[u][:, :], ACT.Exp, scale=-0.5).then_inc(rstd_ready, 1)
                    act.wait_ge(normed, i * 2 + 2)

            @block.tensor
            def _(pe):
                with pe.Fori(0, NG // 2) as i:
                    for u in range(2):
                        pe.wait_ge(squared, i * 2 + (u + 1))
                        nc.tensor.matmul(k.bank[u][:, :], k.ones_mean[:, :], sq[u][:, :], start=True, stop=True
                                         ).then_inc(mean_ready, 1)

            @block.vector
            def _(dve):
                dve.memset(rms_eps[:, :], RMS_EPS).then_inc(eps_ready, 1)
                dve.wait_ge(loaded, 80)
                with dve.Fori(0, NG // 2) as i:
                    for u in range(2):
                        dve.wait_ge(rstd_ready, i * 2 + (u + 1))
                        g_at = ds(i * (2 * G) + u * G, G)
                        dve.scalar_tensor_tensor(xn[:, g_at], k.X[:, g_at], cols[:, 0:1], rstd[u][:, :], ALU.mult,
                                                 ALU.mult).then_inc(normed, 1)
        with Stage(k, "conv") as r:
            taps, h_ready, u_ready, u_kept = r.sems("taps", "h_ready", "u_ready", "u_kept")
            block = r.block()

            @block.vector
            def _(dve):
                with dve.Fori(0, NG // 2) as i:
                    for u in range(2):
                        x = xn[:, ds(i * (2 * G) + u * G, G)].rearrange("p (b t) -> p b t", t=T)
                        c = conv[u][:, :].rearrange("p (b t) -> p b t", t=T)
                        dve.tensor_scalar(c, x, cols[:, 5:6], cols[:, 1:2], ALU.mult, ALU.add).then_inc(taps, 1)
                        for j in (1, 2, 3):
                            dve.wait_ge(taps, i * 8 + (4 * u + j))
                            dve.scalar_tensor_tensor(c[:, :, j:T], x[:, :, 0:T - j], cols[:, 5 - j:6 - j], c[:, :, j:T],
                                                     ALU.mult, ALU.add).then_inc(taps, 1)
                    dve.wait_ge(h_ready, i * 2 + 2)

            @block.scalar
            def _(act):
                act.preload_act_table(ACT.Silu)
                with act.Fori(0, NG // 2) as i:
                    for u in range(2):
                        act.wait_ge(taps, i * 8 + 4 * (u + 1))
                        act.activation(hT[:, ds(i * (2 * G) + u * G, G)], conv[u][:, :], ACT.Silu).then_inc(h_ready, 1)
                    for u in range(2):
                        act.wait_ge(u_ready, i * 2 + (u + 1))
                        act.activation(uT[:, ds(i * (2 * G) + u * G, G)], k.bank[u][0:DK, :], ACT.Silu, bias=bau[:, :]
                                       ).then_inc(u_kept, 1)

            @block.tensor
            def _(pe):
                with pe.Fori(0, NG // 2) as i:
                    for u in range(2):
                        pe.wait_ge(h_ready, i * 2 + (u + 1))
                        nc.tensor.matmul(k.bank[u][0:DK, :], w_au[:, :], hT[:, ds(i * (2 * G) + u * G, G)],
                                         start=True, stop=True).then_inc(u_ready, 1)


def delta_spikes(k, s, hT, spikes):
    nc = k.nc
    with Stage(k, "spk") as t:
        drive = t.sb("drive", [P, DP, N])
        w = t.sb("w", [P, DP * P])
        charge, left = t.sb("charge", [P, DP * B]), t.sb("left", [P, DP * B])
        loaded, driven, kept, cleared, charged, fired, spent = t.sems(
            "loaded", "driven", "kept", "cleared", "charged", "fired", "spent")
        block = t.block()

        @block.sync
        def _(sync):
            sync.dma_start(w[:, :], k.a["L1_attn_Wspike"]).then_inc(loaded, 16)

        @block.tensor
        def _(pe):
            pe.wait_ge(loaded, 16)
            with pe.Fori(0, NG // 2) as i:
                for u in range(2):
                    for hp in range(DP):
                        last = nc.tensor.matmul(k.bank[4 * u + hp][:, :], w[:, hp * P:(hp + 1) * P],
                                                hT[:, ds(i * (2 * G) + u * G, G)], start=True, stop=True)
                    last.then_inc(driven, 1)
                pe.wait_ge(kept, i * 2 + 2)

        @block.scalar
        def _(act):
            with act.Fori(0, NG // 2) as i:
                for u in range(2):
                    act.wait_ge(driven, i * 2 + (u + 1))
                    act.activation(drive[:, :, ds(i * (2 * G) + u * G, G)], k.psum[:, 4 * u:4 * u + 4, :], ACT.Copy
                                   ).then_inc(kept, 1)

        @block.vector
        def _(dve):
            dve.memset(left[:, :], 0.0).then_inc(spent, 1)
            dve.wait_ge(kept, NG)
            with dve.Fori(0, T) as pos:
                at = lambda ap: ap[:, :, :].rearrange("p h (b t) -> p (h b) t", t=T)[:, :, ds(pos, 1)].rearrange(
                    "p n o -> p (n o)")
                dve.wait_ge(spent, pos + 1)
                dve.scalar_tensor_tensor(charge[:, :], left[:, :], DECAY, at(drive), ALU.mult, ALU.add
                                         ).then_inc(charged, 1)
                dve.wait_ge(charged, pos + 1)
                dve.tensor_scalar(at(spikes), charge[:, :], THRESHOLD, None, ALU.is_gt).then_inc(fired, 1)
                dve.wait_ge(fired, pos + 1)
                dve.scalar_tensor_tensor(left[:, :], at(spikes), -THRESHOLD, charge[:, :], ALU.mult, ALU.add
                                         ).then_inc(spent, 1)


def delta_weights(k, s):
    nc = k.nc
    a = k.a
    w = Core()
    w.q, w.k, w.v = (s.sb(n, [P, DP * P]) for n in ("wq", "wk", "wv"))
    w.alpha = s.sb("w_alpha", [DK, DP * P])
    w.beta = s.sb("w_beta", [P, DP, P])
    w.o = s.sb("wo", [P, DP, D])
    w.alpha_spike = s.sb("alpha_spike", [P, 3, DP, P], BF16)
    w.beta_spike = s.sb("beta_spike", [P, 3, DP, P], BF16)
    w.head_ones = s.sb("head_ones_bf16", [P, P], BF16)
    w.bias = s.sb("bias", [P, 2, DP])
    w.levels, w.minus_levels = (s.sb(n, [P, LEVELS, T // 2]) for n in ("level_masks", "minus_masks"))
    w.eye2 = s.sb("eye2", [P, T])
    w.eye_bf = s.sb("eye_bf16", [P, P], BF16)
    w.head_sum, w.head_mean = s.sb("head_sum", [P, P]), s.sb("head_mean", [P, P])
    with Stage(k, "dw") as t:
        raw_beta, cols = t.sb("raw_beta", [P, DH]), t.sb("cols", [P, 3, DP])
        wide = t.sb("wide", [P, 2, DP, P])
        left = t.sb("left", [P, 2, DP, P])
        loaded, step = t.sems("loaded", "dve_step")
        block = t.block()

        @block.sync
        def _(sync):
            loads = [(w.q[:, :], a["L1_attn_Wq"]), (w.k[:, :], a["L1_attn_Wk"]), (w.v[:, :], a["L1_attn_Wv"]),
                     (w.alpha[:, :], a["L1_attn_Wad"]), (raw_beta[:, :], a["L1_attn_Wbeta"]),
                     (w.o[:, :, :], a["L1_attn_Wo"].rearrange("(n p) o -> p n o", p=P)),
                     (w.levels[:, :, :], a["level_masks"]), (w.eye2[:, :], a["eye2"]), (w.head_sum[:, :], a["head_sum"])]
            for dst, src in loads:
                sync.dma_start(dst, src).then_inc(loaded, 16)
            with nc.allow_non_contiguous_dma(reason="columns"):
                for c, name in enumerate(("alpha_spike", "beta_spike")):
                    sync.dma_start(cols[:, c, :], a[f"L1_attn_{name}"].rearrange("o (n j) d -> (o j d) n", j=2)
                                   ).then_inc(loaded, 16)
                sync.dma_start(cols[:, 2, :], a["L1_attn_head_norm_w"].rearrange("(n j) d -> (j d) n", j=2)
                               ).then_inc(loaded, 16)
                sync.dma_start(w.bias[:, 0, :], a["L1_attn_bad"].rearrange("(n p) -> p n", p=P)).then_inc(loaded, 16)
                for j in range(2):
                    sync.dma_start(w.bias[j * DK:(j + 1) * DK, 1, :],
                                   a["L1_attn_bbeta"].rearrange("(n j) -> j n", j=2)[j, :].partition_broadcast(DK)
                                   ).then_inc(loaded, 16)

        @block.vector
        def _(dve):
            dve.wait_ge(loaded, 16 * 15)
            dve.tensor_copy(w.head_ones[:, :], w.head_sum[:, :])
            dve.tensor_scalar(w.minus_levels[:, :, :], w.levels[:, :, :], -1.0, None, ALU.mult)
            dve.tensor_copy(w.eye_bf[:, :], k.eye[:, :])
            dve.tensor_scalar(w.head_mean[:, :], w.head_sum[:, :], 1.0 / DK, None, ALU.mult)
            dve.tensor_copy(w.beta[:, :, :].rearrange("p n (j c) -> p (n j) c", j=2),
                            raw_beta[:, :].unsqueeze(2).to_broadcast([P, DH, DK]))
            over = lambda ap: ap.unsqueeze(2).to_broadcast([P, DP, P])
            dve.tensor_tensor(w.o[:, :, :], w.o[:, :, :], over(cols[:, 2, :]), ALU.mult)
            for c, base in enumerate((k.eye, w.head_sum)):
                last = dve.tensor_tensor(wide[:, c, :, :], base[:, :].unsqueeze(1).to_broadcast([P, DP, P]),
                                         over(cols[:, c, :]), ALU.mult)
            last.then_inc(step, 1)
            n = 1
            for c, dst in enumerate((w.alpha_spike, w.beta_spike)):
                src = wide[:, c, :, :]
                for part in range(3):
                    dve.wait_ge(step, n)
                    dve.tensor_copy(dst[:, part, :, :], src).then_inc(step, 1)
                    n += 1
                    if part < 2:
                        dve.wait_ge(step, n)
                        dve.tensor_tensor(left[:, part, :, :], src, dst[:, part, :, :], ALU.subtract).then_inc(step, 1)
                        n += 1
                        src = left[:, part, :, :]
    return w


def delta_rule(k, s, hT, uT, spikes, yT):
    nc = k.nc
    w = delta_weights(k, s)
    two = lambda name, shape, dt=F32: [s.sb(f"{name}{u}", shape, dt) for u in range(2)]
    h_t = two("h", [P, TT])
    raw, kq = two("raw", [P, HB, 2, T]), two("kq", [P, HB, 2, T])
    inv = two("inv", [P, 2, 512])
    alpha, v = two("alpha", [P, HB, T]), two("v", [P, 2, DP, DK])
    blocks = [[alpha[u]] + [s.sb(f"decay{2 ** l}_{u}", [P, HB, T >> l]) for l in range(1, LEVELS - 1)] for u in range(2)]
    kS_diag, R_diag, RT_diag, Z_diag = (two(n, [P, HB, 2 * T]) for n in ("kS_diag", "R_diag", "RT_diag", "Z_diag"))
    CT_diag = [two(f"CT{m}_diag", [P, HB, 2 * T]) for m in range(2)]
    PT = two("PT", [P, HB, T])
    kq_flat = [kq[u][:, :, :, :].rearrange("p (c n) w t -> p c (n w t)", c=2) for u in range(2)]
    sq, log = inv, kq_flat
    ysq, yn = ([kq_flat[u][:, c, :] for u in range(2)] for c in range(2))
    ylog, yinv = ([inv[u][:, c, :] for u in range(2)] for c in range(2))
    RV, W = ([m[u].rearrange("p (n t) -> p n t", t=T) for u in range(2)] for m in (ylog, yinv))
    U_diag, beta = Z_diag, PT
    floor, small, rms_eps = s.sb("floor", [P, 1]), s.sb("small", [P, 1]), s.sb("rms_eps2", [P, 1])
    (h_staged, logits, raw_ready, sq_ready, sig_ready, counted, v_ready, gates_ready, v_kept, n2_ready, ln1, ex1, ln2,
     kq_logits, inv_ready, normed, kS_ready, kq_ready, diag_ready, y_ready, ysq_ready, yms_ready, ylog_ready, yinv_ready, yn_ready,
     out_ready, out_kept, cleared) = s.sems(
        "h_staged", "logits_ready", "raw_ready", "sq_ready", "sig_ready", "counted", "v_ready", "gates_ready", "v_kept",
        "n2_ready", "ln1", "ex1", "ln2", "kq_logits", "inv_ready", "normed", "kS_ready", "kq_ready", "diag_ready", "y_ready",
        "ysq_ready", "yms_ready", "ylog_ready", "yinv_ready", "yn_ready", "out_ready", "out_kept", "cleared")
    level_ready, level_kept, scaled, kS_scaled, decays_ready, ct_cleared = (
        s.sems(*[f"{name}{l}" for l in range(LEVELS)]) for name in (
            "level_ready", "level_kept", "scaled", "kS_scaled", "decays_ready", "ct_cleared"))
    z_ready, z_kept_a, z_kept_v, r_ready, r_kept_a, r_kept_v, rt_ready, rt_kept_a, rt_kept_v = (
        s.sems(*[f"{name}{l}" for l in range(LEVELS - 1)]) for name in (
            "z_ready", "z_kept_a", "z_kept_v", "r_ready", "r_kept_a", "r_kept_v", "rt_ready", "rt_kept_a", "rt_kept_v"))
    rt_first, rv_ready, rv_kept, crv_ready, w_ready, u_ready, u_kept = s.sems(
        "rt_first", "rv_ready", "rv_kept", "crv_ready", "w_ready", "u_ready", "u_kept")
    block = s.block()
    LAST = NT // 2 - 1

    def upto(tile):
        i, n = tile
        return i * 2 + (n + 1)

    def tokens(tile):
        i, n = tile
        return ds(i * (2 * TT) + n * TT, TT)

    def par(tile):
        return tile[1] % 2

    def bank(u, n):
        return k.bank[4 * u + n]

    def hb(ap):
        return ap.rearrange("p (n t) -> p n t", t=T)

    def squares(ap):
        return ap.rearrange("p (n t) -> p n t", t=2 * T)

    HALVES = [slice(j * DK, (j + 1) * DK) for j in range(2)]

    def product(out, lhsT_diag, rhs):
        for n in range(HB):
            last = nc.tensor.matmul(out[:, n * T:(n + 1) * T], lhsT_diag[:, n, :], rhs(n), start=True, stop=True)
        return last

    def square_product(u, lhsT_diag, rhs, plus_identity=False):
        for m in range(2):
            if plus_identity:
                nc.tensor.matmul(squares(bank(u, 2 + m)), w.eye_bf[:, :],
                                 w.eye_bf[:, :].unsqueeze(1).to_broadcast([P, HB // 2, 2 * T]), start=True, stop=False)
            for c in range(HB // 2):
                n = m * (HB // 2) + c
                last = nc.tensor.matmul(bank(u, 2 + m)[:, c * 2 * T:(c + 1) * 2 * T], lhsT_diag[:, n, :], rhs[:, n, :],
                                        start=not plus_identity, stop=not plus_identity or c == HB // 2 - 1)
        return last

    def wide_product(u, bank0, lhsT_diag, pairs):
        for n in range(HB):
            c = n % (HB // 2)
            last = nc.tensor.matmul(bank(u, bank0 + n // (HB // 2))[:, c * 2 * T:(c + 1) * 2 * T], lhsT_diag[:, n, :],
                                    pairs[:, n, :, :].rearrange("p w t -> p (w t)"), start=True, stop=True)
        return last

    def pairs_of(u, bank0):
        return k.psum[:, 4 * u + bank0:4 * u + bank0 + 2, :].rearrange("p m (n w t) -> p (m n) w t", w=2, t=T)

    def right(ap, l):
        return ap.rearrange("p n w (c two l) -> p n w c two l", two=2, l=1 << l)[:, :, :, :, 1, :]

    def in_turn(eng, front, half, end):
        front((0, 0))
        half(None, (0, 0), (0, 1))
        with eng.Fori(0, LAST) as i:
            half((i, 0), (i, 1), (i, 2))
            half((i, 1), (i, 2), (i, 3))
        half((LAST, 0), (LAST, 1), None)
        end((LAST, 1))

    @block.tensor
    def _(pe):
        pe.wait_ge(cleared, 1)

        def project_gates(y, hp):
            u, c, hc = par(y), slice(hp * TT, (hp + 1) * TT), slice(hp * P, (hp + 1) * P)
            if hp == 0:
                pe.wait_ge(h_staged, upto(y))
            nc.tensor.matmul(bank(u, 2)[:, c], w.alpha[:, hc], uT[:, tokens(y)], start=True, stop=False)
            for part in range(3):
                nc.tensor.matmul(bank(u, 2)[:, c], w.alpha_spike[:, part, hp, :], spikes[:, hp, tokens(y)],
                                 start=False, stop=(part == 2))
            nc.tensor.matmul(bank(u, 3)[:, c], w.beta[:, hp, :], h_t[u][:, :], start=True, stop=False)
            for part in range(3):
                last = nc.tensor.matmul(bank(u, 3)[:, c], w.beta_spike[:, part, hp, :], spikes[:, hp, tokens(y)],
                                        start=False, stop=(part == 2))
            if hp == DP - 1:
                last.then_inc(logits, 1)

        def project_kq(y, hp):
            u, c, hc = par(y), slice(hp * TT, (hp + 1) * TT), slice(hp * P, (hp + 1) * P)
            nc.tensor.matmul(bank(u, 0)[:, c], w.k[:, hc], h_t[u][:, :], start=True, stop=True)
            last = nc.tensor.matmul(bank(u, 1)[:, c], w.q[:, hc], h_t[u][:, :], start=True, stop=True)
            if hp == DP - 1:
                last.then_inc(kq_logits, 1)

        def norms(y):
            u = par(y)
            pe.wait_ge(sq_ready, upto(y))
            pe.wait_ge(raw_ready, upto(y))
            for c in range(2):
                last = nc.tensor.matmul(bank(u, c)[:, :], w.head_sum[:, :], sq[u][:, c, :], start=True, stop=True)
            last.then_inc(n2_ready, 1)

        def count_and_values(y):
            u = par(y)
            pe.wait_ge(ln1, upto(y))
            for hp in range(DP):
                last = nc.tensor.matmul(bank(u, 0)[:, hp * TT:(hp + 1) * TT], w.head_ones[:, :],
                                        spikes[:, hp, tokens(y)], start=True, stop=True)
            last.then_inc(counted, 1)
            wv = w.v[:, :].rearrange("p (n j v) -> p j n v", j=2, v=DK)
            for b in range(2):
                for j in range(2):
                    last = nc.tensor.matmul(
                        bank(u, 1)[j * DK:(j + 1) * DK, b * 256:(b + 1) * 256].rearrange("p (n v) -> p n v", v=DK),
                        h_t[u][:, b * T:(b + 1) * T], wv[:, j, :, :], start=True, stop=True)
            last.then_inc(v_ready, 1)

        def diagonal(y):
            u = par(y)
            pe.wait_ge(gates_ready, upto(y))
            pe.wait_ge(sig_ready, upto(y))
            pe.wait_ge(v_kept, upto(y))
            pe.wait_ge(kS_ready, upto(y))
            wide_product(u, 2, kS_diag[u], raw[u]).then_inc(diag_ready, 1)

        def level(x, l):
            u = par(x)
            if l == 0:
                pe.wait_ge(kq_ready, upto(x))
            else:
                pe.wait_ge(scaled[l - 1], upto(x))
                pe.wait_ge(kS_scaled[l - 1], upto(x))
                pe.wait_ge(level_kept[l - 1], upto(x))
            wide_product(u, 0, kS_diag[u], kq[u]).then_inc(level_ready[l], 1)

        def first_c(x):
            u = par(x)
            pe.wait_ge(level_kept[0], upto(x))
            for n in range(HB):
                c = n % (HB // 2)
                last = nc.tensor.transpose(bank(u, 2 + n // (HB // 2))[:, c * 2 * T:(c + 1) * 2 * T],
                                           CT_diag[0][u][:, n, :], k.eye[:, :])
            last.then_inc(r_ready[0], 1)

        def z(x, l):
            u = par(x)
            pe.wait_ge(level_kept[l], upto(x))
            if l == 1:
                pe.wait_ge(r_kept_v[0], upto(x))
            else:
                pe.wait_ge(rt_kept_a[l - 1], upto(x))
                pe.wait_ge(rt_kept_v[l - 1], upto(x))
            square_product(u, CT_diag[l % 2][u], R_diag[u], plus_identity=True).then_inc(z_ready[l], 1)

        def r(x, l):
            u = par(x)
            pe.wait_ge(z_kept_a[l], upto(x))
            pe.wait_ge(z_kept_v[l], upto(x))
            if l == 1:
                pe.wait_ge(rt_first, upto(x))
            square_product(u, RT_diag[u], Z_diag[u]).then_inc(r_ready[l], 1)

        def rt(x, l):
            u = par(x)
            before_a, before_v = (r_kept_a[l], r_kept_v[l]) if l < LEVELS - 2 else (z_kept_a[l], z_kept_v[l])
            pe.wait_ge(before_a, upto(x))
            pe.wait_ge(before_v, upto(x))
            square_product(u, Z_diag[u], RT_diag[u]).then_inc(rt_ready[l], 1)

        def read_v(w_):
            u = par(w_)
            pe.wait_ge(rt_kept_a[4], upto(w_))
            pe.wait_ge(rt_kept_v[4], upto(w_))
            product(bank(u, 2), RT_diag[u], lambda n: v[u][:, n % 2, n // 2, :]).then_inc(rv_ready, 1)

        def corrected(w_):
            u = par(w_)
            pe.wait_ge(level_kept[5], upto(w_))
            pe.wait_ge(rv_kept, upto(w_))
            product(bank(u, 3), CT_diag[1][u], lambda n: RV[u][:, n, :]).then_inc(crv_ready, 1)

        def solve(w_):
            u = par(w_)
            pe.wait_ge(w_ready, upto(w_))
            product(bank(u, 2), RT_diag[u], lambda n: W[u][:, n, :]).then_inc(u_ready, 1)

        def outputs(w_):
            u = par(w_)
            pe.wait_ge(u_kept, upto(w_))
            product(bank(u, 0), U_diag[u], lambda n: PT[u][:, n, :]).then_inc(y_ready, 1)

        def head_norm(w_):
            u = par(w_)
            pe.wait_ge(ysq_ready, upto(w_))
            nc.tensor.matmul(bank(u, 1)[:, :], w.head_mean[:, :], ysq[u][:, :], start=True, stop=True
                             ).then_inc(yms_ready, 1)

        def project_out(w_):
            u = par(w_)
            pe.wait_ge(yn_ready, upto(w_))
            for hp in range(DP):
                last = nc.tensor.matmul(bank(u, 3)[:, 0:TT], w.o[:, hp, :], yn[u][:, hp * TT:(hp + 1) * TT],
                                        start=(hp == 0), stop=(hp == DP - 1))
            last.then_inc(out_ready, 1)

        def front(y):
            for hp in range(DP):
                project_gates(y, hp)
            for hp in range(DP):
                project_kq(y, hp)
            norms(y)
            count_and_values(y)
            diagonal(y)
            level(y, 0)

        def end(w_):
            read_v(w_)
            corrected(w_)
            solve(w_)
            outputs(w_)
            head_norm(w_)
            project_out(w_)

        def half(w_, x, y):
            first_c(x)
            if w_:
                read_v(w_)
            level(x, 1)
            if w_:
                corrected(w_)
            z(x, 1)
            if w_:
                solve(w_)
            level(x, 2)
            r(x, 1)
            if w_:
                outputs(w_)
            rt(x, 1)
            if w_:
                head_norm(w_)
            z(x, 2)
            level(x, 3)
            if w_:
                project_out(w_)
            r(x, 2)
            if y:
                if w_:
                    pe.wait_ge(out_kept, upto(w_))
                project_gates(y, 0)
                project_gates(y, 1)
            rt(x, 2)
            if y:
                project_gates(y, 2)
                project_gates(y, 3)
            z(x, 3)
            if y:
                project_kq(y, 0)
                project_kq(y, 1)
            level(x, 4)
            r(x, 3)
            if y:
                project_kq(y, 2)
                project_kq(y, 3)
            rt(x, 3)
            if y:
                norms(y)
            z(x, 4)
            level(x, 5)
            if y:
                count_and_values(y)
            rt(x, 4)
            if y:
                diagonal(y)
                level(y, 0)

        in_turn(pe, front, half, end)

    @block.scalar
    def _(act):
        act.wait_ge(cleared, 1)

        def gate(y, g):
            u = par(y)
            if g == 0:
                act.wait_ge(logits, upto(y))
            for hp in range(DP):
                last = act.activation((alpha, beta)[g][u][:, 2 * hp:2 * hp + 2, :].rearrange("p n t -> p (n t)"),
                                      bank(u, 2 + g)[:, hp * TT:(hp + 1) * TT], ACT.Sigmoid, bias=w.bias[:, g, hp:hp + 1])
            if g == 1:
                last.then_inc(sig_ready, 1)

        def square(y):
            u = par(y)
            act.wait_ge(raw_ready, upto(y))
            act.activation(sq[u][:, :, :].rearrange("p w (n t) -> p w n t", t=T),
                           raw[u][:, :, :, :].rearrange("p n w t -> p w n t"), ACT.Square).then_inc(sq_ready, 1)
            act.preload_act_table_set(LOG_EXP)

        def norm(y, step):
            u = par(y)
            if step == 0:
                act.wait_ge(n2_ready, upto(y))
                act.activation(log[u][:, :, :], k.psum[:, 4 * u:4 * u + 2, :], ACT.Ln, bias=floor[:, :]
                               ).then_inc(ln1, 1)
            if step == 1:
                act.wait_ge(ln1, upto(y))
                act.activation(inv[u][:, :, :], log[u][:, :, :], ACT.Exp, scale=0.5).then_inc(ex1, 1)
            if step == 2:
                act.wait_ge(ex1, upto(y))
                act.activation(log[u][:, :, :], inv[u][:, :, :], ACT.Ln, bias=small[:, :]).then_inc(ln2, 1)
            if step == 3:
                act.wait_ge(ln2, upto(y))
                act.activation(inv[u][:, :, :], log[u][:, :, :], ACT.Exp, scale=-1.0).then_inc(inv_ready, 1)

        def keep(x, dst, ready, kept):
            u = par(x)
            act.wait_ge(ready, upto(x))
            act.activation(dst[u][:, 0:HB // 2, :], squares(bank(u, 2)), ACT.Copy).then_inc(kept, 1)

        def keep_rv(w_):
            act.wait_ge(rv_ready, upto(w_))
            act.activation(RV[par(w_)], hb(bank(par(w_), 2)), ACT.Copy).then_inc(rv_kept, 1)

        def keep_u(w_):
            u = par(w_)
            act.wait_ge(u_ready, upto(w_))
            for h in HALVES:
                last = act.activation(U_diag[u][h, :, h], hb(bank(u, 2)[h, :]), ACT.Copy)
            last.then_inc(u_kept, 1)

        def square_y(w_):
            act.wait_ge(y_ready, upto(w_))
            act.activation(ysq[par(w_)][:, :], bank(par(w_), 0), ACT.Square).then_inc(ysq_ready, 1)

        def norm_y(w_):
            u = par(w_)
            act.wait_ge(yms_ready, upto(w_))
            act.activation(ylog[u][:, :], bank(u, 1), ACT.Ln, bias=rms_eps[:, :]).then_inc(ylog_ready, 1)
            act.wait_ge(ylog_ready, upto(w_))
            act.activation(yinv[u][:, :], ylog[u][:, :], ACT.Exp, scale=-0.5).then_inc(yinv_ready, 1)

        def front(y):
            gate(y, 0)
            gate(y, 1)
            square(y)
            for step in range(4):
                norm(y, step)

        def end(w_):
            keep_rv(w_)
            keep_u(w_)
            square_y(w_)
            norm_y(w_)

        def half(w_, x, y):
            if w_:
                keep_rv(w_)
            keep(x, Z_diag, z_ready[1], z_kept_a[1])
            if w_:
                keep_u(w_)
            keep(x, R_diag, r_ready[1], r_kept_a[1])
            if w_:
                square_y(w_)
            keep(x, RT_diag, rt_ready[1], rt_kept_a[1])
            if w_:
                norm_y(w_)
            keep(x, Z_diag, z_ready[2], z_kept_a[2])
            keep(x, R_diag, r_ready[2], r_kept_a[2])
            keep(x, RT_diag, rt_ready[2], rt_kept_a[2])
            if y:
                gate(y, 0)
            keep(x, Z_diag, z_ready[3], z_kept_a[3])
            if y:
                gate(y, 1)
            keep(x, R_diag, r_ready[3], r_kept_a[3])
            if y:
                square(y)
            keep(x, RT_diag, rt_ready[3], rt_kept_a[3])
            if y:
                norm(y, 0)
            keep(x, Z_diag, z_ready[4], z_kept_a[4])
            if y:
                norm(y, 1)
                norm(y, 2)
                norm(y, 3)
            keep(x, RT_diag, rt_ready[4], rt_kept_a[4])

        in_turn(act, front, half, end)

    @block.gpsimd
    def _(pool):
        used = {2: r_ready[0], 3: z_ready[1], 4: z_ready[2], 5: z_ready[3], 0: z_ready[4]}

        def clear(x, l):
            u = par(x)
            k.hold(pool)
            pool.wait_ge(used[l], upto(x))
            if l == 2:
                pool.wait_ge(rt_first, upto(x))
            pool.memset(CT_diag[l % 2][u][:, :, :], 0.0).then_inc(ct_cleared[l], 1)

        def clear_behind(w_, x):
            k.hold(pool)
            pool.wait_ge(z_ready[1], upto(x))
            pool.memset(CT_diag[1][par(w_)][:, :, :], 0.0).then_inc(ct_cleared[1], 1)

        def scale(x, l):
            u = par(x)
            pool.wait_ge(level_ready[l], upto(x))
            if l > 0:
                pool.wait_ge(decays_ready[l - 1], upto(x))
            L = 1 << l
            total = blocks[u][l][:, :, :].rearrange("p n (c two) -> p n c two", two=2)[:, :, :, 1]
            for h in HALVES:
                ks = kS_diag[u][:, :, h].rearrange("p n (c two l) -> p n c two l", two=2, l=L)[:, :, :, 0, :]
                last = pool.tensor_tensor(ks, ks, total.unsqueeze(3).to_broadcast([P, HB, T // (2 * L), L]), ALU.mult)
            last.then_inc(kS_scaled[l], 1)

        def first_rt(x):
            u = par(x)
            pool.wait_ge(level_kept[0], upto(x))
            pool.tensor_tensor(RT_diag[u][:, :, :], CT_diag[0][u][:, :, :],
                               k.eye[:, :].unsqueeze(1).to_broadcast([P, HB, 2 * T]), ALU.add).then_inc(rt_first, 1)

        def front(y):
            scale(y, 0)

        def end(w_):
            pass

        def half(w_, x, y):
            first_rt(x)
            clear(x, 2)
            scale(x, 1)
            if w_:
                clear_behind(w_, x)
            clear(x, 3)
            scale(x, 2)
            clear(x, 4)
            scale(x, 3)
            clear(x, 5)
            scale(x, 4)
            clear(x, 0)
            if y:
                scale(y, 0)

        for l in range(2):
            for u in range(2):
                pool.memset(CT_diag[l][u][:, :, :], 0.0).then_inc(ct_cleared[l], 1)
        in_turn(pool, front, half, end)

    @block.vector
    def _(dve):
        for m in (kS_diag, Z_diag):
            for u in range(2):
                dve.memset(m[u][:, :, :], 0.0)
        dve.memset(floor[:, :], NORM_FLOOR)
        dve.memset(rms_eps[:, :], RMS_EPS)
        dve.memset(small[:, :], 1e-6).then_inc(cleared, 1)

        def stage(y):
            dve.tensor_copy(h_t[par(y)][:, :], hT[:, tokens(y)]).then_inc(h_staged, 1)

        def keep_raw(y):
            u = par(y)
            dve.wait_ge(kq_logits, upto(y))
            for c in range(2):
                last = dve.tensor_copy(raw[u][:, :, c, :], hb(bank(u, c)))
            last.then_inc(raw_ready, 1)

        def gates(y):
            u = par(y)
            dve.wait_ge(counted, upto(y))
            dve.wait_ge(sig_ready, upto(y))
            count = hb(bank(u, 0))
            dve.scalar_tensor_tensor(alpha[u][:, :, :], count, 0.5, alpha[u][:, :, :], ALU.is_lt, ALU.max)
            dve.scalar_tensor_tensor(beta[u][:, :, :], count, 1.0, beta[u][:, :, :], ALU.min, ALU.min
                                     ).then_inc(gates_ready, 1)
            dve.wait_ge(v_ready, upto(y))
            dve.tensor_copy(v[u][:, :, :, :].rearrange("p b n v -> p (b n v)"), bank(u, 1)).then_inc(v_kept, 1)

        def normalise(y):
            u = par(y)
            dve.wait_ge(inv_ready, upto(y))
            dve.tensor_tensor(raw[u][:, :, :, :], raw[u][:, :, :, :],
                              inv[u][:, :, :].rearrange("p w (n t) -> p n w t", t=T), ALU.mult).then_inc(normed, 1)

        def weigh(y):
            u = par(y)
            dve.wait_ge(normed, upto(y))
            dve.wait_ge(gates_ready, upto(y))
            for h in HALVES:
                last = dve.tensor_tensor(kS_diag[u][h, :, h], raw[u][h, :, 0, :], beta[u][h, :, :], ALU.mult)
            last.then_inc(kS_ready, 1)
            dve.tensor_tensor(kq[u][:, :, :, :], raw[u][:, :, :, :],
                              alpha[u][:, :, :].unsqueeze(2).to_broadcast([P, HB, 2, T]), ALU.mult
                              ).then_inc(kq_ready, 1)

        def diagonal(y):
            u = par(y)
            dve.wait_ge(diag_ready, upto(y))
            dve.tensor_tensor(PT[u][:, :, :], pairs_of(u, 2)[:, :, 1, :], w.eye2[:, :].unsqueeze(1).to_broadcast([P, HB, T]),
                              ALU.mult).then_inc(cleared, 1)

        def level(x, l):
            u, L = par(x), 1 << l
            dve.wait_ge(level_ready[l], upto(x))
            if l < LEVELS - 1:
                pair = blocks[u][l][:, :, :].rearrange("p n (c two) -> p n c two", two=2)
                if l > 0:
                    dve.wait_ge(decays_ready[l - 1], upto(x))
                    dve.wait_ge(scaled[l - 1], upto(x))
                if l < LEVELS - 2:
                    dve.tensor_tensor(blocks[u][l + 1][:, :, :], pair[:, :, :, 0], pair[:, :, :, 1], ALU.mult
                                      ).then_inc(decays_ready[l], 1)
                for c in range(2):
                    half_kq = right(kq[u][:, :, :, :], l)[:, :, c, :, :]
                    last = dve.tensor_tensor(half_kq, half_kq, pair[:, :, :, 0].unsqueeze(3).to_broadcast(
                        [P, HB, T // (2 * L), L]), ALU.mult)
                last.then_inc(scaled[l], 1)
            out = right(pairs_of(u, 0), l)
            mask, minus = (m[:, l:l + 1, :].rearrange("p o (c l) -> p o c l", l=L) for m in (w.levels, w.minus_levels))
            shape = [P, HB, T // (2 * L), L]
            pt = PT[u][:, :, :].rearrange("p n (c two l) -> p n c two l", two=2, l=L)[:, :, :, 1, :]
            dve.wait_ge(ct_cleared[l], upto(x))
            if l == 0:
                dve.wait_ge(cleared, upto(x) + 1)
            else:
                dve.wait_ge(level_kept[l - 1], upto(x))
            for h in HALVES:
                ct = CT_diag[l % 2][u][h, :, h].rearrange("p n (c two l) -> p n c two l", two=2, l=L)
                dve.tensor_tensor(ct[:, :, :, 1, :], out[h, :, 0, :, :], minus[h, :, :, :].to_broadcast([DK] + shape[1:]),
                                  ALU.mult)
            dve.copy_predicated(pt, mask.bitcast(U32).to_broadcast(shape), out[:, :, 1, :, :]
                                ).then_inc(level_kept[l], 1)

        def first(x):
            u = par(x)
            eye = k.eye[:, :].unsqueeze(1)
            dve.wait_ge(r_ready[0], upto(x))
            dve.tensor_tensor(R_diag[u][:, :, :], k.psum[:, 4 * u + 2:4 * u + 4, :].rearrange(
                "p m (n t) -> p (m n) t", t=2 * T), eye.to_broadcast([P, HB, 2 * T]), ALU.add).then_inc(r_kept_v[0], 1)

        def keep(x, dst, ready, kept):
            u = par(x)
            dve.wait_ge(ready, upto(x))
            dve.tensor_scalar(dst[u][:, HB // 2:HB, :], squares(bank(u, 3)), 1.0, None, ALU.mult).then_inc(kept, 1)

        def subtract(w_):
            u = par(w_)
            dve.wait_ge(crv_ready, upto(w_))
            dve.tensor_tensor(W[u].rearrange("p (n b) v -> p n b v", b=2),
                              bank(u, 3).rearrange("p (n b v) -> p n b v", b=2, v=DK),
                              v[u][:, :, :, :].rearrange("p b n v -> p n b v"), ALU.add).then_inc(w_ready, 1)

        def normalise_y(w_):
            u = par(w_)
            dve.wait_ge(yinv_ready, upto(w_))
            dve.tensor_tensor(yn[u][:, :], yinv[u][:, :], bank(u, 0), ALU.mult).then_inc(yn_ready, 1)

        def keep_out(w_):
            dve.wait_ge(out_ready, upto(w_))
            dve.tensor_scalar(yT[:, tokens(w_)], bank(par(w_), 3)[:, 0:TT], 1.0, None, ALU.mult).then_inc(out_kept, 1)

        def front(y):
            stage(y)
            keep_raw(y)
            normalise(y)
            gates(y)
            weigh(y)
            diagonal(y)
            level(y, 0)

        def end(w_):
            subtract(w_)
            normalise_y(w_)
            keep_out(w_)

        def half(w_, x, y):
            if y:
                stage(y)
            first(x)
            level(x, 1)
            if w_:
                subtract(w_)
            keep(x, Z_diag, z_ready[1], z_kept_v[1])
            level(x, 2)
            keep(x, R_diag, r_ready[1], r_kept_v[1])
            keep(x, RT_diag, rt_ready[1], rt_kept_v[1])
            if w_:
                normalise_y(w_)
            keep(x, Z_diag, z_ready[2], z_kept_v[2])
            level(x, 3)
            keep(x, R_diag, r_ready[2], r_kept_v[2])
            if w_:
                keep_out(w_)
            keep(x, RT_diag, rt_ready[2], rt_kept_v[2])
            keep(x, Z_diag, z_ready[3], z_kept_v[3])
            level(x, 4)
            keep(x, R_diag, r_ready[3], r_kept_v[3])
            if y:
                keep_raw(y)
            keep(x, RT_diag, rt_ready[3], rt_kept_v[3])
            keep(x, Z_diag, z_ready[4], z_kept_v[4])
            if y:
                gates(y)
            level(x, 5)
            if y:
                normalise(y)
            keep(x, RT_diag, rt_ready[4], rt_kept_v[4])
            if y:
                weigh(y)
                diagonal(y)
                level(y, 0)

        in_turn(dve, front, half, end)


def delta_output(k, s, yT):
    nc = k.nc
    a = k.a
    FF = 512
    with Stage(k, "dout") as t:
        w_u1, w_u2 = t.sb("w_u1", [P, DK]), t.sb("w_u2", [DK, D])
        w_1, w_3, w_2 = t.sb("w_1", [P, FF]), t.sb("w_3", [P, FF]), t.sb("w_2", [P, FF // P, D])
        bu1, bu2, ff_norm = t.sb("bu1", [DK, 1]), t.sb("bu2", [P, 1]), t.sb("ff_norm", [P, 1])
        rms_eps = t.sb("rms_eps", [P, 1])
        u1 = t.sb("u1", [DK, N])
        two = lambda name, shape: [t.sb(f"{name}{u}", shape) for u in range(2)]
        gate, sq, log, rstd, gated, z = (two(n, [P, G]) for n in ("gate", "sq", "log", "rstd", "gated", "z"))
        act1, hid = two("act1", [P, G]), two("hid", [P, G])
        (loaded,) = t.sems("loaded")
        with Stage(k, "dg1") as r:
            u_ready, u_kept = r.sems("u_ready", "u_kept")
            block = r.block()

            @block.sync
            def _(sync):
                for dst, src in ((w_u1[:, :], a["L1_attn_Wu1"]), (w_u2[:, :], a["L1_attn_Wu2"]),
                                 (w_1[:, :], a["L1_attn_Wff1"]), (w_3[:, :], a["L1_attn_Wff3"]),
                                 (w_2[:, :, :], a["L1_attn_Wff2"].rearrange("(c p) d -> p c d", p=P))):
                    sync.dma_start(dst, src).then_inc(loaded, 16)
                with nc.allow_non_contiguous_dma(reason="columns"):
                    for dst, name in ((bu1, "bu1"), (bu2, "bu2"), (ff_norm, "ff_norm_w")):
                        sync.dma_start(dst[:, :], column(a[f"L1_attn_{name}"])).then_inc(loaded, 16)

            @block.tensor
            def _(pe):
                pe.wait_ge(loaded, 128)
                with pe.Fori(0, NG // 2) as i:
                    for u in range(2):
                        nc.tensor.matmul(k.bank[u][0:DK, :], w_u1[:, :], k.X[:, ds(i * (2 * G) + u * G, G)],
                                         start=True, stop=True).then_inc(u_ready, 1)
                    pe.wait_ge(u_kept, i * 2 + 2)

            @block.scalar
            def _(act):
                act.preload_act_table(ACT.Silu)
                act.wait_ge(loaded, 128)
                with act.Fori(0, NG // 2) as i:
                    for u in range(2):
                        act.wait_ge(u_ready, i * 2 + (u + 1))
                        act.activation(u1[:, ds(i * (2 * G) + u * G, G)], k.bank[u][0:DK, :], ACT.Silu, bias=bu1[:, :]
                                       ).then_inc(u_kept, 1)
        with Stage(k, "dg2") as r:
            g_ready, gate_ready, gated_ready, y1_ready = r.sems("g_ready", "gate_ready", "gated_ready", "y1_ready")
            block = r.block()

            @block.tensor
            def _(pe):
                with pe.Fori(0, NG // 2) as i:
                    for u in range(2):
                        nc.tensor.matmul(k.bank[u][:, :], w_u2[:, :], u1[:, ds(i * (2 * G) + u * G, G)],
                                         start=True, stop=True).then_inc(g_ready, 1)
                    pe.wait_ge(gate_ready, i * 2 + 2)

            @block.scalar
            def _(act):
                act.preload_act_table(ACT.Sigmoid)
                with act.Fori(0, NG // 2) as i:
                    for u in range(2):
                        act.wait_ge(g_ready, i * 2 + (u + 1))
                        act.activation(gate[u][:, :], k.bank[u][:, :], ACT.Sigmoid, bias=bu2[:, :]
                                       ).then_inc(gate_ready, 1)
                    act.wait_ge(gated_ready, i * 2 + 2)

            @block.vector
            def _(dve):
                dve.memset(rms_eps[:, :], RMS_EPS)
                with dve.Fori(0, NG // 2) as i:
                    for u in range(2):
                        dve.wait_ge(gate_ready, i * 2 + (u + 1))
                        y = yT[:, ds(i * (2 * G) + u * G, G)]
                        dve.tensor_tensor(gated[u][:, :], y, gate[u][:, :], ALU.mult).then_inc(gated_ready, 1)
                        dve.wait_ge(gated_ready, i * 2 + (u + 1))
                        dve.tensor_tensor(y, gated[u][:, :], k.X[:, ds(i * (2 * G) + u * G, G)], ALU.add
                                          ).then_inc(y1_ready, 1)
        with Stage(k, "dff") as r:
            zT = r.sb("zT", [P, N])
            with Stage(k, "drms") as q:
                squared, mean_ready, log_ready, rstd_ready, z_ready = q.sems(
                    "squared", "mean_ready", "log_ready", "rstd_ready", "z_ready")
                block = q.block()

                @block.scalar
                def _(act):
                    act.preload_act_table_set(LOG_EXP)
                    with act.Fori(0, NG // 2) as i:
                        for u in range(2):
                            act.activation(sq[u][:, :], yT[:, ds(i * (2 * G) + u * G, G)], ACT.Square
                                           ).then_inc(squared, 1)
                        for u in range(2):
                            act.wait_ge(mean_ready, i * 2 + (u + 1))
                            act.activation(log[u][:, :], k.bank[u][:, :], ACT.Ln, bias=rms_eps[:, :]
                                           ).then_inc(log_ready, 1)
                            act.wait_ge(log_ready, i * 2 + (u + 1))
                            act.activation(rstd[u][:, :], log[u][:, :], ACT.Exp, scale=-0.5).then_inc(rstd_ready, 1)
                        act.wait_ge(z_ready, i * 2 + 2)

                @block.tensor
                def _(pe):
                    with pe.Fori(0, NG // 2) as i:
                        for u in range(2):
                            pe.wait_ge(squared, i * 2 + (u + 1))
                            nc.tensor.matmul(k.bank[u][:, :], k.ones_mean[:, :], sq[u][:, :], start=True, stop=True
                                             ).then_inc(mean_ready, 1)

                @block.vector
                def _(dve):
                    with dve.Fori(0, NG // 2) as i:
                        for u in range(2):
                            dve.wait_ge(rstd_ready, i * 2 + (u + 1))
                            g_at = ds(i * (2 * G) + u * G, G)
                            dve.scalar_tensor_tensor(zT[:, g_at], yT[:, g_at], ff_norm[:, :], rstd[u][:, :], ALU.mult,
                                                     ALU.mult).then_inc(z_ready, 1)
            up1_ready, up3_ready, silu_ready, hid_ready, down_ready, summed, added = r.sems(
                "up1_ready", "up3_ready", "silu_ready", "hid_ready", "down_ready", "summed", "added")
            block = r.block()
            C = FF // P
            UNITS = 2 * C

            @block.tensor
            def _(pe):
                with pe.Fori(0, NG // 2) as i:
                    def up(n):
                        if n >= 2:
                            pe.wait_ge(hid_ready, i * UNITS + (n - 1))
                        f = slice((n % C) * P, (n % C + 1) * P)
                        for m, (wt, ready) in enumerate(((w_1, up1_ready), (w_3, up3_ready))):
                            nc.tensor.matmul(k.bank[2 * (n % 2) + m][:, :], wt[:, f],
                                             zT[:, ds(i * (2 * G) + (n // C) * G, G)], start=True, stop=True
                                             ).then_inc(ready, 1)

                    def down(n):
                        pe.wait_ge(hid_ready, i * UNITS + (n + 1))
                        last = nc.tensor.matmul(k.bank[4 + n // C][:, :], w_2[:, n % C, :], hid[n % 2][:, :],
                                                start=(n % C == 0), stop=(n % C == C - 1))
                        if n % C == C - 1:
                            last.then_inc(down_ready, 1)
                    up(0)
                    for n in range(1, UNITS):
                        up(n)
                        down(n - 1)
                    down(UNITS - 1)
                    pe.wait_ge(added, i * 2 + 2)

            @block.scalar
            def _(act):
                act.preload_act_table(ACT.Silu)
                with act.Fori(0, NG // 2) as i:
                    for n in range(UNITS):
                        act.wait_ge(up1_ready, i * UNITS + (n + 1))
                        act.activation(act1[n % 2][:, :], k.bank[2 * (n % 2)][:, :], ACT.Silu).then_inc(silu_ready, 1)

            @block.vector
            def _(dve):
                with dve.Fori(0, NG // 2) as i:
                    for u in range(2):
                        g_at = ds(i * (2 * G) + u * G, G)
                        dve.tensor_tensor(k.X[:, g_at], k.X[:, g_at], yT[:, g_at], ALU.add).then_inc(summed, 1)
                        for c in range(C):
                            n = u * C + c
                            dve.wait_ge(silu_ready, i * UNITS + (n + 1))
                            dve.wait_ge(up3_ready, i * UNITS + (n + 1))
                            dve.tensor_tensor(hid[n % 2][:, :], act1[n % 2][:, :], k.bank[2 * (n % 2) + 1][:, :], ALU.mult
                                              ).then_inc(hid_ready, 1)
                        dve.wait_ge(down_ready, i * 2 + (u + 1))
                        dve.wait_ge(summed, i * 2 + (u + 1))
                        dve.tensor_tensor(k.X[:, g_at], k.X[:, g_at], k.bank[4 + u][:, :], ALU.add).then_inc(added, 1)


def delta_stage(k):
    with Stage(k, "delta") as s:
        hT = s.sb("hT", [P, N])
        with Stage(k, "dr") as r:
            uT, spikes = r.sb("uT", [DK, N]), r.sb("spikes", [P, DP, N], BF16)
            delta_inputs(k, r, hT, uT)
            delta_spikes(k, r, hT, spikes)
            delta_rule(k, r, hT, uT, spikes, hT)
        delta_output(k, s, hT)


def context_mlp(k):
    nc = k.nc
    H = BG // 2
    with Stage(k, "cmlp") as s:
        turn_context(k, s, "cmlp_ctx")
        hid = [s.sb(f"hid{u}", [P, H, T]) for u in range(2)]
        ctx_g = [s.sb(f"ctxT{u}", [P, G]) for u in range(2)]
        x_g = [s.sb(f"x{u}", [P, G]) for u in range(2)]
        row_g = [s.sb(f"rows{u}", [P, H, D]) for u in range(2)]
        staged, h_ready, gelu_ready, y_ready, added = s.sems("operands_staged", "h_ready", "gelu_ready",
                                                             "y_ready", "added")
        block = s.block()
        h_bank, y_bank = k.bank[0:2], k.bank[2:6]

        @block.vector
        def _(dve):
            with dve.Fori(0, NG // 2) as i:
                for u in range(2):
                    dve.tensor_copy(ctx_g[u][:, :], k.ctxT[:, ds(i * (2 * G) + u * G, G)])
                    dve.tensor_copy(row_g[u][:, :, :], k.ctx_rows[:, ds(i * (2 * H) + u * H, H), :])
                    dve.tensor_copy(x_g[u][:, :], k.X[:, ds(i * (2 * G) + u * G, G)]).then_inc(staged, 1)
                for u in range(2):
                    dve.wait_ge(y_ready, i * 2 + (u + 1))
                    for half in range(2):
                        x = k.X[:, ds(i * (2 * G) + u * G, G)].rearrange("p (n c t) -> p n c t", c=2, t=T)[:, :, half, :]
                        y = y_bank[2 * u + half][:, 0:G // 2].rearrange("p (n t) -> p n t", t=T)
                        dve.tensor_tensor(x, x, y, ALU.add).then_inc(added, 1)

        @block.tensor
        def _(pe):
            with pe.Fori(0, NG // 2) as i:
                for u in range(2):
                    pe.wait_ge(staged, i * 2 + (u + 1))
                    for n in range(H):
                        for half in range(2):
                            c = (2 * n + half) * T
                            last = nc.tensor.matmul(h_bank[u][half * T:half * T + T, n * T:(n + 1) * T],
                                                    ctx_g[u][:, c:c + T], x_g[u][:, c:c + T],
                                                    start=True, stop=True)
                    last.then_inc(h_ready, 1)
                for u in range(2):
                    pe.wait_ge(gelu_ready, i * 2 + (u + 1))
                    for n in range(H):
                        for half in range(2):
                            r = slice(half * T, half * T + T)
                            last = nc.tensor.matmul(y_bank[2 * u + half][:, n * T:(n + 1) * T],
                                                    row_g[u][r, n, :], hid[u][r, n, :], start=True, stop=True)
                    last.then_inc(y_ready, 1)

        @block.scalar
        def _(act):
            with act.Fori(0, NG // 2) as i:
                for u in range(2):
                    act.wait_ge(h_ready, i * 2 + (u + 1))
                    act.activation(hid[u][:, :, :].rearrange("p n t -> p (n t)"), h_bank[u][:, 0:H * T],
                                   ACT.Gelu_apprx_tanh).then_inc(gelu_ready, 1)


FE, FK, FH = 8, 16, 512
FC = FH // P
EK = FE * FK


def pick_tokens(k, s):
    nc = k.nc
    f = Core()
    f.picks = s.sb("picks", [P, 2, 2, 2, NT // 2])
    with Stage(k, "gate") as t:
        gate_rows, gateT = t.sb("gate_rows", [FE, D]), t.sb("gateT", [P, FE])
        x_g = [t.sb(f"x{u}", [P, G]) for u in range(2)]
        shifted, expd, probs = (t.sb(n, [P, NT, FE]) for n in ("shifted", "exp", "probs"))
        top, total, inv = (t.sb(n, [P, NT]) for n in ("top", "total", "inv"))
        probsT = t.sb("probsT", [P, 4, T])
        rest = t.sb("rest", [P, 4, T])
        values, places_u, places = t.sb("values", [P, 4, FK]), t.sb("places_u", [P, 4, FK], U32), t.sb("places", [P, 4, FK])
        is_expert, is_tile = t.sb("is_expert", [P, FE]), t.sb("is_tile", [P, NT // 2])
        spread = t.sb("spread", [P, 2, 4, FE, FK])
        (gate_loaded, gate_turned, gateT_ready, staged, scored, step, exp_ready, turned, spread_ready, moved) = t.sems(
            "gate_loaded", "gate_turned", "gateT_ready", "staged", "scored", "dve_step", "exp_ready", "turned",
            "spread_ready", "moved")
        block = t.block()
        GATE = k.bank[0][:, 0:NT * FE]
        TURNED = k.bank[1][:, 0:4 * T]

        @block.sync
        def _(sync):
            sync.dma_start(gate_rows[:, :], k.a["L1_ffn_gate_w"]).then_inc(gate_loaded, 16)

        @block.tensor
        def _(pe):
            pe.wait_ge(gate_loaded, 16)
            nc.tensor.transpose(k.bank[2][:, 0:FE], gate_rows[:, :], k.eye[0:FE, 0:FE]).then_inc(gate_turned, 1)
            pe.wait_ge(gateT_ready, 1)
            with pe.Fori(0, NG // 2) as i:
                for u in range(2):
                    pe.wait_ge(staged, i * 2 + (u + 1))
                    for n in range(4):
                        last = nc.tensor.matmul(k.bank[0][:, ds(i * (8 * FE) + (u * 4 + n) * FE, FE)],
                                                x_g[u][:, n * D:(n + 1) * D], gateT[:, :], start=True, stop=True)
                    last.then_inc(scored, 1)
            pe.wait_ge(step, 6)
            for h in range(2):
                last = nc.tensor.transpose(TURNED[:, h * TT:(h + 1) * TT],
                                           probs[:, h * 16:(h + 1) * 16, :].rearrange("p n e -> p (n e)"), k.eye[:, :])
            last.then_inc(turned, 1)
            pe.wait_ge(spread_ready, 2)
            for w in range(2):
                for c in range(4):
                    last = nc.tensor.matmul(k.bank[2][:, (4 * w + c) * 16:(4 * w + c + 1) * 16],
                                            spread[:, w, c, :, :].rearrange("p e r -> p (e r)"), is_tile[:, :],
                                            start=True, stop=True)
            last.then_inc(moved, 1)

        @block.vector
        def _(dve):
            eye = k.eye[:, :]
            dve.tensor_reduce(is_expert[:, :], eye.rearrange("p (n e) -> p e n", e=FE), AX_X, ALU.add).then_inc(step, 1)
            dve.tensor_reduce(is_tile[:, :], eye.rearrange("p (n e) -> p n e", e=FE), AX_X, ALU.add).then_inc(step, 1)
            dve.wait_ge(gate_turned, 1)
            dve.tensor_copy(gateT[:, :], k.bank[2][:, 0:FE]).then_inc(gateT_ready, 1)
            dve.tensor_copy(x_g[0][:, :], k.X[:, 0:G]).then_inc(staged, 1)
            dve.tensor_copy(x_g[1][:, :], k.X[:, G:2 * G]).then_inc(staged, 1)
            with dve.Fori(0, NG // 2 - 1) as i:
                for u in range(2):
                    dve.wait_ge(scored, i * 2 + (u + 1))
                    dve.tensor_copy(x_g[u][:, :], k.X[:, ds(i * (2 * G) + (u + 2) * G, G)]).then_inc(staged, 1)
            dve.wait_ge(scored, NG)
            sc = GATE.rearrange("p (n e) -> p n e", e=FE)
            over = lambda ap: ap.unsqueeze(2).to_broadcast([P, NT, FE])
            dve.tensor_reduce(top[:, :], sc, AX_X, ALU.max).then_inc(step, 1)
            dve.wait_ge(step, 3)
            dve.tensor_tensor(shifted[:, :, :], sc, over(top[:, :]), ALU.subtract).then_inc(spread_ready, 1)
            dve.wait_ge(exp_ready, 1)
            dve.tensor_reduce(total[:, :], expd[:, :, :], AX_X, ALU.add).then_inc(step, 1)
            dve.wait_ge(step, 4)
            dve.reciprocal(inv[:, :], total[:, :]).then_inc(step, 1)
            dve.wait_ge(step, 5)
            dve.tensor_tensor(probs[:, :, :], expd[:, :, :], over(inv[:, :]), ALU.mult).then_inc(step, 1)
            dve.wait_ge(turned, 1)
            dve.tensor_copy(probsT[:, :, :].rearrange("p c t -> p (c t)"), TURNED).then_inc(step, 1)
            n = 7
            for c in range(4):
                first, second = slice(0, 8), slice(8, 16)
                dve.wait_ge(step, n)
                dve.max(values[:, c, first], probsT[:, c, :]).then_inc(step, 1)
                dve.wait_ge(step, n + 1)
                dve.max_index(places_u[:, c, first], values[:, c, first], probsT[:, c, :]).then_inc(step, 1)
                dve.match_replace(rest[:, c, :], values[:, c, first], probsT[:, c, :], -1.0).then_inc(step, 1)
                dve.wait_ge(step, n + 3)
                dve.max(values[:, c, second], rest[:, c, :]).then_inc(step, 1)
                dve.wait_ge(step, n + 4)
                dve.max_index(places_u[:, c, second], values[:, c, second], rest[:, c, :]).then_inc(step, 1)
                n += 5
            dve.wait_ge(step, n)
            dve.tensor_copy(places[:, :, :], places_u[:, :, :]).then_inc(step, 1)
            dve.wait_ge(step, n + 1)
            for w, src in enumerate((places, values)):
                for c in range(4):
                    last = dve.tensor_tensor(spread[:, w, c, :, :], src[:, c, :].unsqueeze(1).to_broadcast([P, FE, FK]),
                                             is_expert[:, :].unsqueeze(2).to_broadcast([P, FE, FK]), ALU.mult)
            last.then_inc(spread_ready, 1)
            dve.wait_ge(moved, 1)
            dve.tensor_copy(f.picks[:, :, :, :, :].rearrange("p w h b n -> p (w h b n)"), k.bank[2][:, 0:P]
                            ).then_inc(step, 1)

        @block.scalar
        def _(act):
            act.wait_ge(spread_ready, 1)
            act.activation(expd[:, :, :], shifted[:, :, :], ACT.Exp).then_inc(exp_ready, 1)
    return f


def picked_experts(k):
    nc = k.nc
    with Stage(k, "topk") as s:
        picked = s.sb("picked", [P, FE, B, FK])
        scatter = s.sb("scatter", [P, B, T])
        outs = s.sb("outs", [P, FE, B, FK])
        with Stage(k, "gather") as r:
            f = pick_tokens(k, r)
            tokens = r.sb("token_number", [P, T])
            place, gate = r.sb("place", [P, B]), r.sb("gate_of", [P, B])
            one_hot = [r.sb(f"one_hot{u}", [P, 4, T]) for u in range(2)]
            x_t = [r.sb(f"x{u}", [P, 2 * TT]) for u in range(2)]
            rows, hot_rows = ([r.sb(f"{n}{u}", [P, 2, P]) for u in range(2)] for n in ("rows", "hot_rows"))
            numbered, ordered, hot_ready, staged, scatter_ready, turned, turned_kept, gathered, kept = r.sems(
                "numbered", "ordered", "hot_ready", "staged", "scatter_ready", "turned", "turned_kept", "gathered", "kept")
            block = r.block()
            NQ = NT // 2

            @block.gpsimd
            def _(pool):
                pool.iota(tokens[:, :], pattern=[[1, T]], base=0, channel_multiplier=0,
                          allow_small_or_imprecise_dtypes=True).then_inc(numbered, 1)

            @block.vector
            def _(dve):
                for w, dst in enumerate((place, gate)):
                    last = dve.tensor_copy(dst[:, :].rearrange("p (h n b) -> p h b n", h=2, b=2), f.picks[:, w, :, :, :])
                last.then_inc(ordered, 1)
                dve.wait_ge(numbered, 1)
                dve.wait_ge(ordered, 1)
                with dve.Fori(0, NQ // 2) as i:
                    for u in range(2):
                        dve.tensor_tensor(one_hot[u][:, :, :], tokens[:, :].unsqueeze(1).to_broadcast([P, 4, T]),
                                          place[:, ds(i * 8 + u * 4, 4)].unsqueeze(2).to_broadcast([P, 4, T]),
                                          ALU.is_equal).then_inc(hot_ready, 1)
                        dve.tensor_copy(x_t[u][:, :], k.X[:, ds(i * (4 * TT) + u * 2 * TT, 2 * TT)]).then_inc(staged, 1)
                        dve.wait_ge(hot_ready, i * 2 + (u + 1))
                        dve.tensor_tensor(scatter[:, ds(i * 8 + u * 4, 4), :], one_hot[u][:, :, :],
                                          gate[:, ds(i * 8 + u * 4, 4)].unsqueeze(2).to_broadcast([P, 4, T]),
                                          ALU.mult).then_inc(scatter_ready, 1)
                    for u in range(2):
                        dve.wait_ge(gathered, i * 2 + (u + 1))
                        for b in range(2):
                            for j in range(2):
                                last = dve.tensor_copy(picked[:, :, ds(i * 8 + (u * 4 + 2 * j + b), 1), :],
                                                       k.bank[2 + 2 * u + b][:, j * EK:(j + 1) * EK].rearrange(
                                                           "p (e n r) -> p e n r", n=1, r=FK))
                        last.then_inc(kept, 1)

            @block.tensor
            def _(pe):
                with pe.Fori(0, NQ // 2) as i:
                    for u in range(2):
                        pe.wait_ge(staged, i * 2 + (u + 1))
                        for j in range(2):
                            nc.tensor.transpose(k.bank[u][:, j * P:(j + 1) * P], x_t[u][:, j * TT:(j + 1) * TT], k.eye[:, :])
                            last = nc.tensor.transpose(
                                k.bank[u][:, (2 + j) * P:(3 + j) * P],
                                one_hot[u][:, 2 * j:2 * j + 2, :].rearrange("p b t -> p (b t)"), k.eye[:, :])
                        last.then_inc(turned, 1)
                    for u in range(2):
                        k.hold(pe)
                        pe.wait_ge(turned_kept, i * 2 + (u + 1))
                        for j in range(2):
                            for b in range(2):
                                r = slice(b * T, (b + 1) * T)
                                last = nc.tensor.matmul(k.bank[2 + 2 * u + b][:, j * EK:(j + 1) * EK], rows[u][r, j, :],
                                                        hot_rows[u][r, j, :], start=True, stop=True)
                        last.then_inc(gathered, 1)

            @block.scalar
            def _(act):
                with act.Fori(0, NQ // 2) as i:
                    for u in range(2):
                        act.wait_ge(turned, i * 2 + (u + 1))
                        act.activation(rows[u][:, :, :].rearrange("p j d -> p (j d)"), k.bank[u][:, 0:2 * P], ACT.Copy)
                        act.activation(hot_rows[u][:, :, :].rearrange("p j d -> p (j d)"), k.bank[u][:, 2 * P:4 * P],
                                       ACT.Copy).then_inc(turned_kept, 1)

        with Stage(k, "experts") as e:
            w1 = [e.sb(f"w1_{u}", [P, FH]) for u in range(2)]
            w2 = [e.sb(f"w2_{u}", [P, FC, D]) for u in range(2)]
            hid = [e.sb(f"hid{u}", [P, 2, 512]) for u in range(3)]
            w_loaded = e.sems("w_loaded0", "w_loaded1")
            h_ready, gelu_ready, y_ready, y_kept = e.sems("h_ready", "gelu_ready", "y_ready", "y_kept")
            block = e.block()
            picks2 = picked[:, :, :, :].rearrange("p e (h n) r -> p (e h) (n r)", h=2)
            outs2 = outs[:, :, :, :].rearrange("p e (h n) r -> p (e h) (n r)", h=2)
            a1, a2 = k.a["L1_ffn_w1"], k.a["L1_ffn_w2"]

            @block.sync
            def _(sync):
                def load(expert, u):
                    sync.dma_start(w1[u][:, :], a1[ds(expert, 1), :, :].rearrange("o d f -> d (o f)")).then_inc(w_loaded[u], 16)
                    sync.dma_start(w2[u][:, :, :], a2[ds(expert, 1), :, :].rearrange("o (c p) d -> p (o c) d", p=P)
                                   ).then_inc(w_loaded[u], 16)
                for u in range(2):
                    load(u, u)
                with sync.Fori(0, FE // 2 - 1) as i:
                    for u in range(2):
                        sync.wait_ge(y_ready, i * 4 + (2 * u + 2))
                        load(i * 2 + (u + 2), u)

            @block.tensor
            def _(pe):
                with pe.Fori(0, FE // 2) as i:
                    def hidden(n):
                        u, half, pair = n // 4, (n // 2) % 2, n % 2
                        if n % 4 == 0:
                            pe.wait_ge(w_loaded[u], i * 32 + 32)
                        for c in range(2):
                            f0 = (2 * pair + c) * P
                            last = nc.tensor.matmul(k.bank[2 * (n % 3) + c][:, :], w1[u][:, f0:f0 + P],
                                                    picks2[:, ds(i * 4 + (n // 2), 1), :].rearrange("p o c -> p (o c)"),
                                                    start=True, stop=True)
                        last.then_inc(h_ready, 1)

                    def output(n):
                        u, half, pair = n // 4, (n // 2) % 2, n % 2
                        pe.wait_ge(gelu_ready, i * 8 + (n + 1))
                        if n >= 4 and pair == 0:
                            pe.wait_ge(y_kept, i * 4 + (n // 2 - 1))
                        for c in range(2):
                            last = nc.tensor.matmul(k.bank[6 + half][:, :], w2[u][:, 2 * pair + c, :], hid[n % 3][:, c, :],
                                                    start=(pair == 0 and c == 0), stop=(pair == 1 and c == 1))
                        if pair == 1:
                            last.then_inc(y_ready, 1)
                    hidden(0)
                    for n in range(8):
                        if n < 7:
                            hidden(n + 1)
                        output(n)
                    pe.wait_ge(y_kept, i * 4 + 4)

            @block.scalar
            def _(act):
                act.preload_act_table(ACT.Gelu)
                with act.Fori(0, FE // 2) as i:
                    for n in range(8):
                        act.wait_ge(h_ready, i * 8 + (n + 1))
                        act.activation(hid[n % 3][:, :, :], k.psum[:, 2 * (n % 3):2 * (n % 3) + 2, :], ACT.Gelu
                                       ).then_inc(gelu_ready, 1)

            @block.vector
            def _(dve):
                with dve.Fori(0, FE // 2) as i:
                    for m in range(4):
                        dve.wait_ge(y_ready, i * 4 + (m + 1))
                        dve.tensor_copy(outs2[:, ds(i * 4 + m, 1), :].rearrange("p o c -> p (o c)"), k.bank[6 + m % 2][:, :]
                                        ).then_inc(y_kept, 1)

        with Stage(k, "scatter") as r:
            y_t = [r.sb(f"y{u}", [P, 4, EK]) for u in range(2)]
            rows = [r.sb(f"rows{u}", [P, 4, D]) for u in range(2)]
            staged, turned, rows_ready, out_ready, added = r.sems("staged", "turned", "rows_ready", "out_ready", "added")
            block = r.block()
            NU = B // 4

            @block.vector
            def _(dve):
                with dve.Fori(0, NU // 2) as i:
                    for u in range(2):
                        dve.tensor_copy(y_t[u][:, :, :].rearrange("p n (e r) -> p e n r", e=FE),
                                        outs[:, :, ds(i * 8 + u * 4, 4), :]).then_inc(staged, 1)
                    for u in range(2):
                        dve.wait_ge(out_ready, i * 2 + (u + 1))
                        x = k.X[:, ds(i * (8 * T) + u * 4 * T, 4 * T)]
                        dve.tensor_tensor(x, x, k.bank[2 + u][:, 0:4 * T], ALU.add).then_inc(added, 1)

            @block.tensor
            def _(pe):
                with pe.Fori(0, NU // 2) as i:
                    for u in range(2):
                        pe.wait_ge(staged, i * 2 + (u + 1))
                        for b in range(4):
                            last = nc.tensor.transpose(k.bank[u][:, b * D:(b + 1) * D], y_t[u][:, b, :], k.eye[:, :])
                        last.then_inc(turned, 1)
                    for u in range(2):
                        pe.wait_ge(rows_ready, i * 2 + (u + 1))
                        for b in range(4):
                            last = nc.tensor.matmul(k.bank[2 + u][:, b * T:(b + 1) * T], rows[u][:, b, :],
                                                    scatter[:, ds(i * 8 + (u * 4 + b), 1), :].rearrange("p o t -> p (o t)"),
                                                    start=True, stop=True)
                        last.then_inc(out_ready, 1)

            @block.scalar
            def _(act):
                with act.Fori(0, NU // 2) as i:
                    for u in range(2):
                        act.wait_ge(turned, i * 2 + (u + 1))
                        act.activation(rows[u][:, :, :].rearrange("p b d -> p (b d)"), k.bank[u][:, :], ACT.Copy
                                       ).then_inc(rows_ready, 1)


def store_tokens(k):
    nc = k.nc
    with Stage(k, "store") as s:
        rows = s.sb("rows", [P, NT, D])
        turned, kept, stored = s.sems("turned", "kept", "stored")
        block = s.block()
        out = k.out.rearrange("(n u) t d -> (u t) n d", u=2)

        @block.tensor
        def _(pe):
            for g in range(NG):
                for j in range(4):
                    last = nc.tensor.transpose(k.bank[g][:, j * D:(j + 1) * D], k.X[:, g * G + j * D:g * G + (j + 1) * D],
                                               k.eye[:, :])
                last.then_inc(turned, 1)

        @block.vector
        def _(dve):
            for g in range(NG):
                dve.wait_ge(turned, g + 1)
                dve.tensor_copy(rows[:, 4 * g:4 * g + 4, :].rearrange("p n d -> p (n d)"),
                                k.bank[g][:, :]).then_inc(kept, 1)

        @block.sync
        def _(sync):
            for g in range(0, NG, 2):
                sync.wait_ge(kept, g + 2)
                sync.dma_start(out[:, 4 * g:4 * g + 8, :], rows[:, 4 * g:4 * g + 8, :]).then_inc(stored, 16)
            sync.wait_ge(stored, 16 * NG // 2)


def host_constants():
    inv_freq = (1.0 / 10000.0 ** (np.arange(0, AK, 2, dtype=np.float32) / AK)).astype(np.float32)
    angle = (np.arange(T, dtype=np.float32)[None, :] * inv_freq[:, None]).astype(np.float32)
    cos, sin = np.cos(angle), np.sin(angle)
    table = np.stack([np.concatenate([cos, cos, cos, cos]), np.concatenate([-sin, sin, -sin, sin])], axis=1)
    s = np.arange(P) % T
    levels = np.zeros((P, LEVELS, T // 2), np.float32)
    for l in range(LEVELS):
        half = 1 << l
        block = np.arange(T // 2) // half
        levels[:, l, :] = (s[:, None] // (2 * half) == block[None, :]) & (s[:, None] % (2 * half) < half)
    head = np.arange(P) // DK
    return {"level_masks": levels, "eye2": np.tile(np.eye(T, dtype=np.float32), (2, 1)),
            "head_sum": (head[:, None] == head[None, :]).astype(np.float32),
            "rope_q": (table * np.float32(AK ** -0.5)).astype(np.float32), "rope_k": table.astype(np.float32)}


STAGES = ["attn", "ln1", "xattn", "ln2", "moe", "ln3", "delta", "ln4", "cmlp", "ln5", "topk", "ln6"]


def decoder(nc, a, out):
    k = Core()
    k.nc, k.a, k.out = nc, a, out
    with ExitStack() as stack:
        def sb(name, shape, dt=F32):
            return stack.enter_context(nc.sbuf_tensor(name, shape, dt))
        k.X = sb("X", [P, N])
        k.ctx_rows = sb("ctx_rows", [P, NT, D])
        k.eye = sb("eye", [P, P])
        k.ones_mean = sb("ones_mean", [P, P])
        k.ln_eps = sb("ln_eps", [P, 1])
        k.psum = stack.enter_context(nc.psum_tensor("psum", [P, 8, 512], F32))
        k.bank = [k.psum[:, i, :] for i in range(8)]
        k.ln_sems = [stack.enter_context(nc.semaphore(f"ln_{n}")) for n in (
            "mean_ready", "centred", "squared", "var_ready", "log_ready", "rstd_ready", "normed")]
        k.ln_calls = 0
        k.ctx_loaded = stack.enter_context(nc.semaphore("ctx_loaded"))
        k.eye_made = stack.enter_context(nc.semaphore("eye_made"))
        load_tokens(k)
        for st in STAGES:
            if st.startswith("ln"):
                layer_norm(k, k.ln_calls)
                k.ln_calls += 1
            else:
                {"attn": rope_attention, "xattn": cross_attention, "moe": soft_mixture, "delta": delta_stage,
                 "cmlp": context_mlp, "topk": picked_experts}[st](k)
        store_tokens(k)


INPUTS = ["x", "ctx_1024"] + [f"L0_attn_{n}" for n in ("Wq", "bq", "Wk", "bk", "Wv", "bv", "Wo", "bo")] + [
    f"L0_xattn_{n}" for n in ("wq_w", "wq_b", "wk_w", "wk_b", "wv_w", "wv_b", "wo_w", "wo_b")] + [
    f"L0_ffn_{n}" for n in ("ln_gamma", "ln_beta", "mu", "scale", "w1", "b1", "w2", "b2")] + [
    f"L1_attn_{n}" for n in ("norm_in_w", "conv_w", "conv_b", "Wq", "Wk", "Wv", "Wo", "Wspike", "Wau", "bau", "Wad", "bad",
                             "alpha_spike", "Wbeta", "bbeta", "beta_spike", "head_norm_w", "Wu1", "bu1", "Wu2", "bu2",
                             "ff_norm_w", "Wff1", "Wff3", "Wff2")] + [
    f"L1_ffn_{n}" for n in ("gate_w", "w1", "w2")]


def kernel(**inputs):
    import concourse.bacc as bacc
    from concourse.bass_utils import run_bass_kernel_spmd

    nc = bacc.Bacc("TRN2", target_bir_lowering=False, num_devices=1)
    operands = {name: np.ascontiguousarray(inputs[name]) for name in INPUTS}
    operands.update(host_constants())
    arrays, args = {}, {}
    for name, array in operands.items():
        arrays[f"in_{name}_dram"] = array
        args[name] = nc.dram_tensor(f"in_{name}_dram", array.shape, mybir.dt.from_np(array.dtype),
                                    kind="ExternalInput").ap()
    out = nc.dram_tensor("out_0_dram", (B, T, D), F32, kind="ExternalOutput").ap()
    decoder(nc, args, out)
    r = run_bass_kernel_spmd(nc, [arrays], core_ids=[0])
    return r.results[0]["out_0_dram"]
```
